# Optimizing a Trainium2 kernel written in Bass

```python
import numpy as np
import jax
import jax.numpy as jnp

def _softmax(x, axis=-1):
    return jax.nn.softmax(x, axis=axis)

def _gelu(x):
    return jax.nn.gelu(x, approximate=True)

def _silu(x):
    return jax.nn.silu(x)

def _sigmoid(x):
    return jax.nn.sigmoid(x)

def _layernorm(x, axis=-1, eps=1e-05):
    m = jnp.mean(x, axis=axis, keepdims=True)
    v = jnp.var(x, axis=axis, keepdims=True)
    return (x - m) / jnp.sqrt(v + eps)

def _scatter_add(tgt, idx, src, axis=0):
    return tgt.at[idx].add(src)

def _segment_sum(src, seg, n):
    return jax.ops.segment_sum(src, seg, n)
kernel_name = 'mk_gnn_preln_d4_gnn_r32_32d014'

def setup_inputs(seed: int=0):
    np.random.seed(seed)
    _w = jnp.asarray

    def _rec_inputs():
        import jax
        import jax.numpy as jnp
        _gk = jax.random.key(seed)
        x = -0.000202 + 1 * jax.random.normal(jax.random.fold_in(_gk, 1), (3125, 128), jnp.float32)
        src = jax.random.randint(jax.random.fold_in(_gk, 2), (50000,), 0, 3125, jnp.int32)
        dst = jax.random.randint(jax.random.fold_in(_gk, 3), (50000,), 0, 3125, jnp.int32)
        _o = jnp.argsort(dst, stable=True)
        src = src[_o]
        dst = dst[_o]
        edge_type_474 = jax.random.randint(jax.random.fold_in(_gk, 13), (50000,), 0, 474, jnp.int32)
        edge_weight1 = 0.000614103 + 0.999867 * jax.random.normal(jax.random.fold_in(_gk, 14), (50000, 1), jnp.float32)
        return (x, src, dst, edge_type_474, edge_weight1)
    x, src, dst, edge_type_474, edge_weight1 = _rec_inputs()

    def _L0_gnn_setup():
        import jax, jax.numpy as jnp
        import numpy as np
        import math
        HEADS = 8
        CH = 16
        SCALE = 1.0 / math.sqrt(CH)

        def _transformer_conv(x, src, dst, qw, qb, kw, kb, vw, vb, sw, sb):
            N = x.shape[0]
            q = (x @ qw + qb).reshape(N, HEADS, CH)
            k = (x @ kw + kb).reshape(N, HEADS, CH)
            v = (x @ vw + vb).reshape(N, HEADS, CH)
            alpha = jnp.sum(q[dst] * k[src], axis=-1) * SCALE
            m = jax.ops.segment_max(alpha, dst, num_segments=N)
            a = jnp.exp(alpha - m[dst])
            denom = jax.ops.segment_sum(a, dst, num_segments=N)
            a = a / denom[dst]
            msg = v[src] * a[:, :, None]
            out = jax.ops.segment_sum(msg, dst, num_segments=N).reshape(N, HEADS * CH)
            return out + x @ sw + sb
        key = jax.random.key(seed)
        ks = jax.random.split(key, 16)
        N, E, IN = (50000, 25000, 128)
        D = HEADS * CH

        def lin(k, fi, fo):
            return jax.random.normal(k, (fi, fo), jnp.float32) / math.sqrt(fi)
        inp = {'x': jax.random.normal(ks[0], (N, IN), jnp.float32), 'edge_index': jax.random.randint(ks[1], (2, E), 0, N, dtype=jnp.int64), 'edge_attr': jax.random.normal(ks[2], (E, 1), jnp.float32), 'q_w0': lin(ks[3], IN, D), 'q_b0': jnp.zeros((D,), jnp.float32), 'k_w0': lin(ks[4], IN, D), 'k_b0': jnp.zeros((D,), jnp.float32), 'v_w0': lin(ks[5], IN, D), 'v_b0': jnp.zeros((D,), jnp.float32), 's_w0': lin(ks[6], IN, D), 's_b0': jnp.zeros((D,), jnp.float32), 'q_w1': lin(ks[7], D, D), 'q_b1': jnp.zeros((D,), jnp.float32), 'k_w1': lin(ks[8], D, D), 'k_b1': jnp.zeros((D,), jnp.float32), 'v_w1': lin(ks[9], D, D), 'v_b1': jnp.zeros((D,), jnp.float32), 's_w1': lin(ks[10], D, D), 's_b1': jnp.zeros((D,), jnp.float32)}
        return inp
    _L0_gnn_all = _L0_gnn_setup()
    _L0_gnn_in = {k: v for k, v in _L0_gnn_all.items() if k in ('q_w0', 'q_b0', 'k_w0', 'k_b0', 'v_w0', 'v_b0', 's_w0', 's_b0', 'q_w1', 'q_b1', 'k_w1', 'k_b1', 'v_w1', 'v_b1', 's_w1', 's_b1')}
    del _L0_gnn_all

    def _L1_gnn_setup():
        import jax, jax.numpy as jnp
        import numpy as np
        N, E, D, H, C = (50000, 25000, 128, 1, 128)
        NEG_SLOPE = 0.2

        def _gat_layer(x, src, dst, W, att_src, att_dst, b):
            n = x.shape[0]
            xl = (x @ W).reshape(n, H, C)
            a_s = jnp.sum(xl * att_src, axis=-1)
            a_d = jnp.sum(xl * att_dst, axis=-1)
            e = jax.nn.leaky_relu(a_s[src] + a_d[dst], NEG_SLOPE)
            m = jax.ops.segment_max(e, dst, num_segments=n)
            e = jnp.exp(e - m[dst])
            z = jax.ops.segment_sum(e, dst, num_segments=n)
            alpha = e / (z[dst] + 1e-16)
            msg = xl[src] * alpha[:, :, None]
            out = jax.ops.segment_sum(msg, dst, num_segments=n)
            return out.mean(axis=1) + b
        key = jax.random.key(seed)
        ks = jax.random.split(key, 12)
        x = jax.random.normal(ks[0], (N, D), dtype=jnp.float32)
        edge_index = jax.random.randint(ks[1], (2, E), 0, N, dtype=jnp.int64)
        s = 1.0 / np.sqrt(D)
        inp = {'x': x, 'edge_index': edge_index}
        for i, base in [(1, 2), (2, 7)]:
            inp[f'W{i}'] = jax.random.normal(ks[base], (D, H * C), dtype=jnp.float32) * s
            inp[f'att_src{i}'] = jax.random.normal(ks[base + 1], (H, C), dtype=jnp.float32) * s
            inp[f'att_dst{i}'] = jax.random.normal(ks[base + 2], (H, C), dtype=jnp.float32) * s
            inp[f'b{i}'] = jnp.zeros((C,), dtype=jnp.float32)
        return inp
    _L1_gnn_all = _L1_gnn_setup()
    _L1_gnn_in = {k: v for k, v in _L1_gnn_all.items() if k in ('W1', 'att_src1', 'att_dst1', 'b1', 'W2', 'att_src2', 'att_dst2', 'b2')}
    del _L1_gnn_all

    def _L2_gnn_setup():
        import jax, jax.numpy as jnp
        import numpy as np
        N = 50000
        E = 25000
        D_MODEL = 128
        N_HEADS = 8
        HEAD_DIM = D_MODEL // N_HEADS
        SCALE = HEAD_DIM ** (-0.5)
        key = jax.random.key(seed)
        k1, k2, k3, k4, k5 = jax.random.split(key, 5)
        node_embeds = jax.random.normal(k1, (N, D_MODEL), dtype=jnp.float32)
        edge_index = jax.random.randint(k2, (2, E), 0, N, dtype=jnp.int32)
        lim_qkv = (6.0 / (D_MODEL + 3 * D_MODEL)) ** 0.5
        lim_out = (6.0 / (D_MODEL + D_MODEL)) ** 0.5
        W_qkv = jax.random.uniform(k3, (3 * D_MODEL, D_MODEL), minval=-lim_qkv, maxval=lim_qkv, dtype=jnp.float32)
        W_out = jax.random.uniform(k4, (D_MODEL, D_MODEL), minval=-lim_out, maxval=lim_out, dtype=jnp.float32)
        return {'node_embeds': node_embeds, 'edge_index': edge_index, 'W_qkv': W_qkv, 'W_out': W_out}
    _L2_gnn_all = _L2_gnn_setup()
    _L2_gnn_in = {k: v for k, v in _L2_gnn_all.items() if k in ('W_qkv', 'W_out')}
    del _L2_gnn_all

    def _L3_gnn_setup():
        import jax, jax.numpy as jnp
        import numpy as np
        N_ENT = 50000
        N_EDGE = 15625
        H_DIM = 128
        N_REL_TAB = 475

        def _edge_softmax(logits, dst, n_nodes):
            m = jax.ops.segment_max(logits, dst, num_segments=n_nodes)
            ex = jnp.exp(logits - m[dst])
            s = jax.ops.segment_sum(ex, dst, num_segments=n_nodes)
            return ex / s[dst]

        def _attn_aggregate(msg, key_emb_dst, dst, n_nodes, w):
            logits = jnp.sum(msg * key_emb_dst, axis=-1)
            a = _edge_softmax(logits, dst, n_nodes)
            neigh = jax.ops.segment_sum(msg * a[:, None], dst, num_segments=n_nodes)
            return jnp.tanh(neigh @ w)
        key = jax.random.key(seed)
        ks = jax.random.split(key, 8)
        scale = 1.0 / np.sqrt(H_DIM)
        return {'ent_emb': jax.random.normal(ks[0], (N_ENT, H_DIM), jnp.float32) * scale, 'rel_emb': jax.random.normal(ks[1], (N_REL_TAB, H_DIM), jnp.float32) * scale, 'w_edge': jax.random.normal(ks[2], (H_DIM, H_DIM), jnp.float32) * scale, 'w_node': jax.random.normal(ks[3], (H_DIM, H_DIM), jnp.float32) * scale, 'w_comp': jax.random.normal(ks[4], (H_DIM, H_DIM), jnp.float32) * scale, 'src': jax.random.randint(ks[5], (N_EDGE,), 0, N_ENT, jnp.int32), 'dst': jax.random.randint(ks[6], (N_EDGE,), 0, N_ENT, jnp.int32), 'rel_id': jax.random.randint(ks[7], (N_EDGE,), 0, N_REL_TAB - 1, jnp.int32)}
    _L3_gnn_all = _L3_gnn_setup()
    _L3_gnn_in = {k: v for k, v in _L3_gnn_all.items() if k in ('rel_emb', 'w_edge', 'w_node', 'w_comp')}
    del _L3_gnn_all
    return {'x': x, 'src': src, 'dst': dst, 'edge_type_474': edge_type_474, 'edge_weight1': edge_weight1, 'L0_gnn_q_w0': _L0_gnn_in['q_w0'], 'L0_gnn_q_b0': _L0_gnn_in['q_b0'], 'L0_gnn_k_w0': _L0_gnn_in['k_w0'], 'L0_gnn_k_b0': _L0_gnn_in['k_b0'], 'L0_gnn_v_w0': _L0_gnn_in['v_w0'], 'L0_gnn_v_b0': _L0_gnn_in['v_b0'], 'L0_gnn_s_w0': _L0_gnn_in['s_w0'], 'L0_gnn_s_b0': _L0_gnn_in['s_b0'], 'L0_gnn_q_w1': _L0_gnn_in['q_w1'], 'L0_gnn_q_b1': _L0_gnn_in['q_b1'], 'L0_gnn_k_w1': _L0_gnn_in['k_w1'], 'L0_gnn_k_b1': _L0_gnn_in['k_b1'], 'L0_gnn_v_w1': _L0_gnn_in['v_w1'], 'L0_gnn_v_b1': _L0_gnn_in['v_b1'], 'L0_gnn_s_w1': _L0_gnn_in['s_w1'], 'L0_gnn_s_b1': _L0_gnn_in['s_b1'], 'L1_gnn_W1': _L1_gnn_in['W1'], 'L1_gnn_att_src1': _L1_gnn_in['att_src1'], 'L1_gnn_att_dst1': _L1_gnn_in['att_dst1'], 'L1_gnn_b1': _L1_gnn_in['b1'], 'L1_gnn_W2': _L1_gnn_in['W2'], 'L1_gnn_att_src2': _L1_gnn_in['att_src2'], 'L1_gnn_att_dst2': _L1_gnn_in['att_dst2'], 'L1_gnn_b2': _L1_gnn_in['b2'], 'L2_gnn_W_qkv': _L2_gnn_in['W_qkv'], 'L2_gnn_W_out': _L2_gnn_in['W_out'], 'L3_gnn_rel_emb': _L3_gnn_in['rel_emb'], 'L3_gnn_w_edge': _L3_gnn_in['w_edge'], 'L3_gnn_w_node': _L3_gnn_in['w_node'], 'L3_gnn_w_comp': _L3_gnn_in['w_comp']}

def reference(x, src, dst, edge_type_474, edge_weight1, L0_gnn_q_w0, L0_gnn_q_b0, L0_gnn_k_w0, L0_gnn_k_b0, L0_gnn_v_w0, L0_gnn_v_b0, L0_gnn_s_w0, L0_gnn_s_b0, L0_gnn_q_w1, L0_gnn_q_b1, L0_gnn_k_w1, L0_gnn_k_b1, L0_gnn_v_w1, L0_gnn_v_b1, L0_gnn_s_w1, L0_gnn_s_b1, L1_gnn_W1, L1_gnn_att_src1, L1_gnn_att_dst1, L1_gnn_b1, L1_gnn_W2, L1_gnn_att_src2, L1_gnn_att_dst2, L1_gnn_b2, L2_gnn_W_qkv, L2_gnn_W_out, L3_gnn_rel_emb, L3_gnn_w_edge, L3_gnn_w_node, L3_gnn_w_comp):
    import jax
    import jax.numpy as jnp

    def _L0_gnn_ref(x, edge_index, edge_attr, q_w0, q_b0, k_w0, k_b0, v_w0, v_b0, s_w0, s_b0, q_w1, q_b1, k_w1, k_b1, v_w1, v_b1, s_w1, s_b1):
        import jax, jax.numpy as jnp
        import numpy as np
        import math
        HEADS = 8
        CH = 16
        SCALE = 1.0 / math.sqrt(CH)

        def _transformer_conv(x, src, dst, qw, qb, kw, kb, vw, vb, sw, sb):
            N = x.shape[0]
            q = (x @ qw + qb).reshape(N, HEADS, CH)
            k = (x @ kw + kb).reshape(N, HEADS, CH)
            v = (x @ vw + vb).reshape(N, HEADS, CH)
            alpha = jnp.sum(q[dst] * k[src], axis=-1) * SCALE
            m = jax.ops.segment_max(alpha, dst, num_segments=N)
            a = jnp.exp(alpha - m[dst])
            denom = jax.ops.segment_sum(a, dst, num_segments=N)
            a = a / denom[dst]
            msg = v[src] * a[:, :, None]
            out = jax.ops.segment_sum(msg, dst, num_segments=N).reshape(N, HEADS * CH)
            return out + x @ sw + sb
        src, dst = (edge_index[0], edge_index[1])
        h = _transformer_conv(x, src, dst, q_w0, q_b0, k_w0, k_b0, v_w0, v_b0, s_w0, s_b0)
        h = jax.nn.relu(h)
        h = _transformer_conv(h, src, dst, q_w1, q_b1, k_w1, k_b1, v_w1, v_b1, s_w1, s_b1)
        return h

    def _L1_gnn_ref(x, edge_index, W1, att_src1, att_dst1, b1, W2, att_src2, att_dst2, b2):
        import jax, jax.numpy as jnp
        import numpy as np
        N, E, D, H, C = (50000, 25000, 128, 1, 128)
        NEG_SLOPE = 0.2

        def _gat_layer(x, src, dst, W, att_src, att_dst, b):
            n = x.shape[0]
            xl = (x @ W).reshape(n, H, C)
            a_s = jnp.sum(xl * att_src, axis=-1)
            a_d = jnp.sum(xl * att_dst, axis=-1)
            e = jax.nn.leaky_relu(a_s[src] + a_d[dst], NEG_SLOPE)
            m = jax.ops.segment_max(e, dst, num_segments=n)
            e = jnp.exp(e - m[dst])
            z = jax.ops.segment_sum(e, dst, num_segments=n)
            alpha = e / (z[dst] + 1e-16)
            msg = xl[src] * alpha[:, :, None]
            out = jax.ops.segment_sum(msg, dst, num_segments=n)
            return out.mean(axis=1) + b
        loops = jnp.arange(N, dtype=edge_index.dtype)
        src = jnp.concatenate([edge_index[0], loops])
        dst = jnp.concatenate([edge_index[1], loops])
        h = _gat_layer(x, src, dst, W1, att_src1, att_dst1, b1)
        h = jax.nn.relu(h)
        h = _gat_layer(h, src, dst, W2, att_src2, att_dst2, b2)
        return jax.nn.relu(h)

    def _L2_gnn_ref(node_embeds, edge_index, W_qkv, W_out):
        import jax, jax.numpy as jnp
        import numpy as np
        N = 50000
        E = 25000
        D_MODEL = 128
        N_HEADS = 8
        HEAD_DIM = D_MODEL // N_HEADS
        SCALE = HEAD_DIM ** (-0.5)
        n = node_embeds.shape[0]
        qkv = (node_embeds @ W_qkv.T).reshape(n, 3, N_HEADS, HEAD_DIM)
        q, k, v = (qkv[:, 0], qkv[:, 1], qkv[:, 2])
        src = edge_index[0]
        tgt = edge_index[1]
        q_e = q[src]
        k_e = k[tgt]
        v_e = v[tgt]
        scores = jnp.sum(q_e * k_e, axis=-1) * SCALE
        scores = jnp.clip(scores, -10.0, 10.0)
        exp_att = jnp.exp(scores)
        att_sum = jax.ops.segment_sum(exp_att, src, num_segments=n)
        weighted_v = exp_att[..., None] * v_e
        out = jax.ops.segment_sum(weighted_v, src, num_segments=n)
        out = out / (att_sum[..., None] + 1e-08)
        out = out.reshape(n, D_MODEL)
        return out @ W_out.T

    def _L3_gnn_ref(ent_emb, rel_emb, w_edge, w_node, w_comp, src, dst, rel_id):
        import jax, jax.numpy as jnp
        import numpy as np
        N_ENT = 50000
        N_EDGE = 15625
        H_DIM = 128
        N_REL_TAB = 475

        def _edge_softmax(logits, dst, n_nodes):
            m = jax.ops.segment_max(logits, dst, num_segments=n_nodes)
            ex = jnp.exp(logits - m[dst])
            s = jax.ops.segment_sum(ex, dst, num_segments=n_nodes)
            return ex / s[dst]

        def _attn_aggregate(msg, key_emb_dst, dst, n_nodes, w):
            logits = jnp.sum(msg * key_emb_dst, axis=-1)
            a = _edge_softmax(logits, dst, n_nodes)
            neigh = jax.ops.segment_sum(msg * a[:, None], dst, num_segments=n_nodes)
            return jnp.tanh(neigh @ w)
        n = ent_emb.shape[0]
        v = ent_emb[dst]
        u = ent_emb[src]
        r = rel_emb[rel_id]
        edge_out = _attn_aggregate(r, v, dst, n, w_edge)
        node_out = _attn_aggregate(u, v, dst, n, w_node)
        comp_out = _attn_aggregate(u + r, v, dst, n, w_comp)
        return ent_emb + edge_out + node_out + comp_out
    edge_index = jnp.stack([src, dst])
    h = jnp.maximum(_layernorm(x, axis=-1), 0.0)
    x = x + _L0_gnn_ref(h, edge_index, edge_weight1, L0_gnn_q_w0, L0_gnn_q_b0, L0_gnn_k_w0, L0_gnn_k_b0, L0_gnn_v_w0, L0_gnn_v_b0, L0_gnn_s_w0, L0_gnn_s_b0, L0_gnn_q_w1, L0_gnn_q_b1, L0_gnn_k_w1, L0_gnn_k_b1, L0_gnn_v_w1, L0_gnn_v_b1, L0_gnn_s_w1, L0_gnn_s_b1)
    h = jnp.maximum(_layernorm(x, axis=-1), 0.0)
    x = x + _L1_gnn_ref(h, edge_index, L1_gnn_W1, L1_gnn_att_src1, L1_gnn_att_dst1, L1_gnn_b1, L1_gnn_W2, L1_gnn_att_src2, L1_gnn_att_dst2, L1_gnn_b2)
    h = jnp.maximum(_layernorm(x, axis=-1), 0.0)
    x = x + _L2_gnn_ref(h, edge_index, L2_gnn_W_qkv, L2_gnn_W_out)
    h = jnp.maximum(_layernorm(x, axis=-1), 0.0)
    x = x + _L3_gnn_ref(h, L3_gnn_rel_emb, L3_gnn_w_edge, L3_gnn_w_node, L3_gnn_w_comp, src, dst, edge_type_474)
    return x

_drawn_inputs = setup_inputs


def setup_inputs(seed=0):
    import zlib

    import numpy as np

    out = dict(_drawn_inputs(seed))
    spreads = {'L0_gnn_q_b0': (0.0, 0.8),
     'L0_gnn_k_b0': (0.0, 2.0),
     'L0_gnn_v_b0': (0.0, 0.1),
     'L0_gnn_s_b0': (0.0, 0.1),
     'L0_gnn_q_b1': (0.0, 0.8),
     'L0_gnn_k_b1': (0.0, 2.0),
     'L0_gnn_v_b1': (0.0, 0.1),
     'L0_gnn_s_b1': (0.0, 0.1),
     'L1_gnn_b1': (0.0, 0.1),
     'L1_gnn_b2': (0.0, 0.1)}
    factors = {'L0_gnn_q_w1': 3.614,
     'L0_gnn_k_w1': 3.382,
     'L1_gnn_att_dst1': 64.0,
     'L1_gnn_att_src2': 34.251,
     'L1_gnn_att_dst2': 64.0,
     'L3_gnn_w_edge': 4.017,
     'L1_gnn_att_src1': 2.784}
    for name, (base, spread) in spreads.items():
        noise = np.random.default_rng([zlib.crc32(name.encode()), seed]).standard_normal(out[name].shape)
        drawn = base * np.exp(spread * noise) if base else spread * noise
        out[name] = jnp.asarray(drawn.astype(out[name].dtype))
    for name, factor in factors.items():
        out[name] = (out[name] * factor).astype(out[name].dtype)
    return out
```

```python
import concourse.bass as bass
from concourse import mybir
from contextlib import ExitStack

N, D, E = 3125, 128, 50000
P = 128
NTL = -(-N // P)
TAIL = N - (NTL - 1) * P
NPAD = NTL * P
EP, EC = 125, 400
TILES = 416
BT = 4
NB = TILES // BT
UN = 4
BIG = float(2.0 ** 100)
TINY = 1e-30
CR = 8
NREL = 475
assert EP * EC == E and TILES % (BT * UN) == 0 and TILES >= (E + NTL * (P - 1)) // P

LAYERS = [
    ("conv", 8, 16, 256, True, "dst"),
    ("conv", 8, 16, 256, True, "dst"),
    ("gat", 1, 128, 132, True, "dst"),
    ("gat", 1, 128, 132, True, "dst"),
    ("qkv", 8, 16, 256, False, "src"),
    ("kg", 3, 128, 128, True, "dst"),
]


def done(count):
    return count + 1 + CR


def build(nc, a, out):
    f32, bf16, i32 = mybir.dt.float32, mybir.dt.bfloat16, mybir.dt.int32
    ALU = mybir.AluOpType
    ACT = mybir.ActivationFunctionType
    X = mybir.AxisListType.X

    rec_dram = {k: nc.dram_tensor(f"rec_{k}", (P * TILES, 4), i32).ap() for k in ("dst", "src")}
    table = [nc.dram_tensor(f"table_{n}", (NPAD, l[3]), f32).ap() for n, l in enumerate(LAYERS)]

    with ExitStack() as ctx:
        def sb(name, shape, dt=f32, c=ctx):
            return c.enter_context(nc.sbuf_tensor(name, shape, dt))

        def sem(name):
            return ctx.enter_context(nc.semaphore(name))

        ident = sb("ident", [P, P])
        ident_bf = sb("ident_bf", [P, P], bf16)
        big_ident = sb("big_ident", [P, P], bf16)
        iota_row = sb("iota_row", [P, P])
        ones_row = sb("ones_row", [P, P])
        rec = {k: sb(f"rec_sb_{k}", [P, TILES, 4], i32) for k in ("dst", "src")}
        local = {k: sb(f"local_{k}", [P, TILES]) for k in ("dst", "src")}
        gid = {k: sb(f"gid_{k}", [P, TILES], i32) for k in ("dst", "src")}

        s_const = sem("s_const")
        s_load = sem("s_load")
        s_fill = sem("s_fill")
        s_chain = sem("s_chain")
        s_npb = sem("s_npb")
        s_cnt = sem("s_cnt")
        s_pos = sem("s_pos")
        s_stage = sem("s_stage")
        s_scat = [sem("s_scat0"), sem("s_scat1")]
        s_issue = sem("s_issue")
        s_rec = sem("s_rec")

        with ExitStack() as part:
            def sp_(name, shape, dt=f32):
                return sb(name, shape, dt, part)

            keys = sp_("keys", [EP, 3, EC], i32)
            cum = sp_("cum", [EP, NTL, EC])
            hot = sp_("hot", [EP, NTL, EC])
            cmp = sp_("cmp", [P, TILES, NTL])
            bin_i = sp_("bin_i", [EP, EC], i32)
            bin_f = sp_("bin_f", [EP, EC])
            iota_bin = sp_("iota_bin", [P, NTL])
            iota_tile = sp_("iota_tile", [P, TILES])
            before = sp_("before", [P, P])
            last = sp_("last", [EP, NTL + 1])
            n_bin = sp_("n_bin", [EP, NTL])
            offs = sp_("offs", [EP, NTL])
            tc_i = sp_("tc_i", [P, NTL], i32)
            tc_f = sp_("tc_f", [P, NTL])
            te_f = sp_("te_f", [P, NTL])
            pos_f = sp_("pos_f", [EP, EC])
            pos_i = sp_("pos_i", [EP, EC], i32)
            lo_i = sp_("lo_i", [EP, EC], i32)
            hi_i = sp_("hi_i", [EP, EC], i32)
            addr = {k: sp_(f"addr_{k}", [EP, EC], i32) for k in ("dst", "src")}
            recs = {k: sp_(f"recs_{k}", [EP, EC, 4], i32) for k in ("dst", "src")}
            gid_f = sp_("gid_f", [P, TILES])
            fill = sp_("fill", [P, TILES, 4], i32)
            SB = 8
            st_idx = sp_("st_idx", [EP, 2, SB], i32)
            st_rec = sp_("st_rec", [EP, 2, SB, 4], i32)
            ps_before = part.enter_context(nc.psum_tensor("ps_before", [P, NTL], f32))
            ps_total = part.enter_context(nc.psum_tensor("ps_total", [P, NTL], f32))
            block = part.enter_context(nc.Block())
            col = {"dst": 0, "src": 1}

            @block.sync
            def _(sp):
                for n, name in enumerate(("dst", "src", "edge_type_474")):
                    sp.dma_start(keys[:, n, :], a[name].rearrange("(p c) -> p c", p=EP)).then_inc(s_load, 16)
                sp.wait_ge(s_const, 8)
                for k in ("dst", "src"):
                    sp.dma_start(rec_dram[k].rearrange("(p t) f -> p (t f)", p=P),
                                 fill[:].rearrange("p t f -> p (t f)")).then_inc(s_fill, 16)
                sp.wait_ge(s_scat[0], 2 * (EC // (2 * SB)) * SB * 16)
                sp.wait_ge(s_scat[1], 2 * (EC // (2 * SB)) * SB * 16)
                for k in ("dst", "src"):
                    sp.dma_start(rec[k][:].rearrange("p t f -> p (t f)"),
                                 rec_dram[k].rearrange("(p t) f -> p (t f)", p=P)).then_inc(s_rec, 16)

            @block.gpsimd
            def _(pool):
                nc.gpsimd.iota(iota_row[:], [[1, P]], base=0, channel_multiplier=0,
                               allow_small_or_imprecise_dtypes=True).then_inc(s_const, 1)
                nc.gpsimd.iota(iota_bin[:], [[1, NTL]], base=0, channel_multiplier=0,
                               allow_small_or_imprecise_dtypes=True).then_inc(s_const, 1)
                nc.gpsimd.iota(iota_tile[:], [[1, TILES]], base=0, channel_multiplier=0,
                               allow_small_or_imprecise_dtypes=True).then_inc(s_const, 1)
                nc.gpsimd.memset(ones_row[:], 1.0).then_inc(s_const, 1)
                nc.gpsimd.memset(fill[:], 0).then_inc(s_const, 1)
                pool.wait_ge(s_const, 5)
                nc.gpsimd.memset(fill[:, :, 1:2], 2 * P).then_inc(s_const, 1)
                nc.gpsimd.affine_select(out=ident[:], in_=ones_row[:], compare_op=ALU.is_equal, fill=0.0, base=0,
                                        pattern=[[-1, P]], channel_multiplier=1).then_inc(s_const, 1)
                nc.gpsimd.affine_select(out=before[:], in_=ones_row[:], compare_op=ALU.is_gt, fill=0.0, base=0,
                                        pattern=[[1, P]], channel_multiplier=-1).then_inc(s_const, 1)
                pool.wait_ge(s_fill, 32)
                for q, k in enumerate(("dst", "src")):
                    pool.wait_ge(s_pos, q + 1)
                    half = EC // (2 * SB)

                    def scatter(m, h, reused):
                        if reused:
                            pool.wait_ge(s_scat[h], m * (SB * 16) + q * half * SB * 16)
                        cols = bass.ds(m * (2 * SB) + h * SB, SB)
                        nc.gpsimd.tensor_copy(st_idx[:, h, :], addr[k][:, cols]).then_inc(s_stage, 1)
                        nc.gpsimd.tensor_copy(st_rec[:, h, :, :], recs[k][:, cols, :]).then_inc(s_stage, 1)
                        pool.wait_ge(s_stage, m * 4 + 2 * h + 2 + q * half * 4)
                        pool.sem_inc(s_issue, 1)
                        for c in range(SB):
                            nc.gpsimd.indirect_dma_start(
                                out=rec_dram[k][:, :],
                                out_offset=bass.IndirectOffsetOnAxis(ap=st_idx[:, h, c:c + 1], axis=0),
                                in_=st_rec[:, h, c, :], in_offset=None).then_inc(s_scat[h], 16)

                    for h in range(2):
                        scatter(0, h, q > 0)
                    with pool.Fori(1, half) as m:
                        for h in range(2):
                            scatter(m, h, True)

            @block.tensor
            def _(pe):
                for q in range(2):
                    pe.wait_ge(s_npb, q + 1)
                    nc.tensor.matmul(ps_before[0:EP, :], before[0:EP, 0:EP], n_bin[:], start=True, stop=True)
                    nc.tensor.matmul(ps_total[:], ones_row[0:EP, :], n_bin[:], start=True, stop=True).then_inc(s_cnt, 1)

            @block.vector
            def _(dve):
                count = [0]

                def link(ins):
                    count[0] += 1
                    ins.then_inc(s_chain, 1)
                    dve.wait_ge(s_chain, count[0])

                dve.sem_inc(s_scat[0], 0) if False else None
                dve.wait_ge(s_const, 8)
                link(nc.vector.tensor_copy(ident_bf[:], ident[:]))
                link(nc.vector.tensor_scalar(big_ident[:], ident[:], BIG, None, ALU.mult))
                link(nc.vector.memset(last[:, 0:1], 0.0))
                dve.wait_ge(s_load, 48)
                for q, k in enumerate(("dst", "src")):
                    key, other = keys[:, col[k], :], keys[:, 1 - col[k], :]
                    link(nc.vector.memset(recs[k][:, :, 3:4], 0))
                    link(nc.vector.tensor_copy(recs[k][:, :, 0], other))
                    link(nc.vector.tensor_scalar(recs[k][:, :, 1], key, P - 1, None, ALU.bitwise_and))
                    link(nc.vector.tensor_copy(recs[k][:, :, 2], keys[:, 2, :]))
                    link(nc.vector.tensor_scalar(bin_i[:], key, 7, None, ALU.logical_shift_right))
                    link(nc.vector.tensor_copy(bin_f[:], bin_i[:]))
                    link(nc.vector.tensor_tensor(
                        hot[:], bin_f[:].unsqueeze(1).broadcast_to([EP, NTL, EC]),
                        iota_bin[0:EP].unsqueeze(2).broadcast_to([EP, NTL, EC]), ALU.is_equal))
                    flat_hot = hot[:].rearrange("p b c -> p (b c)")
                    link(nc.vector.tensor_tensor_scan(cum[:].rearrange("p b c -> p (b c)"), flat_hot, flat_hot,
                                                      0.0, ALU.add, ALU.max))
                    link(nc.vector.tensor_copy(last[:, 1:NTL + 1], cum[:, :, EC - 1]))
                    nc.vector.tensor_tensor(n_bin[:], last[:, 1:NTL + 1], last[:, 0:NTL],
                                            ALU.subtract).then_inc(s_npb, 1)
                    dve.wait_ge(s_cnt, q + 1)
                    link(nc.vector.tensor_scalar(tc_f[:], ps_total[:], float(P - 1), None, ALU.add))
                    link(nc.vector.tensor_copy(tc_i[:], tc_f[:]))
                    link(nc.vector.tensor_scalar(tc_i[:], tc_i[:], 7, None, ALU.logical_shift_right))
                    link(nc.vector.tensor_copy(tc_f[:], tc_i[:]))
                    link(nc.vector.tensor_tensor_scan(te_f[:], tc_f[:], tc_f[:], 0.0, ALU.add, ALU.max))
                    link(nc.vector.tensor_tensor(tc_f[:], te_f[:], tc_f[:], ALU.subtract))
                    link(nc.vector.scalar_tensor_tensor(offs[:], tc_f[0:EP], float(P), ps_before[0:EP, :],
                                                        ALU.mult, ALU.add))
                    link(nc.vector.tensor_tensor(offs[:], offs[:], last[:, 0:NTL], ALU.subtract))
                    link(nc.vector.tensor_scalar(offs[:], offs[:], -1.0, None, ALU.add))
                    link(nc.vector.tensor_tensor(cum[:], cum[:], offs[:].unsqueeze(2).broadcast_to([EP, NTL, EC]),
                                                 ALU.add))
                    link(nc.vector.tensor_tensor(cum[:], cum[:], hot[:], ALU.mult))
                    link(nc.vector.tensor_reduce(pos_f[:], cum[:].rearrange("p b c -> p c b"), X, ALU.add))
                    link(nc.vector.tensor_copy(pos_i[:], pos_f[:]))
                    link(nc.vector.tensor_scalar(lo_i[:], pos_i[:], P - 1, None, ALU.bitwise_and))
                    link(nc.vector.tensor_scalar(hi_i[:], pos_i[:], 7, None, ALU.logical_shift_right))
                    nc.vector.scalar_tensor_tensor(addr[k][:], lo_i[:], float(TILES), hi_i[:],
                                                   ALU.mult, ALU.add).then_inc(s_pos, 1)
                    link(nc.vector.tensor_tensor(
                        cmp[:], iota_tile[:].unsqueeze(2).broadcast_to([P, TILES, NTL]),
                        te_f[:].unsqueeze(1).broadcast_to([P, TILES, NTL]), ALU.is_ge))
                    link(nc.vector.tensor_reduce(gid_f[:], cmp[:], X, ALU.add))
                    link(nc.vector.tensor_scalar(gid_f[:], gid_f[:], float(NTL - 1), None, ALU.min))
                    link(nc.vector.tensor_copy(gid[k][:], gid_f[:]))
                dve.wait_ge(s_rec, 32)
                for k in ("dst", "src"):
                    link(nc.vector.tensor_copy(local[k][:], rec[k][:, :, 1]))

        HEAD = {n: l[1] for n, l in enumerate(LAYERS)}
        WMAX = 3 * (P + 1)
        XN = sb("XN", [P, NTL, D])
        HN = sb("HN", [P, NTL, D])
        QN = sb("QN", [P, NTL, D])
        SK = sb("SK", [P, NTL, D + 4])
        ARENA = sb("ARENA", [P, NTL * 136 + NTL * 256])
        MX = sb("MX", [P, NTL, 8])
        AD = sb("AD", [P, NTL, 1])
        NV = sb("NV", [P, NTL, 8])
        NW = sb("NW", [P, NTL, 8])
        W4 = [sb(f"W4_{n}", [D, 4 * D]) for n in range(2)]
        B4 = [sb(f"B4_{n}", [P, 4 * D]) for n in range(2)]
        WG = [sb(f"WG_{n}", [D, D]) for n in range(2)]
        VG = [sb(f"VG_{n}", [P, 3, D]) for n in range(2)]
        WQKV = sb("WQKV", [D, 3 * D])
        WOUT = sb("WOUT", [D, D])
        WKG = sb("WKG", [D, 3, D])
        HS = sb("HS", [P, 2, 3, P])
        HT = sb("HT", [P, 2, 3, P])
        idx = sb("idx", [P, UN, BT], i32)
        idx_rel = sb("idx_rel", [P, UN, BT], i32)
        gat_buf = sb("gat_buf", [P, UN, BT, 256])
        OH = sb("OH", [P, UN, BT, P])
        OHT = sb("OHT", [P, 2, BT, P])
        NM = sb("NM", [P, 2, BT, P], bf16)
        PR = sb("PR", [P, 2, BT, D])
        SC = sb("SC", [P, 2, BT, 8])
        SR = sb("SR", [P, 2, BT * 8])
        S3 = sb("S3", [P, 2, BT * 24], bf16)
        ST = sb("ST", [96, 2, P], bf16)
        SEL = {h: sb(f"SEL{h}", [BT * 3 * h, BT, h, P], bf16) for h in (8, 3, 1)}
        RT = {h: sb(f"RT{h}", [BT * 3 * h, BT, h]) for h in (8, 3, 1)}
        RE = {h: sb(f"RE{h}", [BT * 3 * h, 3, BT, h]) for h in (8, 3, 1)}
        MS = sb("MS", [P, BT, 8])
        MT = sb("MT", [P, 2, BT, 8])
        CA = sb("CA", [P, 2, BT, 8])
        CO = sb("CO", [P, 2, BT, 8])
        SU = sb("SU", [P, 2, BT, 8])
        WV = sb("WV", [P, 2, BT, WMAX])
        SUMR = sb("SUMR", [P, 2, D])

        psum = [ctx.enter_context(nc.psum_tensor(f"bank{n}", [P, 512], f32)) for n in range(8)]
        ps_qe = psum[0:2]
        ps_oht = psum[2]
        ps_me = psum[3]
        ps_st = psum[3]
        ps_sb = psum[4:6]
        ps_ct = psum[6:8]
        ps_ht = psum[0:2]
        ps_pj = psum[4:6]

        names = ("idx_ready rel_ready gather_issued oh_ready ohtps_ready oht_ready nm_ready qe_ready prod_ready pair_ready "
                 "s_ready hi_ready rem_ready s3_ready stps_ready st_ready sb_ready sb_read mt_ready ca_ready "
                 "m_ready me_ready dif_ready sub_ready a_ready co_ready wv_ready ct_ready scaled acc_ready ur_ready").split()
        S = {n: sem(n) for n in names}
        gathered = [sem(f"gathered{k}") for k in range(UN)]
        s_w = sem("s_w")
        s_cst = sem("s_cst")
        s_node = sem("s_node")
        s_hn = sem("s_hn")
        s_var = sem("s_var")
        s_rt = sem("s_rt")
        s_hs = sem("s_hs")
        s_htps = sem("s_htps")
        s_ht = sem("s_ht")
        s_pj = sem("s_pj")
        s_pjr = sem("s_pjr")
        s_tw = sem("s_tw")
        s_td = sem("s_td")
        s_start = sem("s_start")
        s_end = sem("s_end")
        s_th = sem("s_th")
        s_out = sem("s_out")
        block = ctx.enter_context(nc.Block())

        def acc(l):
            h, c = LAYERS[l][1], LAYERS[l][2]
            return ARENA[:, 0:NTL * h * (c + 1)].rearrange("p (t h c) -> p t h c", t=NTL, h=h)

        KV = ARENA[:, NTL * 136:NTL * 136 + NTL * 256].rearrange("p (t c) -> p t c", t=NTL)

        def gb(l):
            return l * NB

        def mb(l):
            return sum(NB for x in LAYERS[:l] if x[4])

        def halves(l):
            return 2 if LAYERS[l][1] == 8 else 1

        def sbb(l):
            return sum(TILES * halves(i) for i in range(l) if LAYERS[i][4])

        def gathers(l):
            return 2 if LAYERS[l][0] == "kg" else 1

        def gbase(l):
            return sum(gathers(i) for i in range(l)) * (NB // UN) * BT * 16

        def arrived(l, q):
            return gbase(l) + (q + 1) * (gathers(l) * BT * 16)

        def steps(eng, body):
            with eng.Fori(0, (NB - UN) // UN) as m:
                for j in range(UN):
                    n = m * UN + (j + 1)
                    body(n, m + (j + 1) // UN, (j + 1) % UN)
            for n in range(NB - UN + 1, NB):
                body(n, n // UN, n % UN)

        def cols(n):
            return bass.ds(n * BT, BT)

        def groups(eng, regs, l, n):
            eng.load(regs, gid[LAYERS[l][5]][0:1, cols(n)])
            return [eng.snap(r, min_val=0, max_val=NTL - 1) for r in regs]

        @block.sync
        def _(sp):
            n_in = 0
            for l in range(2):
                sp.dma_start(W4[l][:], a[f"W4_{l}"]).then_inc(s_w, 16)
                sp.dma_start(B4[l][:], a[f"B4_{l}"].partition_broadcast(P)).then_inc(s_w, 16)
                sp.dma_start(WG[l][:], a[f"L1_gnn_W{l + 1}"]).then_inc(s_w, 16)
                for i, name in enumerate((f"att_src{l + 1}", f"att_dst{l + 1}", f"b{l + 1}")):
                    sp.dma_start(VG[l][:, i, :], a[f"L1_gnn_{name}"].partition_broadcast(P)).then_inc(s_w, 16)
            sp.dma_start(WQKV[:], a["WQKV"]).then_inc(s_w, 16)
            sp.dma_start(WOUT[:], a["WOUT"]).then_inc(s_w, 16)
            for i, name in enumerate(("w_edge", "w_node", "w_comp")):
                sp.dma_start(WKG[:, i, :], a[f"L3_gnn_{name}"]).then_inc(s_w, 16)
            sp.dma_start(XN[:, 0:NTL - 1, :],
                         a["x"][0:(NTL - 1) * P, :].rearrange("(t p) d -> p t d", p=P)).then_inc(s_w, 16)
            sp.wait_ge(s_cst, 1)
            sp.dma_start(XN[0:TAIL, NTL - 1, :], a["x"][(NTL - 1) * P:N, :]).then_inc(s_w, 16)
            for l, (kind, _, _, width, _, _) in enumerate(LAYERS):
                sp.wait_ge(s_tw, l + 1)
                src = {"conv": KV, "qkv": KV, "gat": SK[:], "kg": HN[:]}[kind]
                sp.dma_start(table[l].rearrange("(t p) c -> p t c", p=P), src).then_inc(s_td, 16)
            sp.wait_ge(s_end, len(LAYERS) + 1)
            sp.dma_start(out[0:(NTL - 1) * P, :].rearrange("(t p) d -> p t d", p=P),
                         XN[:, 0:NTL - 1, :]).then_inc(s_out, 16)
            sp.dma_start(out[(NTL - 1) * P:N, :], XN[0:TAIL, NTL - 1, :]).then_inc(s_out, 16)
            sp.wait_ge(s_out, 32)

        N_W = 16 * (2 * 6 + 5 + 2)

        @block.gpsimd
        def _(pool):
            nc.gpsimd.memset(XN[:, NTL - 1, :], 0.0).then_inc(s_cst, 1)
            for h in (8, 3, 1):
                nc.gpsimd.iota(RT[h][:], [[-3 * h, BT], [-1, h]], base=0, channel_multiplier=1,
                               allow_small_or_imprecise_dtypes=True).then_inc(s_cst, 1)
            def stage(j, t, par, src, parts):
                pool.wait_ge(s_htps, j + 1)
                nc.gpsimd.tensor_copy(HS[:, par, 0:parts, :], src(t)).then_inc(s_hs, 1)

            def node_tiles(q, src, parts):
                pool.wait_ge(s_hn, q + 1)
                with pool.Fori(0, NTL // 2) as m:
                    for par in range(2):
                        stage(m * 2 + (q * NTL + par), m * 2 + par, par, src, parts)
                stage(q * NTL + NTL - 1, NTL - 1, 0, src, parts)

            def h_tile(t):
                return HN[:, bass.ds(t, 1), :]

            for l, (kind, _, _, width, _, key) in enumerate(LAYERS):
                node_tiles(l, h_tile, 1)
                pool.wait_ge(s_td, 16 * (l + 1))
                with pool.Fori(0, NB // UN) as m:
                    for k in range(UN):
                        n = m * UN + k
                        pool.wait_ge(S["wv_ready"], done(gb(l) + n - UN))
                        nc.gpsimd.tensor_copy(idx[:, k, :], rec[key][:, cols(n), 0]).then_inc(S["idx_ready"], 1)
                        if kind == "kg":
                            nc.gpsimd.tensor_copy(idx_rel[:, k, :], rec[key][:, cols(n), 2]).then_inc(S["rel_ready"], 1)
                            pool.wait_ge(S["rel_ready"], done(n))
                            pool.sem_inc(S["gather_issued"], 1)
                        pool.wait_ge(S["idx_ready"], done(gb(l) + n))
                        pool.sem_inc(S["gather_issued"], 1)
                        for t in range(BT):
                            nc.gpsimd.indirect_dma_start(
                                out=gat_buf[:, k, t, 0:width], out_offset=None, in_=table[l][:, :],
                                in_offset=bass.IndirectOffsetOnAxis(ap=idx[:, k, t:t + 1], axis=0),
                            ).then_inc(gathered[k], 16)
                            if kind == "kg":
                                nc.gpsimd.indirect_dma_start(
                                    out=gat_buf[:, k, t, D:2 * D], out_offset=None, in_=a["L3_gnn_rel_emb"][:, :],
                                    in_offset=bass.IndirectOffsetOnAxis(ap=idx_rel[:, k, t:t + 1], axis=0),
                                ).then_inc(gathered[k], 16)
            a5 = acc(5)
            node_tiles(6, lambda t: a5[:, bass.ds(t, 1), :, 0:D].rearrange("p a h d -> p (a h) d"), 3)

        @block.scalar
        def _(act):
            def node_sqrt(q):
                act.wait_ge(s_var, q + 1)
                nc.scalar.activation(NW[:, :, 0], NV[:, :, 0], ACT.Sqrt).then_inc(s_rt, 1)

            def evacuate_ht(j, par, parts=1):
                act.wait_ge(s_htps, j + 3)
                act.wait_ge(s_pj, j + 1)
                nc.scalar.activation(HT[:, par, 0:parts, :],
                                     ps_ht[par][:, 0:parts * P].rearrange("p (a b) -> p a b", a=parts),
                                     ACT.Copy).then_inc(s_ht, 1)

            def node_tiles(base, parts=1):
                with act.Fori(0, NTL // 2) as m:
                    for par in range(2):
                        evacuate_ht(m * 2 + (base + par), par, parts)
                evacuate_ht(base + NTL - 1, 0, parts)

            def softmax_layer(l):
                kind, h, c, width, has_max, key = LAYERS[l]

                def transposed_onehots(n, q, k):
                    par = k % 2
                    act.wait_ge(S["ohtps_ready"], done(gb(l) + n))
                    if has_max:
                        act.wait_ge(S["me_ready"], done(mb(l) + n - 2))
                    act.wait_ge(S["qe_ready"], done(gb(l) + n - 2))
                    v = ps_oht[:].rearrange("p (t e) -> p t e", t=BT)
                    nc.scalar.activation(OHT[:, par], v, ACT.Copy).then_inc(S["oht_ready"], 1)
                    nc.scalar.activation(NM[:, par], v, ACT.Copy, bias=-1.0).then_inc(S["nm_ready"], 1)

                def scores_transposed(n, q, k):
                    if not has_max:
                        return
                    rows = BT * 3 * h
                    act.wait_ge(S["stps_ready"], done(mb(l) + n))
                    nc.scalar.activation(ST[0:rows, k % 2, :],
                                         ps_st[0:rows, 128:192].bitcast(bf16), ACT.Copy).then_inc(S["st_ready"], 1)

                def exponentials(n, q, k):
                    par = k % 2
                    act.wait_ge(S["sub_ready"], done(gb(l) + n))
                    act.wait_ge(S["ct_ready"], done((gb(l) + n - 1) * BT - 1))
                    if has_max:
                        act.wait_ge(S["ca_ready"], done((mb(l) + n + 1) * BT - 1))
                        nc.scalar.activation(CO[:, par, :, 0:h], CA[:, par, :, 0:h], ACT.Exp).then_inc(S["co_ready"], 1)
                    w = WV[:, par, :, 0:h * (c + 1)].rearrange("p t (h c) -> p t h c", h=h)
                    nc.scalar.activation(w[:, :, :, c], SU[:, par, :, 0:h], ACT.Exp).then_inc(S["a_ready"], 1)

                def step(n, q, k, more=True):
                    scores_transposed(n, q, k)
                    if more:
                        transposed_onehots(n + 1, q + (k + 1) // UN, (k + 1) % UN)
                    exponentials(n, q, k)

                transposed_onehots(0, 0, 0)
                step(0, 0, 0)
                steps(act, lambda n, q, k: step(n, q, k, not (isinstance(n, int) and n == NB - 1)))

            node_sqrt(0)
            node_tiles(0)
            softmax_layer(0)
            node_tiles(NTL)
            softmax_layer(1)
            node_sqrt(1)
            node_tiles(2 * NTL)
            softmax_layer(2)
            node_tiles(3 * NTL)
            softmax_layer(3)
            node_sqrt(2)
            node_tiles(4 * NTL)
            softmax_layer(4)
            node_tiles(5 * NTL)
            node_sqrt(3)
            softmax_layer(5)
            TH = HT

            def last_tile(j, m_par):
                evacuate_ht(j, m_par, 3)

            with act.Fori(0, NTL // 2) as m:
                for par in range(2):
                    j = m * 2 + (6 * NTL + par)
                    evacuate_ht(j, par, 3)
                    act.wait_ge(s_pj, j + 3)
                    act.wait_ge(s_pjr, j + 1)
                    nc.scalar.activation(PR[:, par, 0:3, :], ps_pj[par][:, 0:3 * P].rearrange("p (a b) -> p a b", a=3),
                                         ACT.Tanh).then_inc(s_th, 1)
            evacuate_ht(7 * NTL - 1, 0, 3)
            act.wait_ge(s_pj, 7 * NTL - 1 + 3)
            act.wait_ge(s_pjr, 7 * NTL - 1 + 1)
            nc.scalar.activation(PR[:, 0, 0:3, :], ps_pj[0][:, 0:3 * P].rearrange("p (a b) -> p a b", a=3),
                                 ACT.Tanh).then_inc(s_th, 1)

        @block.tensor
        def _(pe):
            regs = [pe.alloc_register(f"pe_group{t}") for t in range(BT)]

            def node_tile(j, par, w, parts, width):
                pe.wait_ge(s_hs, j + 1)
                pe.wait_ge(s_ht, j + 1)
                for i in range(parts):
                    last = nc.tensor.transpose(ps_ht[par][:, i * P:(i + 1) * P], HS[:, par, i, :], ident[:])
                last.then_inc(s_htps, 1)
                pe.wait_ge(s_ht, j + 3)
                pe.wait_ge(s_pjr, j + 1)
                for i in range(parts):
                    last = nc.tensor.matmul(ps_pj[par][:, i * P:i * P + width], HT[:, par, i, :], w(i),
                                            start=True, stop=True)
                last.then_inc(s_pj, 1)

            def node_tiles(base, w, parts, width):
                with pe.Fori(0, NTL // 2) as m:
                    for par in range(2):
                        node_tile(m * 2 + (base + par), par, w, parts, width)
                node_tile(base + NTL - 1, 0, w, parts, width)

            def softmax_layer(l):
                kind, h, c, width, has_max, key = LAYERS[l]
                w = h * (c + 1)
                slots = 4 if w <= 256 else 2
                per_bank = slots // 2
                expand = {"conv": QN, "qkv": QN, "gat": AD, "kg": HN}[kind]
                ew = 1 if kind == "gat" else D
                nh = halves(l)
                hp = h // nh

                def onehots_transposed(n, q, k):
                    pe.wait_ge(S["oh_ready"], done(gb(l) + n))
                    pe.wait_ge(S["nm_ready"], done(gb(l) + n - 1))
                    for t in range(BT):
                        last = nc.tensor.transpose(ps_oht[:, t * P:(t + 1) * P], OH[:, k, t, :], ident[:])
                    last.then_inc(S["ohtps_ready"], 1)

                def expansion(n, q, k):
                    par = k % 2
                    gs = groups(pe, regs, l, n)
                    pe.wait_ge(S["oht_ready"], done(gb(l) + n))
                    pe.wait_ge(S["prod_ready"], done(gb(l) + n - 2))
                    for t in range(BT):
                        last = nc.tensor.matmul(ps_qe[par][:, t * P:t * P + ew], OHT[:, par, t, :],
                                                expand[:, bass.ds(gs[t], 1), :].rearrange("p a d -> p (a d)"),
                                                start=True, stop=True)
                    last.then_inc(S["qe_ready"], 1)

                def parts_transposed(n, q, k):
                    if has_max:
                        pe.wait_ge(S["s3_ready"], done(mb(l) + n))
                        nc.tensor.transpose(ps_st[0:96, 128:192].bitcast(bf16), S3[:, k % 2, :],
                                            ident_bf[:]).then_inc(S["stps_ready"], 1)

                def masked_scores(n, q, k):
                    if not has_max:
                        return
                    par, rows = k % 2, BT * 3 * h
                    pe.wait_ge(S["st_ready"], done(mb(l) + n))
                    pe.wait_ge(S["nm_ready"], done(gb(l) + n))
                    for t in range(BT):
                        for g in range(nh):
                            u = t * nh + g
                            pe.wait_ge(S["sb_read"], done(sbb(l) + n * (BT * nh) + u - 2))
                            bank = ps_sb[u % 2]
                            nc.tensor.matmul(bank[:, 0:hp * P], big_ident[:],
                                             NM[:, par, t, :].unsqueeze(1).broadcast_to([P, hp, P]),
                                             start=True, stop=False)
                            for i in range(hp):
                                last = nc.tensor.matmul(bank[:, i * P:(i + 1) * P], SEL[h][0:rows, t, g * hp + i, :],
                                                        ST[0:rows, par, :], start=False, stop=(i == hp - 1))
                            last.then_inc(S["sb_ready"], 1)

                def maxima_expanded(n, q, k):
                    if has_max:
                        par = k % 2
                        pe.wait_ge(S["mt_ready"], done((mb(l) + n + 1) * BT - 1))
                        for t in range(BT):
                            last = nc.tensor.matmul(ps_me[:, par * 32 + t * 8:par * 32 + t * 8 + h],
                                                    OHT[:, par, t, :], MT[:, par, t, 0:h], start=True, stop=True)
                        last.then_inc(S["me_ready"], 1)

                def sums(n, q, k):
                    par = k % 2
                    pe.wait_ge(S["wv_ready"], done(gb(l) + n))
                    for t in range(BT):
                        if t % per_bank == 0:
                            pe.wait_ge(S["acc_ready"], done((gb(l) + n) * BT + t + per_bank - 1 - slots))
                        s = t % slots
                        dst = ps_ct[s // 2][:, (s % 2) * 256:(s % 2) * 256 + w] if slots == 4 else ps_ct[s][:, 0:w]
                        nc.tensor.matmul(dst, OH[:, k, t, :], WV[:, par, t, 0:w],
                                         start=True, stop=True).then_inc(S["ct_ready"], 1)

                def step(n, q, k, more=True):
                    parts_transposed(n, q, k)
                    if more:
                        onehots_transposed(n + 1, q + (k + 1) // UN, (k + 1) % UN)
                    masked_scores(n, q, k)
                    if not (isinstance(n, int) and n == 0):
                        sums(n - 1, None, (k - 1) % UN)
                    maxima_expanded(n, q, k)
                    if more:
                        expansion(n + 1, q + (k + 1) // UN, (k + 1) % UN)

                onehots_transposed(0, 0, 0)
                pe.wait_ge(s_start, l + 1)
                expansion(0, 0, 0)
                step(0, 0, 0)
                steps(pe, lambda n, q, k: step(n, q, k, not (isinstance(n, int) and n == NB - 1)))
                sums(NB - 1, None, (NB - 1) % UN)

            pe.wait_ge(s_w, N_W)
            for q, (w, width) in enumerate(((W4[0], 512), (W4[1], 512), (WG[0], 128), (WG[1], 128), (WQKV, 384))):
                node_tiles(q * NTL, lambda i, w=w, width=width: w[:, 0:width], 1, width)
                softmax_layer(q)
            node_tiles(5 * NTL, lambda i: WOUT[:], 1, D)
            softmax_layer(5)
            node_tiles(6 * NTL, lambda i: WKG[:, i, :], 3, P)

        @block.vector
        def _(dve):
            regs = [dve.alloc_register(f"dve_group{t}") for t in range(BT)]
            count = [0]

            def link(ins):
                count[0] += 1
                ins.then_inc(s_node, 1)
                dve.wait_ge(s_node, count[0])

            def over(v, n=D):
                return v.unsqueeze(2).broadcast_to([P, NTL, n])

            def along(v):
                return v.unsqueeze(1).broadcast_to([P, NTL, D])

            def layer_norm_relu(q):
                link(nc.vector.tensor_reduce(NV[:, :, 1], XN[:], X, ALU.add))
                link(nc.vector.tensor_scalar(NV[:, :, 1], NV[:, :, 1], 1.0 / D, None, ALU.mult))
                link(nc.vector.tensor_tensor(HN[:], XN[:], over(NV[:, :, 1]), ALU.subtract))
                link(nc.vector.tensor_tensor(QN[:], HN[:], HN[:], ALU.mult))
                link(nc.vector.tensor_reduce(NV[:, :, 2], QN[:], X, ALU.add))
                nc.vector.tensor_scalar(NV[:, :, 0], NV[:, :, 2], 1.0 / D, 1e-5, ALU.mult, ALU.add).then_inc(s_var, 1)
                dve.wait_ge(s_rt, q + 1)
                link(nc.vector.reciprocal(NW[:, :, 1], NW[:, :, 0]))
                link(nc.vector.tensor_tensor(HN[:], HN[:], over(NW[:, :, 1]), ALU.mult))
                link(nc.vector.tensor_scalar(HN[:], HN[:], 0.0, None, ALU.max))

            def products(base, body):
                with dve.Fori(0, NTL // 2) as m:
                    for par in range(2):
                        dve.wait_ge(s_pj, m * 2 + (base + par + 3))
                        body(m * 2 + par, par).then_inc(s_pjr, 1)
                dve.wait_ge(s_pj, base + NTL - 1 + 3)
                body(NTL - 1, 0).then_inc(s_pjr, 1)

            def at(v, t):
                return v[:, bass.ds(t, 1), :].rearrange("p a d -> p (a d)")

            def settle(base):
                dve.wait_ge(s_pjr, base + NTL + 2)

            def normalised_heads(l, guard_add):
                h, c = LAYERS[l][1], LAYERS[l][2]
                s = acc(l)
                w = NV[:, :, 0:h]
                if guard_add:
                    link(nc.vector.tensor_scalar(w, s[:, :, :, c], guard_add, None, ALU.add))
                else:
                    link(nc.vector.tensor_scalar(w, s[:, :, :, c], TINY, None, ALU.max))
                link(nc.vector.reciprocal(NW[:, :, 0:h], w))
                for i in range(0, h, 1 if h == 3 else h):
                    pass
                if h == 8:
                    hn = HN[:].rearrange("p t (h c) -> p (t h) c", h=h)
                    link(nc.vector.tensor_tensor(
                        hn, s.rearrange("p t h c -> p (t h) c")[:, :, 0:c],
                        NW[:].rearrange("p t h -> p (t h)").unsqueeze(2).broadcast_to([P, NTL * h, c]), ALU.mult))
                elif h == 1:
                    link(nc.vector.tensor_tensor(HN[:], s[:, :, 0, 0:c], over(NW[:, :, 0]), ALU.mult))
                else:
                    for i in range(h):
                        link(nc.vector.tensor_tensor(s[:, :, i, 0:c], s[:, :, i, 0:c], over(NW[:, :, i]), ALU.mult))

            def softmax_layer(l):
                kind, h, c, width, has_max, key = LAYERS[l]
                w = h * (c + 1)
                slots = 4 if w <= 256 else 2
                per_bank = slots // 2
                nh = halves(l)
                hp = h // nh
                sums = acc(l)

                def onehots(n, q, k):
                    nc.vector.tensor_tensor(
                        OH[:, k], iota_row[:].unsqueeze(1).broadcast_to([P, BT, P]),
                        local[key][:, cols(n)].unsqueeze(2).broadcast_to([P, BT, P]),
                        ALU.is_equal).then_inc(S["oh_ready"], 1)

                def scores(n, q, k):
                    par = k % 2
                    s = SC[:, par, :, 0:h]
                    dve.wait_ge(S["qe_ready"], done(gb(l) + n))
                    dve.wait_ge(gathered[k], arrived(l, q))
                    qe = ps_qe[par][:].rearrange("p (t d) -> p t d", t=BT)
                    g = gat_buf[:, k]
                    if kind in ("conv", "qkv"):
                        nc.vector.tensor_tensor(PR[:, 0], qe, g[:, :, 0:D], ALU.mult).then_inc(S["prod_ready"], 1)
                        dve.wait_ge(S["prod_ready"], done(gb(l) + n))
                        nc.vector.tensor_reduce(SC[:, par, :, :].rearrange("p t h -> p (t h)"),
                                                PR[:, 0].rearrange("p t (h c) -> p (t h) c", h=h),
                                                X, ALU.add).then_inc(S["s_ready"], 1)
                    elif kind == "gat":
                        nc.vector.tensor_tensor(PR[:, 0, :, 0:1], qe[:, :, 0:1], g[:, :, D:D + 1],
                                                ALU.add).then_inc(S["prod_ready"], 1)
                        dve.wait_ge(S["prod_ready"], done(gb(l) + n))
                        nc.vector.scalar_tensor_tensor(s, PR[:, 0, :, 0:1], 0.2, PR[:, 0, :, 0:1],
                                                       ALU.mult, ALU.max).then_inc(S["s_ready"], 1)
                    else:
                        nc.vector.tensor_tensor(PR[:, 0], qe, g[:, :, D:2 * D], ALU.mult)
                        nc.vector.tensor_tensor(PR[:, 1], qe, g[:, :, 0:D], ALU.mult).then_inc(S["prod_ready"], 1)
                        dve.wait_ge(S["prod_ready"], done(gb(l) + n))
                        nc.vector.tensor_reduce(SC[:, par, :, 0], PR[:, 0], X, ALU.add)
                        nc.vector.tensor_reduce(SC[:, par, :, 1], PR[:, 1], X, ALU.add).then_inc(S["pair_ready"], 1)
                        dve.wait_ge(S["pair_ready"], done(n))
                        nc.vector.tensor_tensor(SC[:, par, :, 2], SC[:, par, :, 0], SC[:, par, :, 1],
                                                ALU.add).then_inc(S["s_ready"], 1)
                    dve.wait_ge(S["s_ready"], done(gb(l) + n))
                    if has_max:
                        s3 = S3[:, par, 0:BT * 3 * h].rearrange("p (t r) -> p t r", t=BT)
                        r = SR[:, par, 0:BT * h].rearrange("p (t h) -> p t h", h=h)
                        nc.vector.tensor_copy(s3[:, :, 0:h], s).then_inc(S["hi_ready"], 1)
                        dve.wait_ge(S["hi_ready"], done(mb(l) + n))
                        nc.vector.tensor_tensor(r, s, s3[:, :, 0:h], ALU.subtract).then_inc(S["rem_ready"], 1)
                        dve.wait_ge(S["rem_ready"], done(2 * (mb(l) + n)))
                        nc.vector.tensor_copy(s3[:, :, h:2 * h], r).then_inc(S["rem_ready"], 1)
                        dve.wait_ge(S["rem_ready"], done(2 * (mb(l) + n) + 1))
                        nc.vector.tensor_tensor(s3[:, :, 2 * h:3 * h], r, s3[:, :, h:2 * h],
                                                ALU.subtract).then_inc(S["s3_ready"], 1)
                    else:
                        nc.vector.tensor_scalar(SU[:, par, :, 0:h], s, -10.0, 10.0, ALU.max,
                                                ALU.min).then_inc(S["sub_ready"], 1)

                def maxima(n, q, k, gs):
                    par = k % 2
                    for t in range(BT):
                        tile_ = (mb(l) + n) * BT + t
                        for g in range(nh):
                            u = t * nh + g
                            dve.wait_ge(S["sb_ready"], done(sbb(l) + n * (BT * nh) + u))
                            nc.vector.tensor_reduce(
                                MS[:, t, g * hp:(g + 1) * hp],
                                ps_sb[u % 2][:, 0:hp * P].rearrange("p (h e) -> p h e", h=hp),
                                X, ALU.max).then_inc(S["sb_read"], 1)
                        m_old = MX[:, bass.ds(gs[t], 1), 0:h].rearrange("p a h -> p (a h)")
                        dve.wait_ge(S["sb_read"], done(sbb(l) + n * (BT * nh) + t * nh + nh - 1))
                        dve.wait_ge(S["m_ready"], done(tile_ - 1))
                        nc.vector.tensor_tensor(MT[:, par, t, 0:h], m_old, MS[:, t, 0:h],
                                                ALU.max).then_inc(S["mt_ready"], 1)
                        dve.wait_ge(S["mt_ready"], done(tile_))
                        nc.vector.tensor_tensor(CA[:, par, t, 0:h], m_old, MT[:, par, t, 0:h],
                                                ALU.subtract).then_inc(S["ca_ready"], 1)
                        dve.wait_ge(S["ca_ready"], done(tile_))
                        nc.vector.tensor_tensor(m_old, MT[:, par, t, 0:h], MS[:, t, 0:h], ALU.max).then_inc(S["m_ready"], 1)

                def below_maximum(n, q, k):
                    par = k % 2
                    su = SU[:, par, :, 0:h]
                    me = ps_me[:, par * 32:(par + 1) * 32].rearrange("p (t h) -> p t h", t=BT)[:, :, 0:h]
                    dve.wait_ge(S["me_ready"], done(mb(l) + n))
                    nc.vector.tensor_tensor(su, SC[:, par, :, 0:h], me, ALU.subtract).then_inc(S["dif_ready"], 1)
                    dve.wait_ge(S["dif_ready"], done(mb(l) + n))
                    nc.vector.tensor_scalar(su, su, 0.0, None, ALU.min).then_inc(S["sub_ready"], 1)

                def weighted(n, k):
                    par = k % 2
                    dve.wait_ge(S["a_ready"], done(gb(l) + n))
                    g = gat_buf[:, k]
                    wv = WV[:, par, :, 0:w].rearrange("p t (h c) -> p t h c", h=h)
                    if h == 8:
                        for t in range(BT):
                            last = nc.vector.tensor_tensor(
                                wv[:, t, :, 0:c], g[:, t, D:2 * D].rearrange("p (h c) -> p h c", h=h),
                                wv[:, t, :, c:c + 1].broadcast_to([P, h, c]), ALU.mult)
                    elif h == 1:
                        last = nc.vector.tensor_tensor(wv[:, :, 0, 0:c], g[:, :, 0:D],
                                                       wv[:, :, 0, c:c + 1].broadcast_to([P, BT, c]), ALU.mult)
                    else:
                        nc.vector.tensor_tensor(PR[:, 0], g[:, :, 0:D], g[:, :, D:2 * D],
                                                ALU.add).then_inc(S["ur_ready"], 1)
                        dve.wait_ge(S["ur_ready"], done(n))
                        for i, rows in enumerate((g[:, :, D:2 * D], g[:, :, 0:D], PR[:, 0])):
                            last = nc.vector.tensor_tensor(wv[:, :, i, 0:c], rows,
                                                           wv[:, :, i, c:c + 1].broadcast_to([P, BT, c]), ALU.mult)
                    last.then_inc(S["wv_ready"], 1)

                def add_up(n, k, gs):
                    par = k % 2
                    for t in range(BT):
                        tile_ = (gb(l) + n) * BT + t
                        s = t % slots
                        ct = ps_ct[s // 2][:, (s % 2) * 256:(s % 2) * 256 + w] if slots == 4 else ps_ct[s][:, 0:w]
                        total = sums[:, bass.ds(gs[t], 1)].rearrange("p a h c -> p (a h) c")
                        dve.wait_ge(S["acc_ready"], done(tile_ - 1))
                        if has_max:
                            dve.wait_ge(S["co_ready"], done(mb(l) + n))
                        if has_max and h == 8:
                            nc.vector.tensor_tensor(total, total, CO[:, par, t, :].unsqueeze(2).broadcast_to([P, h, c + 1]),
                                                    ALU.mult).then_inc(S["scaled"], 1)
                            dve.wait_ge(S["scaled"], done(tile_))
                        dve.wait_ge(S["ct_ready"], done(tile_ + per_bank - 1 - t % per_bank))
                        ctv = ct.rearrange("p (h c) -> p h c", h=h)
                        if h == 8:
                            last = nc.vector.tensor_tensor(total, total, ctv, ALU.add)
                        else:
                            for i in range(h):
                                last = nc.vector.scalar_tensor_tensor(total[:, i, :], total[:, i, :],
                                                                      CO[:, par, t, i:i + 1], ctv[:, i, :],
                                                                      ALU.mult, ALU.add)
                        last.then_inc(S["acc_ready"], 1)

                def step(n, q, k, more=True, previous=True):
                    scores(n, q, k)
                    if more:
                        onehots(n + 1, None, (k + 1) % UN)
                    if previous:
                        weighted(n - 1, (k - 1) % UN)
                    if has_max:
                        maxima(n, q, k, groups(dve, regs, l, n))
                    if previous:
                        add_up(n - 1, (k - 1) % UN, groups(dve, regs, l, n - 1))
                    if has_max:
                        below_maximum(n, q, k)

                onehots(0, 0, 0)
                step(0, 0, 0, previous=False)
                steps(dve, lambda n, q, k: step(n, q, k, not (isinstance(n, int) and n == NB - 1)))
                weighted(NB - 1, (NB - 1) % UN)
                add_up(NB - 1, (NB - 1) % UN, groups(dve, regs, l, NB - 1))
                dve.wait_ge(S["acc_ready"], done(gb(l + 1) * BT - 1))
                dve.sem_inc(s_end, 1)

            def clear(l):
                link(nc.vector.memset(acc(l), 0.0))
                link(nc.vector.memset(MX[:], -BIG))

            for s in S.values():
                dve.sem_inc(s, CR)
            dve.sem_inc(s_ht, 2)
            dve.sem_inc(s_htps, 2)
            dve.sem_inc(s_pj, 2)
            dve.sem_inc(s_pjr, 2)
            dve.wait_ge(s_cst, 4)
            link(nc.vector.memset(S3[:], 0.0))
            for h in (8, 3, 1):
                for part in range(3):
                    link(nc.vector.tensor_scalar(RE[h][:, part], RT[h][:], float(part * h), None, ALU.is_equal))
                link(nc.vector.tensor_tensor(RE[h][:, 0], RE[h][:, 0], RE[h][:, 1], ALU.add))
                link(nc.vector.tensor_tensor(RE[h][:, 0], RE[h][:, 0], RE[h][:, 2], ALU.add))
                link(nc.vector.tensor_copy(SEL[h][:], RE[h][:, 0].unsqueeze(3).broadcast_to([BT * 3 * h, BT, h, P])))
            dve.wait_ge(s_w, N_W)
            for l in range(2):
                link(nc.vector.tensor_scalar(B4[l][:, 0:D], B4[l][:, 0:D], 0.25, None, ALU.mult))

            layer_norm_relu(0)
            for l in range(2):
                dve.sem_inc(s_hn, 1)

                def conv_products(t, par, l=l):
                    ps = ps_pj[par]
                    nc.vector.scalar_tensor_tensor(at(QN, t), ps[:, 0:D], 0.25, B4[l][:, 0:D], ALU.mult, ALU.add)
                    nc.vector.tensor_tensor(at(KV, t), ps[:, D:3 * D], B4[l][:, D:3 * D], ALU.add)
                    return nc.vector.tensor_tensor(at(SK[:, :, 0:D], t), ps[:, 3 * D:4 * D], B4[l][:, 3 * D:4 * D],
                                                   ALU.add)

                products(l * NTL, conv_products)
                settle(l * NTL)
                dve.sem_inc(s_tw, 1)
                clear(l)
                dve.sem_inc(s_start, 1)
                softmax_layer(l)
                normalised_heads(l, None)
                link(nc.vector.tensor_tensor(HN[:], HN[:], SK[:, :, 0:D], ALU.add))
                if l == 0:
                    link(nc.vector.tensor_scalar(HN[:], HN[:], 0.0, None, ALU.max))
            link(nc.vector.tensor_tensor(XN[:], XN[:], HN[:], ALU.add))

            layer_norm_relu(1)
            for g in range(2):
                l = 2 + g
                dve.sem_inc(s_hn, 1)
                products(l * NTL, lambda t, par: nc.vector.tensor_copy(at(SK[:, :, 0:D], t), ps_pj[par][:, 0:D]))
                settle(l * NTL)
                link(nc.vector.tensor_tensor(QN[:], SK[:, :, 0:D], along(VG[g][:, 0, :]), ALU.mult))
                link(nc.vector.tensor_reduce(SK[:, :, D], QN[:], X, ALU.add))
                link(nc.vector.memset(SK[:, :, D + 1:D + 4], 0.0))
                dve.sem_inc(s_tw, 1)
                link(nc.vector.tensor_tensor(QN[:], SK[:, :, 0:D], along(VG[g][:, 1, :]), ALU.mult))
                link(nc.vector.tensor_reduce(AD[:, :, 0], QN[:], X, ALU.add))
                link(nc.vector.tensor_tensor(NV[:, :, 0], SK[:, :, D], AD[:, :, 0], ALU.add))
                link(nc.vector.scalar_tensor_tensor(MX[:, :, 0], NV[:, :, 0], 0.2, NV[:, :, 0], ALU.mult, ALU.max))
                link(nc.vector.tensor_copy(acc(l)[:, :, 0, 0:D], SK[:, :, 0:D]))
                link(nc.vector.memset(acc(l)[:, :, 0, D:D + 1], 1.0))
                dve.sem_inc(s_start, 1)
                softmax_layer(l)
                normalised_heads(l, 1e-16)
                link(nc.vector.tensor_tensor(HN[:], HN[:], along(VG[g][:, 2, :]), ALU.add))
                link(nc.vector.tensor_scalar(HN[:], HN[:], 0.0, None, ALU.max))
            link(nc.vector.tensor_tensor(XN[:], XN[:], HN[:], ALU.add))

            layer_norm_relu(2)
            dve.sem_inc(s_hn, 1)

            def qkv_products(t, par):
                ps = ps_pj[par]
                nc.vector.tensor_scalar(at(QN, t), ps[:, 0:D], 0.25, None, ALU.mult)
                return nc.vector.tensor_copy(at(KV, t), ps[:, D:3 * D])

            products(4 * NTL, qkv_products)
            settle(4 * NTL)
            dve.sem_inc(s_tw, 1)
            clear(4)
            dve.sem_inc(s_start, 1)
            softmax_layer(4)
            normalised_heads(4, 1e-8)
            dve.sem_inc(s_hn, 1)
            products(5 * NTL, lambda t, par: nc.vector.tensor_tensor(at(XN, t), at(XN, t), ps_pj[par][:, 0:D], ALU.add))
            settle(5 * NTL)

            layer_norm_relu(3)
            dve.sem_inc(s_tw, 1)
            clear(5)
            dve.sem_inc(s_start, 1)
            softmax_layer(5)
            normalised_heads(5, None)
            link(nc.vector.tensor_tensor(XN[:], XN[:], HN[:], ALU.add))
            dve.sem_inc(s_hn, 1)

            def add_tanh(t, par, q):
                dve.wait_ge(s_pjr, q + 6 * NTL + 1)
                dve.wait_ge(s_th, q + 1)
                nc.vector.tensor_reduce(SUMR[:, par, :], PR[:, par, 0:3, :].rearrange("p a d -> p d a"), X,
                                        ALU.add).then_inc(S["ur_ready"], 1)
                dve.wait_ge(S["ur_ready"], done(NB + q))
                nc.vector.tensor_tensor(at(XN, t), at(XN, t), SUMR[:, par, :], ALU.add).then_inc(s_pjr, 1)

            with dve.Fori(0, NTL // 2) as m:
                for par in range(2):
                    add_tanh(m * 2 + par, par, m * 2 + par)
            add_tanh(NTL - 1, 0, NTL - 1)
            settle(6 * NTL)
            dve.sem_inc(s_end, 1)


def kernel(**inputs):
    import numpy as np
    import concourse.bacc as bacc
    from concourse.bass_utils import run_bass_kernel_spmd

    x = {k: np.asarray(v) for k, v in inputs.items()}
    arrays = {k: x[k] for k in ("x", "src", "dst", "edge_type_474", "L1_gnn_W1", "L1_gnn_W2", "L3_gnn_rel_emb",
                                "L3_gnn_w_edge", "L3_gnn_w_node", "L3_gnn_w_comp")}
    for l in range(2):
        for kind in ("W4", "B4"):
            part = "w" if kind == "W4" else "b"
            arrays[f"{kind}_{l}"] = np.concatenate([x[f"L0_gnn_{n}_{part}{l}"] for n in "qkvs"], axis=-1)
        for n in (f"att_src{l + 1}", f"att_dst{l + 1}", f"b{l + 1}"):
            arrays[f"L1_gnn_{n}"] = x[f"L1_gnn_{n}"].reshape(D)
    arrays["WQKV"] = np.ascontiguousarray(x["L2_gnn_W_qkv"].T)
    arrays["WOUT"] = np.ascontiguousarray(x["L2_gnn_W_out"].T)

    nc = bacc.Bacc("TRN2", target_bir_lowering=False, num_devices=1)
    feed, aps = {}, {}
    for name, v in arrays.items():
        feed[f"in_{name}"] = np.ascontiguousarray(v)
        aps[name] = nc.dram_tensor(f"in_{name}", v.shape, mybir.dt.from_np(v.dtype), kind="ExternalInput").ap()
    out = nc.dram_tensor("out", (N, D), mybir.dt.float32, kind="ExternalOutput").ap()
    build(nc, aps, out)
    r = run_bass_kernel_spmd(nc, [feed], core_ids=[0])
    return r.results[0]["out"]
```

```python
import concourse.bass as bass
from concourse import mybir
from contextlib import ExitStack

N, D, E = 3125, 128, 50000
P = 128
NTL = -(-N // P)
TAIL = N - (NTL - 1) * P
NPAD = NTL * P
EP, EC = 125, 400
BT = 4
SLOTS = BT * P
NB = (E + NTL * (SLOTS - 1)) // SLOTS
TILES = NB * BT
UN = 4
LOOPS = (NB - 5) // UN
BIG = float(2.0 ** 100)
TINY = 1e-30
CR = 8
NREL = 475
SHIFT = SLOTS.bit_length() - 1
assert EP * EC == E and SLOTS == 1 << SHIFT and NB - 1 - LOOPS * UN >= 2

LAYERS = [
    ("conv", 8, 16, 256, True, "dst"),
    ("conv", 8, 16, 256, True, "dst"),
    ("gat", 1, 128, 132, True, "dst"),
    ("gat", 1, 128, 132, True, "dst"),
    ("qkv", 8, 16, 256, False, "src"),
    ("kg", 3, 128, 128, True, "dst"),
]


def done(count):
    return count + 1 + CR


def build(nc, a, out):
    f32, bf16, i32 = mybir.dt.float32, mybir.dt.bfloat16, mybir.dt.int32
    ALU = mybir.AluOpType
    ACT = mybir.ActivationFunctionType
    X = mybir.AxisListType.X

    rec_dram = {k: nc.dram_tensor(f"rec_{k}", (P * TILES, 4), i32).ap() for k in ("dst", "src")}
    table = [nc.dram_tensor(f"table_{n}", (NPAD, l[3]), f32).ap() for n, l in enumerate(LAYERS)]

    with ExitStack() as ctx:
        def sb(name, shape, dt=f32, c=ctx):
            return c.enter_context(nc.sbuf_tensor(name, shape, dt))

        def sem(name):
            return ctx.enter_context(nc.semaphore(name))

        ident = sb("ident", [P, P])
        ident_bf = sb("ident_bf", [P, P], bf16)
        big_ident = sb("big_ident", [P, P], bf16)
        iota_row = sb("iota_row", [P, P])
        ones_row = sb("ones_row", [P, P])
        other_end = {k: sb(f"other_end_{k}", [P, TILES], i32) for k in ("dst", "src")}
        relation = sb("relation", [P, TILES], i32)
        addr = {"src": sb("addr_src", [EP, EC], i32)}
        recs = {"src": sb("recs_src", [EP, EC, 4], i32)}
        neg_local = {k: sb(f"neg_local_{k}", [P, TILES]) for k in ("dst", "src")}
        gid = {k: sb(f"gid_{k}", [P, NB], i32) for k in ("dst", "src")}

        s_const = sem("s_const")
        s_load = sem("s_load")
        s_fill = sem("s_fill")
        s_chain = sem("s_chain")
        s_npb = sem("s_npb")
        s_cnt = sem("s_cnt")
        s_pos = sem("s_pos")
        s_stage = sem("s_stage")
        s_scat = [sem("s_scat0"), sem("s_scat1")]
        s_issue = sem("s_issue")
        s_rec = sem("s_rec")

        with ExitStack() as part:
            def sp_(name, shape, dt=f32):
                return sb(name, shape, dt, part)

            keys = sp_("keys", [EP, 3, EC], i32)
            cum = sp_("cum", [EP, NTL, EC])
            hot = sp_("hot", [EP, NTL, EC])
            cmp = sp_("cmp", [P, NB, NTL])
            bin_i = sp_("bin_i", [EP, EC], i32)
            bin_f = sp_("bin_f", [EP, EC])
            iota_bin = sp_("iota_bin", [P, NTL])
            iota_batch = sp_("iota_batch", [P, NB])
            before = sp_("before", [P, P])
            last = sp_("last", [EP, NTL + 1])
            n_bin = sp_("n_bin", [EP, NTL])
            offs = sp_("offs", [EP, NTL])
            tc_i = sp_("tc_i", [P, NTL], i32)
            tc_f = sp_("tc_f", [P, NTL])
            te_f = sp_("te_f", [P, NTL])
            pos_f = sp_("pos_f", [EP, EC])
            pos_i = sp_("pos_i", [EP, EC], i32)
            lo_i = sp_("lo_i", [EP, EC], i32)
            hi_i = sp_("hi_i", [EP, EC], i32)
            addr["dst"] = sp_("addr_dst", [EP, EC], i32)
            recs["dst"] = sp_("recs_dst", [EP, EC, 4], i32)
            rec = sp_("rec", [P, TILES, 4], i32)
            gid_f = sp_("gid_f", [P, NB])
            fill = sp_("fill", [P, TILES, 4], i32)
            SB = 8
            st_idx = sp_("st_idx", [EP, 2, SB], i32)
            st_rec = sp_("st_rec", [EP, 2, SB, 4], i32)
            ps_before = part.enter_context(nc.psum_tensor("ps_before", [P, NTL], f32))
            ps_total = part.enter_context(nc.psum_tensor("ps_total", [P, NTL], f32))
            block = part.enter_context(nc.Block())
            col = {"dst": 0, "src": 1}

            @block.sync
            def _(sp):
                for n, name in enumerate(("dst", "src", "edge_type_474")):
                    sp.dma_start(keys[:, n, :], a[name].rearrange("(p c) -> p c", p=EP)).then_inc(s_load, 16)
                sp.wait_ge(s_const, 8)
                for k in ("dst", "src"):
                    sp.dma_start(rec_dram[k].rearrange("(p t) f -> p (t f)", p=P),
                                 fill[:].rearrange("p t f -> p (t f)")).then_inc(s_fill, 16)
                for h in range(2):
                    sp.wait_ge(s_scat[h], EC // 2 * 16)
                sp.dma_start(rec[:].rearrange("p t f -> p (t f)"),
                             rec_dram["dst"].rearrange("(p t) f -> p (t f)", p=P)).then_inc(s_rec, 16)

            @block.gpsimd
            def _(pool):
                nc.gpsimd.iota(iota_row[:], [[1, P]], base=0, channel_multiplier=0,
                               allow_small_or_imprecise_dtypes=True).then_inc(s_const, 1)
                nc.gpsimd.iota(iota_bin[:], [[1, NTL]], base=0, channel_multiplier=0,
                               allow_small_or_imprecise_dtypes=True).then_inc(s_const, 1)
                nc.gpsimd.iota(iota_batch[:], [[1, NB]], base=0, channel_multiplier=0,
                               allow_small_or_imprecise_dtypes=True).then_inc(s_const, 1)
                nc.gpsimd.memset(ones_row[:], 1.0).then_inc(s_const, 1)
                nc.gpsimd.memset(fill[:], 0).then_inc(s_const, 1)
                pool.wait_ge(s_const, 5)
                nc.gpsimd.memset(fill[:, :, 1:2], 2 * P).then_inc(s_const, 1)
                nc.gpsimd.affine_select(out=ident[:], in_=ones_row[:], compare_op=ALU.is_equal, fill=0.0, base=0,
                                        pattern=[[-1, P]], channel_multiplier=1).then_inc(s_const, 1)
                nc.gpsimd.affine_select(out=before[:], in_=ones_row[:], compare_op=ALU.is_gt, fill=0.0, base=0,
                                        pattern=[[1, P]], channel_multiplier=-1).then_inc(s_const, 1)
                pool.wait_ge(s_fill, 32)
                pool.wait_ge(s_pos, 1)

                def scatter(m, h, reused):
                    if reused:
                        pool.wait_ge(s_scat[h], m * (SB * 16))
                    at_ = bass.ds(m * (2 * SB) + h * SB, SB)
                    nc.gpsimd.tensor_copy(st_idx[:, h, :], addr["dst"][:, at_]).then_inc(s_stage, 1)
                    nc.gpsimd.tensor_copy(st_rec[:, h, :, :], recs["dst"][:, at_, :]).then_inc(s_stage, 1)
                    pool.wait_ge(s_stage, m * 4 + 2 * h + 2)
                    pool.sem_inc(s_issue, 1)
                    for c in range(SB):
                        nc.gpsimd.indirect_dma_start(
                            out=rec_dram["dst"][:, :],
                            out_offset=bass.IndirectOffsetOnAxis(ap=st_idx[:, h, c:c + 1], axis=0),
                            in_=st_rec[:, h, c, :], in_offset=None).then_inc(s_scat[h], 16)

                for h in range(2):
                    scatter(0, h, False)
                with pool.Fori(1, EC // (2 * SB)) as m:
                    for h in range(2):
                        scatter(m, h, True)

            @block.tensor
            def _(pe):
                for q in range(2):
                    pe.wait_ge(s_npb, q + 1)
                    nc.tensor.matmul(ps_before[0:EP, :], before[0:EP, 0:EP], n_bin[:], start=True, stop=True)
                    nc.tensor.matmul(ps_total[:], ones_row[0:EP, :], n_bin[:], start=True, stop=True).then_inc(s_cnt, 1)

            @block.vector
            def _(dve):
                count = [0]

                def link(ins):
                    count[0] += 1
                    ins.then_inc(s_chain, 1)
                    dve.wait_ge(s_chain, count[0])

                dve.sem_inc(s_scat[0], 0) if False else None
                dve.wait_ge(s_const, 8)
                link(nc.vector.tensor_copy(ident_bf[:], ident[:]))
                link(nc.vector.tensor_scalar(big_ident[:], ident[:], BIG, None, ALU.mult))
                link(nc.vector.memset(last[:, 0:1], 0.0))
                dve.wait_ge(s_load, 48)
                for q, k in enumerate(("dst", "src")):
                    key, other = keys[:, col[k], :], keys[:, 1 - col[k], :]
                    link(nc.vector.memset(recs[k][:, :, 3:4], 0))
                    link(nc.vector.tensor_copy(recs[k][:, :, 0], other))
                    link(nc.vector.tensor_scalar(recs[k][:, :, 1], key, P - 1, None, ALU.bitwise_and))
                    link(nc.vector.tensor_copy(recs[k][:, :, 2], keys[:, 2, :]))
                    link(nc.vector.tensor_scalar(bin_i[:], key, 7, None, ALU.logical_shift_right))
                    link(nc.vector.tensor_copy(bin_f[:], bin_i[:]))
                    link(nc.vector.tensor_tensor(
                        hot[:], bin_f[:].unsqueeze(1).broadcast_to([EP, NTL, EC]),
                        iota_bin[0:EP].unsqueeze(2).broadcast_to([EP, NTL, EC]), ALU.is_equal))
                    flat_hot = hot[:].rearrange("p b c -> p (b c)")
                    link(nc.vector.tensor_tensor_scan(cum[:].rearrange("p b c -> p (b c)"), flat_hot, flat_hot,
                                                      0.0, ALU.add, ALU.max))
                    link(nc.vector.tensor_copy(last[:, 1:NTL + 1], cum[:, :, EC - 1]))
                    nc.vector.tensor_tensor(n_bin[:], last[:, 1:NTL + 1], last[:, 0:NTL],
                                            ALU.subtract).then_inc(s_npb, 1)
                    dve.wait_ge(s_cnt, q + 1)
                    link(nc.vector.tensor_scalar(tc_f[:], ps_total[:], float(SLOTS - 1), None, ALU.add))
                    link(nc.vector.tensor_copy(tc_i[:], tc_f[:]))
                    link(nc.vector.tensor_scalar(tc_i[:], tc_i[:], SHIFT, None, ALU.logical_shift_right))
                    link(nc.vector.tensor_copy(tc_f[:], tc_i[:]))
                    link(nc.vector.tensor_tensor_scan(te_f[:], tc_f[:], tc_f[:], 0.0, ALU.add, ALU.max))
                    link(nc.vector.tensor_tensor(tc_f[:], te_f[:], tc_f[:], ALU.subtract))
                    link(nc.vector.scalar_tensor_tensor(offs[:], tc_f[0:EP], float(SLOTS), ps_before[0:EP, :],
                                                        ALU.mult, ALU.add))
                    link(nc.vector.tensor_tensor(offs[:], offs[:], last[:, 0:NTL], ALU.subtract))
                    link(nc.vector.tensor_scalar(offs[:], offs[:], -1.0, None, ALU.add))
                    link(nc.vector.tensor_tensor(cum[:], cum[:], offs[:].unsqueeze(2).broadcast_to([EP, NTL, EC]),
                                                 ALU.add))
                    link(nc.vector.tensor_tensor(cum[:], cum[:], hot[:], ALU.mult))
                    link(nc.vector.tensor_reduce(pos_f[:], cum[:].rearrange("p b c -> p c b"), X, ALU.add))
                    link(nc.vector.tensor_copy(pos_i[:], pos_f[:]))
                    link(nc.vector.tensor_scalar(lo_i[:], pos_i[:], P - 1, None, ALU.bitwise_and))
                    link(nc.vector.tensor_scalar(hi_i[:], pos_i[:], 7, None, ALU.logical_shift_right))
                    nc.vector.scalar_tensor_tensor(addr[k][:], lo_i[:], float(TILES), hi_i[:],
                                                   ALU.mult, ALU.add).then_inc(s_pos, 1)
                    link(nc.vector.tensor_tensor(
                        cmp[:], iota_batch[:].unsqueeze(2).broadcast_to([P, NB, NTL]),
                        te_f[:].unsqueeze(1).broadcast_to([P, NB, NTL]), ALU.is_ge))
                    link(nc.vector.tensor_reduce(gid_f[:], cmp[:], X, ALU.add))
                    link(nc.vector.tensor_scalar(gid_f[:], gid_f[:], float(NTL - 1), None, ALU.min))
                    link(nc.vector.tensor_copy(gid[k][:], gid_f[:]))
                dve.wait_ge(s_rec, 16)
                link(nc.vector.tensor_copy(other_end["dst"][:], rec[:, :, 0]))
                link(nc.vector.tensor_copy(relation[:], rec[:, :, 2]))
                link(nc.vector.tensor_scalar(neg_local["dst"][:], rec[:, :, 1], -1.0, None, ALU.mult))

        HEAD = {n: l[1] for n, l in enumerate(LAYERS)}
        WMAX = 3 * (P + 1)
        XN = sb("XN", [P, NTL, D])
        HN = sb("HN", [P, NTL, D])
        QN = sb("QN", [P, NTL, D])
        SK = sb("SK", [P, NTL, D + 4])
        ARENA = sb("ARENA", [P, NTL * 136 + NTL * 256])
        MX = sb("MX", [P, NTL, 8])
        AD = sb("AD", [P, NTL, 1])
        NV = sb("NV", [P, NTL, 8])
        NW = sb("NW", [P, NTL, 8])
        W4 = [sb(f"W4_{n}", [D, 4 * D]) for n in range(2)]
        B4 = [sb(f"B4_{n}", [P, 4 * D]) for n in range(2)]
        WG = [sb(f"WG_{n}", [D, D]) for n in range(2)]
        VG = [sb(f"VG_{n}", [P, 3, D]) for n in range(2)]
        WQKV = sb("WQKV", [D, 3 * D])
        WOUT = sb("WOUT", [D, D])
        WKG = sb("WKG", [D, 3, D])
        HS = sb("HS", [P, 2, 3, P])
        HT = sb("HT", [P, 2, 3, P])
        idx = sb("idx", [P, UN, BT], i32)
        idx_rel = sb("idx_rel", [P, UN, BT], i32)
        gat_buf = sb("gat_buf", [P, UN, BT, 256])
        OH = sb("OH", [P, UN, BT, P])
        OD = sb("OD", [P, 2, BT, P])
        OHT = sb("OHT", [P, UN, BT, P])
        NM = sb("NM", [P, UN, BT, P], bf16)
        PR = sb("PR", [P, 2, BT, D])
        UR = sb("UR", [P, BT, D])
        SC = sb("SC", [P, 2, BT, 8])
        SR = sb("SR", [P, 2, BT * 8])
        S3 = sb("S3", [P, 2, BT * 24], bf16)
        ST = sb("ST", [96, 2, P], bf16)
        SEL = {h: sb(f"SEL{h}", [BT * 3 * h, BT, h, P], bf16) for h in (8, 3, 1)}
        RT = {h: sb(f"RT{h}", [BT * 3 * h, BT, h]) for h in (8, 3, 1)}
        RE = {h: sb(f"RE{h}", [BT * 3 * h, 3, BT, h]) for h in (8, 3, 1)}
        MS = sb("MS", [P, 2, 8])
        MT = sb("MT", [P, 2, 8])
        CA = sb("CA", [P, 2, 8])
        CO = sb("CO", [P, 2, 8])
        SU = sb("SU", [P, 2, BT, 8])
        WV = sb("WV", [P, 2, BT * WMAX])

        psum = [ctx.enter_context(nc.psum_tensor(f"bank{n}", [P, 512], f32)) for n in range(8)]
        ps_qe = psum[0:2]
        ps_oht = psum[2]
        ps_me = psum[3]
        ps_sb = psum[4:6]
        ps_ct = psum[6:8]
        ps_ht = psum[0:2]
        ps_pj = psum[4:6]

        names = ("idx_ready rel_ready od_ready edge_ready gather_issued oh_ready ohtps_ready oht_ready nm_ready qe_ready prod_ready pair_ready "
                 "s_ready hi_ready rem_ready s3_ready stps_ready st_ready sb_ready sb_read mt_ready ca_ready "
                 "m_ready me_ready dif_ready sub_ready a_ready co_ready wv_ready ct_ready scaled acc_ready ur_ready").split()
        S = {n: sem(n) for n in names}
        s_stage2 = sem("s_stage2")
        s_scat2 = [sem(f"s_scat2{k}") for k in range(UN)]
        s_rec2 = sem("s_rec2")
        st2_idx = sb("st2_idx", [EP, UN, 2], i32)
        st2_rec = sb("st2_rec", [EP, UN, 2, 4], i32)
        gathered = [sem(f"gathered{k}") for k in range(UN)]
        s_w = sem("s_w")
        s_cst = sem("s_cst")
        s_node = sem("s_node")
        s_hn = sem("s_hn")
        s_var = sem("s_var")
        s_rt = sem("s_rt")
        s_hs = sem("s_hs")
        s_htps = sem("s_htps")
        s_ht = sem("s_ht")
        s_pj = sem("s_pj")
        s_pjr = sem("s_pjr")
        s_tw = sem("s_tw")
        s_td = sem("s_td")
        s_start = sem("s_start")
        s_end = sem("s_end")
        s_th = sem("s_th")
        s_out = sem("s_out")
        block = ctx.enter_context(nc.Block())

        def weights_of(l, par):
            h, c = LAYERS[l][1], LAYERS[l][2]
            return WV[:, par, 0:BT * h * (c + 1)].rearrange("p (t h c) -> p t h c", t=BT, h=h)

        def acc(l):
            h, c = LAYERS[l][1], LAYERS[l][2]
            return ARENA[:, 0:NTL * h * (c + 1)].rearrange("p (t h c) -> p t h c", t=NTL, h=h)

        KV = ARENA[:, NTL * 136:NTL * 136 + NTL * 256].rearrange("p (t c) -> p t c", t=NTL)

        REC2 = ARENA[:, NTL * 136:NTL * 136 + 4 * TILES].bitcast(i32)

        def ps_st(k):
            return ps_ct[(k + 1) % 2][:, 448:512].bitcast(bf16)

        def gb(l):
            return l * NB

        def mb(l):
            return sum(NB for x in LAYERS[:l] if x[4])

        def sbb(l):
            return sum(NB * x[1] for x in LAYERS[:l] if x[4])

        def gathers(l):
            return 2 if LAYERS[l][0] == "kg" else 1

        def arrived(l, q, k):
            before = sum(gathers(i) for i in range(l)) * len(range(k, NB, UN)) * BT * 16
            return before + (q + 1) * (gathers(l) * BT * 16)

        def following(n, q, k, by):
            return n + by, (q + (k + by) // UN if q is not None else None), (k + by) % UN

        def steps(eng, body):
            with eng.Fori(0, LOOPS) as m:
                for j in range(UN):
                    body(m * UN + (j + 1), m + (j + 1) // UN, (j + 1) % UN)
            for n in range(LOOPS * UN + 1, NB):
                body(n, n // UN, n % UN)

        def exists(n, by):
            return by <= NB - 1 - LOOPS * UN if not isinstance(n, int) else 0 <= n + by < NB

        def cols(n):
            return bass.ds(n * BT, BT)

        def groups(eng, regs, l, n):
            at_ = bass.ds(n, len(regs))
            eng.load(regs, gid[LAYERS[l][5]][0:1, at_])
            return [eng.snap(r, min_val=0, max_val=NTL - 1) for r in regs]

        @block.sync
        def _(sp):
            n_in = 0
            for l in range(2):
                sp.dma_start(W4[l][:], a[f"W4_{l}"]).then_inc(s_w, 16)
                sp.dma_start(B4[l][:], a[f"B4_{l}"].partition_broadcast(P)).then_inc(s_w, 16)
                sp.dma_start(WG[l][:], a[f"L1_gnn_W{l + 1}"]).then_inc(s_w, 16)
                for i, name in enumerate((f"att_src{l + 1}", f"att_dst{l + 1}", f"b{l + 1}")):
                    sp.dma_start(VG[l][:, i, :], a[f"L1_gnn_{name}"].partition_broadcast(P)).then_inc(s_w, 16)
            sp.dma_start(WQKV[:], a["WQKV"]).then_inc(s_w, 16)
            sp.dma_start(WOUT[:], a["WOUT"]).then_inc(s_w, 16)
            for i, name in enumerate(("w_edge", "w_node", "w_comp")):
                sp.dma_start(WKG[:, i, :], a[f"L3_gnn_{name}"]).then_inc(s_w, 16)
            sp.dma_start(XN[:, 0:NTL - 1, :],
                         a["x"][0:(NTL - 1) * P, :].rearrange("(t p) d -> p t d", p=P)).then_inc(s_w, 16)
            sp.wait_ge(s_cst, 1)
            sp.dma_start(XN[0:TAIL, NTL - 1, :], a["x"][(NTL - 1) * P:N, :]).then_inc(s_w, 16)
            for l, (kind, _, _, width, _, _) in enumerate(LAYERS):
                sp.wait_ge(s_tw, l + 1)
                src = {"conv": KV, "qkv": KV, "gat": SK[:], "kg": HN[:]}[kind]
                sp.dma_start(table[l].rearrange("(t p) c -> p t c", p=P), src).then_inc(s_td, 16)
                if l == 1:
                    sp.wait_ge(s_td, 32)
                    for k in range(UN):
                        sp.wait_ge(s_scat2[k], 2 * (EC // 16) * 32)
                    sp.dma_start(REC2, rec_dram["src"].rearrange("(p t) f -> p (t f)", p=P)).then_inc(s_rec2, 16)
            sp.wait_ge(s_end, len(LAYERS) + 1)
            sp.dma_start(out[0:(NTL - 1) * P, :].rearrange("(t p) d -> p t d", p=P),
                         XN[:, 0:NTL - 1, :]).then_inc(s_out, 16)
            sp.dma_start(out[(NTL - 1) * P:N, :], XN[0:TAIL, NTL - 1, :]).then_inc(s_out, 16)
            sp.wait_ge(s_out, 32)

        N_W = 16 * (2 * 6 + 5 + 2)

        @block.gpsimd
        def _(pool):
            nc.gpsimd.memset(XN[:, NTL - 1, :], 0.0).then_inc(s_cst, 1)
            for h in (8, 3, 1):
                nc.gpsimd.iota(RT[h][:], [[-3 * h, BT], [-1, h]], base=0, channel_multiplier=1,
                               allow_small_or_imprecise_dtypes=True).then_inc(s_cst, 1)
            def stage(j, t, par, src, parts):
                pool.wait_ge(s_htps, j + 1)
                nc.gpsimd.tensor_copy(HS[:, par, 0:parts, :], src(t)).then_inc(s_hs, 1)

            def node_tiles(q, src, parts):
                pool.wait_ge(s_hn, q + 1)
                with pool.Fori(0, NTL // 2) as m:
                    for par in range(2):
                        stage(m * 2 + (q * NTL + par), m * 2 + par, par, src, parts)
                stage(q * NTL + NTL - 1, NTL - 1, 0, src, parts)

            def h_tile(t):
                return HN[:, bass.ds(t, 1), :]

            for l, (kind, _, _, width, _, key) in enumerate(LAYERS):
                node_tiles(l, h_tile, 1)
                pool.wait_ge(s_td, 16 * (l + 1))

                def scatter(n, k):
                    at_ = bass.ds(n * 2 + l * (EC // 2), 2)
                    nc.gpsimd.tensor_copy(st2_idx[:, k, :], addr["src"][:, at_]).then_inc(s_stage2, 1)
                    nc.gpsimd.tensor_copy(st2_rec[:, k, :, :], recs["src"][:, at_, :]).then_inc(s_stage2, 1)
                    pool.wait_ge(s_stage2, (n + l * (EC // 4)) * 2 + 2)
                    pool.sem_inc(S["gather_issued"], 1)
                    for c in range(2):
                        nc.gpsimd.indirect_dma_start(
                            out=rec_dram["src"][:, :],
                            out_offset=bass.IndirectOffsetOnAxis(ap=st2_idx[:, k, c:c + 1], axis=0),
                            in_=st2_rec[:, k, c, :], in_offset=None).then_inc(s_scat2[k], 16)

                def scattered(m, k):
                    pool.wait_ge(s_scat2[k], (m + 1 + l * (EC // 16)) * 32)

                def gather(n, k):
                    pool.wait_ge(S["wv_ready"], done(gb(l) + n - UN))
                    nc.gpsimd.tensor_copy(idx[:, k, :], other_end[key][:, cols(n)]).then_inc(S["idx_ready"], 1)
                    if kind == "kg":
                        nc.gpsimd.tensor_copy(idx_rel[:, k, :], relation[:, cols(n)]).then_inc(S["rel_ready"], 1)
                        pool.wait_ge(S["rel_ready"], done(n))
                        pool.sem_inc(S["gather_issued"], 1)
                    pool.wait_ge(S["idx_ready"], done(gb(l) + n))
                    pool.sem_inc(S["gather_issued"], 1)
                    for t in range(BT):
                        nc.gpsimd.indirect_dma_start(
                            out=gat_buf[:, k, t, 0:width], out_offset=None, in_=table[l][:, :],
                            in_offset=bass.IndirectOffsetOnAxis(ap=idx[:, k, t:t + 1], axis=0),
                        ).then_inc(gathered[k], 16)
                        if kind == "kg":
                            nc.gpsimd.indirect_dma_start(
                                out=gat_buf[:, k, t, D:2 * D], out_offset=None, in_=a["L3_gnn_rel_emb"][:, :],
                                in_offset=bass.IndirectOffsetOnAxis(ap=idx_rel[:, k, t:t + 1], axis=0),
                            ).then_inc(gathered[k], 16)

                both = EC // 16 if l < 2 else 0
                if both:
                    with pool.Fori(0, both) as m:
                        for k in range(UN):
                            scatter(m * UN + k, k)
                            gather(m * UN + k, k)
                            scattered(m, k)
                with pool.Fori(both, NB // UN) as m:
                    for k in range(UN):
                        gather(m * UN + k, k)
                for n in range(NB // UN * UN, NB):
                    gather(n, n % UN)
            a5 = acc(5)
            node_tiles(6, lambda t: a5[:, bass.ds(t, 1), :, 0:D].rearrange("p a h d -> p (a h) d"), 3)

        @block.scalar
        def _(act):
            def node_sqrt(q):
                act.wait_ge(s_var, q + 1)
                nc.scalar.activation(NW[:, :, 0], NV[:, :, 0], ACT.Sqrt).then_inc(s_rt, 1)

            def evacuate_ht(j, par, parts=1):
                act.wait_ge(s_htps, j + 3)
                act.wait_ge(s_pj, j + 1)
                nc.scalar.activation(HT[:, par, 0:parts, :],
                                     ps_ht[par][:, 0:parts * P].rearrange("p (a b) -> p a b", a=parts),
                                     ACT.Copy).then_inc(s_ht, 1)

            def node_tiles(base, parts=1):
                with act.Fori(0, NTL // 2) as m:
                    for par in range(2):
                        evacuate_ht(m * 2 + (base + par), par, parts)
                evacuate_ht(base + NTL - 1, 0, parts)

            def softmax_layer(l):
                kind, h, c, width, has_max, key = LAYERS[l]

                def transposed_onehots(n, q, k):
                    act.wait_ge(S["ohtps_ready"], done(gb(l) + n))
                    if has_max:
                        act.wait_ge(S["me_ready"], done(mb(l) + n - UN))
                    act.wait_ge(S["qe_ready"], done(gb(l) + n - UN))
                    v = ps_oht[:].rearrange("p (t e) -> p t e", t=BT)
                    nc.scalar.activation(OHT[:, k], v, ACT.Copy).then_inc(S["oht_ready"], 1)
                    nc.scalar.activation(NM[:, k], v, ACT.Copy, bias=-1.0).then_inc(S["nm_ready"], 1)

                def distances(n, q, k):
                    act.wait_ge(S["oh_ready"], done(gb(l) + n - 2))
                    for t in range(BT):
                        last = nc.scalar.activation(OD[:, k % 2, t, :], iota_row[:], ACT.Abs,
                                                    bias=neg_local[key][:, bass.ds(n * BT + t, 1)])
                    last.then_inc(S["od_ready"], 1)

                def onehots(n, q, k):
                    act.wait_ge(S["ct_ready"], done(gb(l) + n - UN))
                    act.wait_ge(S["od_ready"], done(gb(l) + n))
                    nc.scalar.activation(OH[:, k], OD[:, k % 2], ACT.Relu, bias=1.0,
                                         scale=-1.0).then_inc(S["oh_ready"], 1)

                def scores_transposed(n, q, k):
                    rows = BT * 3 * h
                    act.wait_ge(S["stps_ready"], done(mb(l) + n))
                    nc.scalar.activation(ST[0:rows, k % 2, :],
                                         ps_st(k)[0:rows, :], ACT.Copy).then_inc(S["st_ready"], 1)

                def exponentials(n, q, k):
                    par = k % 2
                    act.wait_ge(S["ct_ready"], done(gb(l) + n - 2))
                    if has_max:
                        act.wait_ge(S["ca_ready"], done(mb(l) + n))
                        nc.scalar.activation(CO[:, par, 0:h], CA[:, par, 0:h], ACT.Exp).then_inc(S["co_ready"], 1)
                    act.wait_ge(S["sub_ready"], done(gb(l) + n))
                    nc.scalar.activation(weights_of(l, par)[:, :, :, c], SU[:, par, :, 0:h],
                                         ACT.Exp).then_inc(S["a_ready"], 1)

                def rows_weighted(n, k):
                    wv = weights_of(l, k % 2)
                    act.wait_ge(S["a_ready"], done(gb(l) + n))
                    for i, first in ((0, D), (1, 0)):
                        for t in range(BT):
                            last = nc.scalar.activation(wv[:, t, i, 0:c], gat_buf[:, k, t, first:first + D],
                                                        ACT.Copy, scale=wv[:, t, i, c:c + 1])
                    last.then_inc(S["edge_ready"], 1)

                def step(n, q, k):
                    if exists(n, 2):
                        transposed_onehots(*following(n, q, k, 2))
                    if has_max and exists(n, 1):
                        scores_transposed(*following(n, q, k, 1))
                    exponentials(n, q, k)
                    if exists(n, 3):
                        onehots(*following(n, q, k, 3))
                    if kind == "kg":
                        rows_weighted(n, k)
                    if exists(n, 4):
                        distances(*following(n, q, k, 4))

                for n in range(3):
                    distances(n, 0, n)
                    onehots(n, 0, n)
                distances(3, 0, 3)
                transposed_onehots(0, 0, 0)
                transposed_onehots(1, 0, 1)
                if has_max:
                    scores_transposed(0, 0, 0)
                step(0, 0, 0)
                steps(act, step)

            node_sqrt(0)
            node_tiles(0)
            softmax_layer(0)
            node_tiles(NTL)
            softmax_layer(1)
            node_sqrt(1)
            node_tiles(2 * NTL)
            softmax_layer(2)
            node_tiles(3 * NTL)
            softmax_layer(3)
            node_sqrt(2)
            node_tiles(4 * NTL)
            softmax_layer(4)
            node_tiles(5 * NTL)
            node_sqrt(3)
            softmax_layer(5)
            TH = HT

            def last_tile(j, m_par):
                evacuate_ht(j, m_par, 3)

            with act.Fori(0, NTL // 2) as m:
                for par in range(2):
                    j = m * 2 + (6 * NTL + par)
                    evacuate_ht(j, par, 3)
                    act.wait_ge(s_pj, j + 3)
                    act.wait_ge(s_pjr, j + 1)
                    nc.scalar.activation(PR[:, par, 0:3, :], ps_pj[par][:, 0:3 * P].rearrange("p (a b) -> p a b", a=3),
                                         ACT.Tanh).then_inc(s_th, 1)
            evacuate_ht(7 * NTL - 1, 0, 3)
            act.wait_ge(s_pj, 7 * NTL - 1 + 3)
            act.wait_ge(s_pjr, 7 * NTL - 1 + 1)
            nc.scalar.activation(PR[:, 0, 0:3, :], ps_pj[0][:, 0:3 * P].rearrange("p (a b) -> p a b", a=3),
                                 ACT.Tanh).then_inc(s_th, 1)

        @block.tensor
        def _(pe):
            regs = [pe.alloc_register("pe_group")]

            def node_tile(j, par, w, parts, width):
                pe.wait_ge(s_hs, j + 1)
                pe.wait_ge(s_ht, j + 1)
                for i in range(parts):
                    last = nc.tensor.transpose(ps_ht[par][:, i * P:(i + 1) * P], HS[:, par, i, :], ident[:])
                last.then_inc(s_htps, 1)
                pe.wait_ge(s_ht, j + 3)
                pe.wait_ge(s_pjr, j + 1)
                for i in range(parts):
                    last = nc.tensor.matmul(ps_pj[par][:, i * P:i * P + width], HT[:, par, i, :], w(i),
                                            start=True, stop=True)
                last.then_inc(s_pj, 1)

            def node_tiles(base, w, parts, width):
                with pe.Fori(0, NTL // 2) as m:
                    for par in range(2):
                        node_tile(m * 2 + (base + par), par, w, parts, width)
                node_tile(base + NTL - 1, 0, w, parts, width)

            def softmax_layer(l):
                kind, h, c, width, has_max, key = LAYERS[l]
                w = h * (c + 1)
                expand = {"conv": QN, "qkv": QN, "gat": AD, "kg": HN}[kind]
                ew = 1 if kind == "gat" else D

                def onehots_transposed(n, q, k):
                    pe.wait_ge(S["oh_ready"], done(gb(l) + n))
                    pe.wait_ge(S["nm_ready"], done(gb(l) + n - 1))
                    for t in range(BT):
                        last = nc.tensor.transpose(ps_oht[:, t * P:(t + 1) * P], OH[:, k, t, :], ident[:])
                    last.then_inc(S["ohtps_ready"], 1)

                def expansion(n, q, k):
                    par = k % 2
                    g, = groups(pe, regs, l, n)
                    pe.wait_ge(S["oht_ready"], done(gb(l) + n))
                    pe.wait_ge(S["prod_ready"], done(gb(l) + n - 2))
                    for t in range(BT):
                        last = nc.tensor.matmul(ps_qe[par][:, t * P:t * P + ew], OHT[:, k, t, :],
                                                expand[:, bass.ds(g, 1), :].rearrange("p a d -> p (a d)"),
                                                start=True, stop=True)
                    last.then_inc(S["qe_ready"], 1)

                def parts_transposed(n, q, k):
                    pe.wait_ge(S["s3_ready"], done(mb(l) + n))
                    nc.tensor.transpose(ps_st(k)[0:96, :], S3[:, k % 2, :],
                                        ident_bf[:]).then_inc(S["stps_ready"], 1)

                def masked_scores(n, k, heads):
                    rows = BT * 3 * h
                    if 0 in heads:
                        pe.wait_ge(S["st_ready"], done(mb(l) + n))
                        pe.wait_ge(S["nm_ready"], done(gb(l) + n))
                    for i in heads:
                        pe.wait_ge(S["sb_read"], done(sbb(l) + n * h + i - 2))
                        bank = ps_sb[(n * h + i) % 2 if isinstance(n, int) else (k * h + i) % 2]
                        nc.tensor.matmul(bank[:], big_ident[:], NM[:, k].rearrange("p t e -> p (t e)"),
                                         start=True, stop=False)
                        for t in range(BT):
                            last = nc.tensor.matmul(bank[:, t * P:(t + 1) * P], SEL[h][0:rows, t, i, :],
                                                    ST[0:rows, k % 2, :], start=False, stop=(t == BT - 1))
                        last.then_inc(S["sb_ready"], 1)

                def maxima_expanded(n, q, k):
                    par = k % 2
                    pe.wait_ge(S["mt_ready"], done(mb(l) + n))
                    for t in range(BT):
                        last = nc.tensor.matmul(ps_me[:, t * 8:t * 8 + h], OHT[:, k, t, :], MT[:, par, 0:h],
                                                start=True, stop=True)
                    last.then_inc(S["me_ready"], 1)

                def sums(n, k):
                    par = k % 2
                    pe.wait_ge(S["wv_ready"], done(gb(l) + n))
                    pe.wait_ge(S["acc_ready"], done(gb(l) + n - 2))
                    for t in range(BT):
                        last = nc.tensor.matmul(ps_ct[par][:, 0:w], OH[:, k, t, :], WV[:, par, t * w:(t + 1) * w],
                                                start=(t == 0), stop=(t == BT - 1))
                    last.then_inc(S["ct_ready"], 1)

                def step(n, q, k):
                    if has_max:
                        masked_scores(n, k, range(0, min(h, 2)))
                    if exists(n, 2):
                        onehots_transposed(*following(n, q, k, 2))
                    if has_max and exists(n, 1):
                        parts_transposed(*following(n, q, k, 1))
                    if exists(n, -1):
                        sums(n - 1, (k - 1) % UN)
                    if has_max:
                        masked_scores(n, k, range(2, h))
                    if has_max and h < 8:
                        maxima_expanded(n, q, k)
                    if exists(n, 2):
                        expansion(*following(n, q, k, 2))
                    if has_max and h == 8:
                        maxima_expanded(n, q, k)

                onehots_transposed(0, 0, 0)
                onehots_transposed(1, 0, 1)
                pe.wait_ge(s_start, l + 1)
                expansion(0, 0, 0)
                expansion(1, 0, 1)
                if has_max:
                    parts_transposed(0, 0, 0)
                step(0, 0, 0)
                steps(pe, step)
                sums(NB - 1, (NB - 1) % UN)

            pe.wait_ge(s_w, N_W)
            for q, (w, width) in enumerate(((W4[0], 512), (W4[1], 512), (WG[0], 128), (WG[1], 128), (WQKV, 384))):
                node_tiles(q * NTL, lambda i, w=w, width=width: w[:, 0:width], 1, width)
                softmax_layer(q)
            node_tiles(5 * NTL, lambda i: WOUT[:], 1, D)
            softmax_layer(5)
            node_tiles(6 * NTL, lambda i: WKG[:, i, :], 3, P)

        @block.vector
        def _(dve):
            regs = [dve.alloc_register(f"dve_group{t}") for t in range(2)]
            count = [0]

            def link(ins):
                count[0] += 1
                ins.then_inc(s_node, 1)
                dve.wait_ge(s_node, count[0])

            def over(v, n=D):
                return v.unsqueeze(2).broadcast_to([P, NTL, n])

            def along(v):
                return v.unsqueeze(1).broadcast_to([P, NTL, D])

            def layer_norm_relu(q):
                link(nc.vector.tensor_reduce(NV[:, :, 1], XN[:], X, ALU.add))
                link(nc.vector.tensor_scalar(NV[:, :, 1], NV[:, :, 1], 1.0 / D, None, ALU.mult))
                link(nc.vector.tensor_tensor(HN[:], XN[:], over(NV[:, :, 1]), ALU.subtract))
                link(nc.vector.tensor_tensor(QN[:], HN[:], HN[:], ALU.mult))
                link(nc.vector.tensor_reduce(NV[:, :, 2], QN[:], X, ALU.add))
                nc.vector.tensor_scalar(NV[:, :, 0], NV[:, :, 2], 1.0 / D, 1e-5, ALU.mult, ALU.add).then_inc(s_var, 1)
                dve.wait_ge(s_rt, q + 1)
                link(nc.vector.reciprocal(NW[:, :, 1], NW[:, :, 0]))
                link(nc.vector.tensor_tensor(HN[:], HN[:], over(NW[:, :, 1]), ALU.mult))
                link(nc.vector.tensor_scalar(HN[:], HN[:], 0.0, None, ALU.max))

            def products(base, body):
                with dve.Fori(0, NTL // 2) as m:
                    for par in range(2):
                        dve.wait_ge(s_pj, m * 2 + (base + par + 3))
                        body(m * 2 + par, par).then_inc(s_pjr, 1)
                dve.wait_ge(s_pj, base + NTL - 1 + 3)
                body(NTL - 1, 0).then_inc(s_pjr, 1)

            def at(v, t):
                return v[:, bass.ds(t, 1), :].rearrange("p a d -> p (a d)")

            def settle(base):
                dve.wait_ge(s_pjr, base + NTL + 2)

            def normalised_heads(l, guard_add):
                h, c = LAYERS[l][1], LAYERS[l][2]
                s = acc(l)
                w = NV[:, :, 0:h]
                if guard_add:
                    link(nc.vector.tensor_scalar(w, s[:, :, :, c], guard_add, None, ALU.add))
                else:
                    link(nc.vector.tensor_scalar(w, s[:, :, :, c], TINY, None, ALU.max))
                link(nc.vector.reciprocal(NW[:, :, 0:h], w))
                for i in range(0, h, 1 if h == 3 else h):
                    pass
                if h == 8:
                    hn = HN[:].rearrange("p t (h c) -> p (t h) c", h=h)
                    link(nc.vector.tensor_tensor(
                        hn, s.rearrange("p t h c -> p (t h) c")[:, :, 0:c],
                        NW[:].rearrange("p t h -> p (t h)").unsqueeze(2).broadcast_to([P, NTL * h, c]), ALU.mult))
                elif h == 1:
                    link(nc.vector.tensor_tensor(HN[:], s[:, :, 0, 0:c], over(NW[:, :, 0]), ALU.mult))
                else:
                    for i in range(h):
                        link(nc.vector.tensor_tensor(s[:, :, i, 0:c], s[:, :, i, 0:c], over(NW[:, :, i]), ALU.mult))

            def softmax_layer(l):
                kind, h, c, width, has_max, key = LAYERS[l]
                w = h * (c + 1)
                sums = acc(l)

                def scores(n, q, k, meanwhile):
                    par = k % 2
                    s = SC[:, par, :, 0:h]
                    todo = list(meanwhile)

                    def other():
                        if todo:
                            todo.pop(0)()

                    dve.wait_ge(S["qe_ready"], done(gb(l) + n))
                    dve.wait_ge(gathered[k], arrived(l, q, k))
                    qe = ps_qe[par][:].rearrange("p (t d) -> p t d", t=BT)
                    g = gat_buf[:, k]
                    if kind in ("conv", "qkv"):
                        nc.vector.tensor_tensor(PR[:, 0], qe, g[:, :, 0:D], ALU.mult).then_inc(S["prod_ready"], 1)
                        dve.wait_ge(S["prod_ready"], done(gb(l) + n))
                        nc.vector.tensor_reduce(SC[:, par, :, :].rearrange("p t h -> p (t h)"),
                                                PR[:, 0].rearrange("p t (h c) -> p (t h) c", h=h),
                                                X, ALU.add).then_inc(S["s_ready"], 1)
                    elif kind == "gat":
                        nc.vector.tensor_tensor(PR[:, 0, :, 0:1], qe[:, :, 0:1], g[:, :, D:D + 1],
                                                ALU.add).then_inc(S["prod_ready"], 1)
                        dve.wait_ge(S["prod_ready"], done(gb(l) + n))
                        nc.vector.scalar_tensor_tensor(s, PR[:, 0, :, 0:1], 0.2, PR[:, 0, :, 0:1],
                                                       ALU.mult, ALU.max).then_inc(S["s_ready"], 1)
                    else:
                        nc.vector.tensor_tensor(PR[:, 0], qe, g[:, :, D:2 * D], ALU.mult)
                        nc.vector.tensor_tensor(PR[:, 1], qe, g[:, :, 0:D], ALU.mult).then_inc(S["prod_ready"], 1)
                        dve.wait_ge(S["prod_ready"], done(gb(l) + n))
                        nc.vector.tensor_reduce(SC[:, par, :, 0], PR[:, 0], X, ALU.add)
                        nc.vector.tensor_reduce(SC[:, par, :, 1], PR[:, 1], X, ALU.add).then_inc(S["pair_ready"], 1)
                        dve.wait_ge(S["pair_ready"], done(n))
                        nc.vector.tensor_tensor(SC[:, par, :, 2], SC[:, par, :, 0], SC[:, par, :, 1],
                                                ALU.add).then_inc(S["s_ready"], 1)
                    other()
                    dve.wait_ge(S["s_ready"], done(gb(l) + n))
                    if has_max:
                        s3 = S3[:, par, 0:BT * 3 * h].rearrange("p (t r) -> p t r", t=BT)
                        r = SR[:, par, 0:BT * h].rearrange("p (t h) -> p t h", h=h)
                        nc.vector.tensor_copy(s3[:, :, 0:h], s).then_inc(S["hi_ready"], 1)
                        dve.wait_ge(S["hi_ready"], done(mb(l) + n))
                        nc.vector.tensor_tensor(r, s, s3[:, :, 0:h], ALU.subtract).then_inc(S["rem_ready"], 1)
                        dve.wait_ge(S["rem_ready"], done(2 * (mb(l) + n)))
                        nc.vector.tensor_copy(s3[:, :, h:2 * h], r).then_inc(S["rem_ready"], 1)
                        dve.wait_ge(S["rem_ready"], done(2 * (mb(l) + n) + 1))
                        nc.vector.tensor_tensor(s3[:, :, 2 * h:3 * h], r, s3[:, :, h:2 * h],
                                                ALU.subtract).then_inc(S["s3_ready"], 1)
                    else:
                        nc.vector.tensor_scalar(SU[:, par, :, 0:h], s, -10.0, 10.0, ALU.max,
                                                ALU.min).then_inc(S["sub_ready"], 1)
                    while todo:
                        other()

                def maxima(n, k, group):
                    par = k % 2
                    for i in range(h):
                        dve.wait_ge(S["sb_ready"], done(sbb(l) + n * h + i))
                        bank = ps_sb[(n * h + i) % 2 if isinstance(n, int) else (k * h + i) % 2]
                        nc.vector.tensor_reduce(MS[:, par, i:i + 1], bank[:], X, ALU.max).then_inc(S["sb_read"], 1)
                    m_old = MX[:, bass.ds(group, 1), 0:h].rearrange("p a h -> p (a h)")
                    dve.wait_ge(S["sb_read"], done(sbb(l) + (n + 1) * h - 1))
                    dve.wait_ge(S["m_ready"], done(mb(l) + n - 1))
                    nc.vector.tensor_tensor(MT[:, par, 0:h], m_old, MS[:, par, 0:h], ALU.max).then_inc(S["mt_ready"], 1)
                    dve.wait_ge(S["mt_ready"], done(mb(l) + n))
                    nc.vector.tensor_tensor(CA[:, par, 0:h], m_old, MT[:, par, 0:h],
                                            ALU.subtract).then_inc(S["ca_ready"], 1)

                def keep_maxima(n, k, group):
                    par = k % 2
                    m_old = MX[:, bass.ds(group, 1), 0:h].rearrange("p a h -> p (a h)")
                    dve.wait_ge(S["ca_ready"], done(mb(l) + n))
                    nc.vector.tensor_tensor(m_old, MT[:, par, 0:h], MS[:, par, 0:h], ALU.max).then_inc(S["m_ready"], 1)

                def below_maximum(n, k, meanwhile):
                    par = k % 2
                    su = SU[:, par, :, 0:h]
                    me = ps_me[:, 0:32].rearrange("p (t h) -> p t h", t=BT)[:, :, 0:h]
                    dve.wait_ge(S["me_ready"], done(mb(l) + n))
                    nc.vector.tensor_tensor(su, SC[:, par, :, 0:h], me, ALU.subtract).then_inc(S["dif_ready"], 1)
                    meanwhile()
                    dve.wait_ge(S["dif_ready"], done(mb(l) + n))
                    nc.vector.tensor_scalar(su, su, 0.0, None, ALU.min).then_inc(S["sub_ready"], 1)

                def weighted(n, k):
                    par = k % 2
                    dve.wait_ge(S["a_ready"], done(gb(l) + n))
                    g = gat_buf[:, k]
                    wv = weights_of(l, par)
                    if h == 8:
                        last = nc.vector.tensor_tensor(
                            wv[:, :, :, 0:c], g[:, :, D:2 * D].rearrange("p t (h c) -> p t h c", h=h),
                            wv[:, :, :, c:c + 1].broadcast_to([P, BT, h, c]), ALU.mult)
                    elif h == 1:
                        last = nc.vector.tensor_tensor(wv[:, :, 0, 0:c], g[:, :, 0:D],
                                                       wv[:, :, 0, c:c + 1].broadcast_to([P, BT, c]), ALU.mult)
                    else:
                        nc.vector.tensor_tensor(UR[:], g[:, :, 0:D], g[:, :, D:2 * D],
                                                ALU.add).then_inc(S["ur_ready"], 1)
                        dve.wait_ge(S["ur_ready"], done(n))
                        dve.wait_ge(S["edge_ready"], done(n))
                        last = nc.vector.tensor_tensor(wv[:, :, 2, 0:c], UR[:],
                                                       wv[:, :, 2, c:c + 1].broadcast_to([P, BT, c]), ALU.mult)
                    last.then_inc(S["wv_ready"], 1)

                def rescale(n, k, group):
                    if has_max and h == 8:
                        total = sums[:, bass.ds(group, 1)].rearrange("p a h c -> p (a h) c")
                        dve.wait_ge(S["acc_ready"], done(gb(l) + n - 1))
                        dve.wait_ge(S["co_ready"], done(mb(l) + n))
                        nc.vector.tensor_tensor(total, total,
                                                CO[:, k % 2, :].unsqueeze(2).broadcast_to([P, h, c + 1]),
                                                ALU.mult).then_inc(S["scaled"], 1)

                def add_up(n, k, group):
                    par = k % 2
                    total = sums[:, bass.ds(group, 1)].rearrange("p a h c -> p (a h) c")
                    ct = ps_ct[par][:, 0:w].rearrange("p (h c) -> p h c", h=h)
                    dve.wait_ge(S["acc_ready"], done(gb(l) + n - 1))
                    dve.wait_ge(S["ct_ready"], done(gb(l) + n))
                    if h == 8:
                        if has_max:
                            dve.wait_ge(S["scaled"], done(gb(l) + n))
                        last = nc.vector.tensor_tensor(total, total, ct, ALU.add)
                    else:
                        dve.wait_ge(S["co_ready"], done(mb(l) + n))
                        for i in range(h):
                            last = nc.vector.scalar_tensor_tensor(total[:, i, :], total[:, i, :],
                                                                  CO[:, par, i:i + 1], ct[:, i, :],
                                                                  ALU.mult, ALU.add)
                    last.then_inc(S["acc_ready"], 1)

                def step(n, q, k):
                    now = before = None
                    if exists(n, -1):
                        before, now = groups(dve, regs, l, n - 1)
                    else:
                        now, _ = groups(dve, regs, l, n)
                    others = []
                    if exists(n, -1):
                        others.append(lambda: weighted(n - 1, (k - 1) % UN))
                    if exists(n, 1):
                        scores(*following(n, q, k, 1), others)
                    else:
                        for other in others:
                            other()
                    if has_max:
                        maxima(n, k, now)
                    if exists(n, -1):
                        rescale(n - 1, (k - 1) % UN, before)
                    if has_max:
                        keep_maxima(n, k, now)
                        below_maximum(n, k, lambda: add_up(n - 1, (k - 1) % UN, before) if exists(n, -1) else None)
                    elif exists(n, -1):
                        add_up(n - 1, (k - 1) % UN, before)

                scores(0, 0, 0, [])
                step(0, 0, 0)
                steps(dve, step)
                k = (NB - 1) % UN
                weighted(NB - 1, k)
                _, g = groups(dve, regs, l, NB - 2)
                rescale(NB - 1, k, g)
                add_up(NB - 1, k, g)
                dve.wait_ge(S["acc_ready"], done(gb(l + 1) - 1))
                dve.sem_inc(s_end, 1)

            def clear(l):
                link(nc.vector.memset(acc(l), 0.0))
                link(nc.vector.memset(MX[:], -BIG))

            for s in S.values():
                dve.sem_inc(s, CR)
            dve.sem_inc(s_ht, 2)
            dve.sem_inc(s_htps, 2)
            dve.sem_inc(s_pj, 2)
            dve.sem_inc(s_pjr, 2)
            dve.wait_ge(s_cst, 4)
            link(nc.vector.memset(S3[:], 0.0))
            for h in (8, 3, 1):
                for part in range(3):
                    link(nc.vector.tensor_scalar(RE[h][:, part], RT[h][:], float(part * h), None, ALU.is_equal))
                link(nc.vector.tensor_tensor(RE[h][:, 0], RE[h][:, 0], RE[h][:, 1], ALU.add))
                link(nc.vector.tensor_tensor(RE[h][:, 0], RE[h][:, 0], RE[h][:, 2], ALU.add))
                link(nc.vector.tensor_copy(SEL[h][:], RE[h][:, 0].unsqueeze(3).broadcast_to([BT * 3 * h, BT, h, P])))
            dve.wait_ge(s_w, N_W)
            for l in range(2):
                link(nc.vector.tensor_scalar(B4[l][:, 0:D], B4[l][:, 0:D], 0.25, None, ALU.mult))

            layer_norm_relu(0)
            for l in range(2):
                dve.sem_inc(s_hn, 1)

                def conv_products(t, par, l=l):
                    ps = ps_pj[par]
                    nc.vector.scalar_tensor_tensor(at(QN, t), ps[:, 0:D], 0.25, B4[l][:, 0:D], ALU.mult, ALU.add)
                    nc.vector.tensor_tensor(at(KV, t), ps[:, D:3 * D], B4[l][:, D:3 * D], ALU.add)
                    return nc.vector.tensor_tensor(at(SK[:, :, 0:D], t), ps[:, 3 * D:4 * D], B4[l][:, 3 * D:4 * D],
                                                   ALU.add)

                products(l * NTL, conv_products)
                settle(l * NTL)
                dve.sem_inc(s_tw, 1)
                clear(l)
                dve.sem_inc(s_start, 1)
                softmax_layer(l)
                normalised_heads(l, None)
                link(nc.vector.tensor_tensor(HN[:], HN[:], SK[:, :, 0:D], ALU.add))
                if l == 0:
                    link(nc.vector.tensor_scalar(HN[:], HN[:], 0.0, None, ALU.max))
            link(nc.vector.tensor_tensor(XN[:], XN[:], HN[:], ALU.add))

            layer_norm_relu(1)
            for g in range(2):
                l = 2 + g
                dve.sem_inc(s_hn, 1)
                products(l * NTL, lambda t, par: nc.vector.tensor_copy(at(SK[:, :, 0:D], t), ps_pj[par][:, 0:D]))
                settle(l * NTL)
                link(nc.vector.tensor_tensor(QN[:], SK[:, :, 0:D], along(VG[g][:, 0, :]), ALU.mult))
                link(nc.vector.tensor_reduce(SK[:, :, D], QN[:], X, ALU.add))
                link(nc.vector.memset(SK[:, :, D + 1:D + 4], 0.0))
                dve.sem_inc(s_tw, 1)
                link(nc.vector.tensor_tensor(QN[:], SK[:, :, 0:D], along(VG[g][:, 1, :]), ALU.mult))
                link(nc.vector.tensor_reduce(AD[:, :, 0], QN[:], X, ALU.add))
                link(nc.vector.tensor_tensor(NV[:, :, 0], SK[:, :, D], AD[:, :, 0], ALU.add))
                link(nc.vector.scalar_tensor_tensor(MX[:, :, 0], NV[:, :, 0], 0.2, NV[:, :, 0], ALU.mult, ALU.max))
                link(nc.vector.tensor_copy(acc(l)[:, :, 0, 0:D], SK[:, :, 0:D]))
                link(nc.vector.memset(acc(l)[:, :, 0, D:D + 1], 1.0))
                dve.sem_inc(s_start, 1)
                softmax_layer(l)
                normalised_heads(l, 1e-16)
                link(nc.vector.tensor_tensor(HN[:], HN[:], along(VG[g][:, 2, :]), ALU.add))
                link(nc.vector.tensor_scalar(HN[:], HN[:], 0.0, None, ALU.max))
            link(nc.vector.tensor_tensor(XN[:], XN[:], HN[:], ALU.add))

            dve.wait_ge(s_rec2, 16)
            rec2 = REC2.rearrange("p (t f) -> p t f", f=4)
            link(nc.vector.tensor_copy(other_end["src"][:], rec2[:, :, 0]))
            link(nc.vector.tensor_scalar(neg_local["src"][:], rec2[:, :, 1], -1.0, None, ALU.mult))
            layer_norm_relu(2)
            dve.sem_inc(s_hn, 1)

            def qkv_products(t, par):
                ps = ps_pj[par]
                nc.vector.tensor_scalar(at(QN, t), ps[:, 0:D], 0.25, None, ALU.mult)
                return nc.vector.tensor_copy(at(KV, t), ps[:, D:3 * D])

            products(4 * NTL, qkv_products)
            settle(4 * NTL)
            dve.sem_inc(s_tw, 1)
            clear(4)
            dve.sem_inc(s_start, 1)
            softmax_layer(4)
            normalised_heads(4, 1e-8)
            dve.sem_inc(s_hn, 1)
            products(5 * NTL, lambda t, par: nc.vector.tensor_tensor(at(XN, t), at(XN, t), ps_pj[par][:, 0:D], ALU.add))
            settle(5 * NTL)

            layer_norm_relu(3)
            dve.sem_inc(s_tw, 1)
            clear(5)
            dve.sem_inc(s_start, 1)
            softmax_layer(5)
            normalised_heads(5, None)
            link(nc.vector.tensor_tensor(XN[:], XN[:], HN[:], ALU.add))
            dve.sem_inc(s_hn, 1)

            def add_tanh(t, par, q):
                dve.wait_ge(s_pjr, q + 6 * NTL + 1)
                dve.wait_ge(s_th, q + 1)
                nc.vector.tensor_reduce(UR[:, par, :], PR[:, par, 0:3, :].rearrange("p a d -> p d a"), X,
                                        ALU.add).then_inc(S["ur_ready"], 1)
                dve.wait_ge(S["ur_ready"], done(NB + q))
                nc.vector.tensor_tensor(at(XN, t), at(XN, t), UR[:, par, :], ALU.add).then_inc(s_pjr, 1)

            with dve.Fori(0, NTL // 2) as m:
                for par in range(2):
                    add_tanh(m * 2 + par, par, m * 2 + par)
            add_tanh(NTL - 1, 0, NTL - 1)
            settle(6 * NTL)
            dve.sem_inc(s_end, 1)


def kernel(**inputs):
    import numpy as np
    import concourse.bacc as bacc
    from concourse.bass_utils import run_bass_kernel_spmd

    x = {k: np.asarray(v) for k, v in inputs.items()}
    arrays = {k: x[k] for k in ("x", "src", "dst", "edge_type_474", "L1_gnn_W1", "L1_gnn_W2", "L3_gnn_rel_emb",
                                "L3_gnn_w_edge", "L3_gnn_w_node", "L3_gnn_w_comp")}
    for l in range(2):
        for kind in ("W4", "B4"):
            part = "w" if kind == "W4" else "b"
            arrays[f"{kind}_{l}"] = np.concatenate([x[f"L0_gnn_{n}_{part}{l}"] for n in "qkvs"], axis=-1)
        for n in (f"att_src{l + 1}", f"att_dst{l + 1}", f"b{l + 1}"):
            arrays[f"L1_gnn_{n}"] = x[f"L1_gnn_{n}"].reshape(D)
    arrays["WQKV"] = np.ascontiguousarray(x["L2_gnn_W_qkv"].T)
    arrays["WOUT"] = np.ascontiguousarray(x["L2_gnn_W_out"].T)

    nc = bacc.Bacc("TRN2", target_bir_lowering=False, num_devices=1)
    feed, aps = {}, {}
    for name, v in arrays.items():
        feed[f"in_{name}"] = np.ascontiguousarray(v)
        aps[name] = nc.dram_tensor(f"in_{name}", v.shape, mybir.dt.from_np(v.dtype), kind="ExternalInput").ap()
    out = nc.dram_tensor("out", (N, D), mybir.dt.float32, kind="ExternalOutput").ap()
    build(nc, aps, out)
    r = run_bass_kernel_spmd(nc, [feed], core_ids=[0])
    return r.results[0]["out"]
```

```python
import concourse.bass as bass
from concourse import mybir
from contextlib import ExitStack

N, D, E = 3125, 128, 50000
P = 128
NTL = -(-N // P)
TAIL = N - (NTL - 1) * P
NPAD = NTL * P
EP, EC = 125, 400
BT = 4
SLOTS = BT * P
NB = (E + NTL * (SLOTS - 1)) // SLOTS
TILES = NB * BT
UN = 4
LOOPS = (NB - 5) // UN
BIG = float(2.0 ** 100)
TINY = 1e-30
CR = 8
NREL = 475
AWAKE = {8: (0, 0, 1, 1, 0), 1: (2, 1, 2, 2, 0), 3: (0, 0, 3, 3, 4)}
SHIFT = SLOTS.bit_length() - 1
assert EP * EC == E and SLOTS == 1 << SHIFT and NB - 1 - LOOPS * UN >= 2

LAYERS = [
    ("conv", 8, 16, 256, True, "dst"),
    ("conv", 8, 16, 256, True, "dst"),
    ("gat", 1, 128, 132, True, "dst"),
    ("gat", 1, 128, 132, True, "dst"),
    ("qkv", 8, 16, 256, False, "src"),
    ("kg", 3, 128, 128, True, "dst"),
]


def done(count):
    return count + 1 + CR


def build(nc, a, out):
    f32, bf16, i32 = mybir.dt.float32, mybir.dt.bfloat16, mybir.dt.int32
    ALU = mybir.AluOpType
    ACT = mybir.ActivationFunctionType
    X = mybir.AxisListType.X

    rec_dram = {k: nc.dram_tensor(f"rec_{k}", (P * TILES, 4), i32).ap() for k in ("dst", "src")}
    table = [nc.dram_tensor(f"table_{n}", (NPAD, l[3]), f32).ap() for n, l in enumerate(LAYERS)]

    with ExitStack() as ctx:
        def sb(name, shape, dt=f32, c=ctx):
            return c.enter_context(nc.sbuf_tensor(name, shape, dt))

        def sem(name):
            return ctx.enter_context(nc.semaphore(name))

        ident = sb("ident", [P, P])
        ident_bf = sb("ident_bf", [P, P], bf16)
        iota_row = sb("iota_row", [P, P])
        ones_row = sb("ones_row", [P, P])
        other_end = {k: sb(f"other_end_{k}", [P, TILES], i32) for k in ("dst", "src")}
        relation = sb("relation", [P, TILES], i32)
        addr = {"src": sb("addr_src", [EP, EC], i32)}
        recs = {"src": sb("recs_src", [EP, EC, 4], i32)}
        neg_local = {k: sb(f"neg_local_{k}", [P, TILES]) for k in ("dst", "src")}
        gid = {k: sb(f"gid_{k}", [P, NB], i32) for k in ("dst", "src")}
        reset = sb("reset", [P, TILES], bf16)
        is_last = sb("is_last", [P, TILES])

        s_const = sem("s_const")
        s_load = sem("s_load")
        s_fill = sem("s_fill")
        s_chain = sem("s_chain")
        s_npb = sem("s_npb")
        s_cnt = sem("s_cnt")
        s_pos = sem("s_pos")
        s_stage = sem("s_stage")
        s_scat = [sem("s_scat0"), sem("s_scat1")]
        s_issue = sem("s_issue")
        s_rec = sem("s_rec")

        with ExitStack() as part:
            def sp_(name, shape, dt=f32):
                return sb(name, shape, dt, part)

            keys = sp_("keys", [EP, 3, EC], i32)
            cum = sp_("cum", [EP, NTL, EC])
            hot = sp_("hot", [EP, NTL, EC])
            cmp = sp_("cmp", [P, NB, NTL])
            bin_i = sp_("bin_i", [EP, EC], i32)
            bin_f = sp_("bin_f", [EP, EC])
            iota_bin = sp_("iota_bin", [P, NTL])
            iota_batch = sp_("iota_batch", [P, NB])
            before = sp_("before", [P, P])
            shift = {d: sp_(f"shift{d}", [P, P]) for d in (0, 1)}
            node1 = sp_("node1", [P, TILES])
            row = sp_("row", [P, 1])
            node128 = sp_("node128", [P, TILES])
            slot_key = sp_("slot_key", [P, TILES])
            rec_f = sp_("rec_f", [P, TILES, 4])
            ones_bf = sp_("ones_bf", [P, P], bf16)
            row_diag = sp_("row_diag", [P, BT, P], bf16)
            node_diag = sp_("node_diag", [P, 2, BT, P], bf16)
            below = sp_("below", [P, 2, BT, P])
            rank = sp_("rank", [P, 2, BT])
            falls = sp_("falls", [P, TILES])
            any_falls = sp_("any_falls", [P, 1])
            unordered = sp_("unordered", [P, 1], i32)
            apart = sp_("apart", [P, BT, P])
            order = sp_("order", [P, 2, BT, P])
            last = sp_("last", [EP, NTL + 1])
            n_bin = sp_("n_bin", [EP, NTL])
            offs = sp_("offs", [EP, NTL])
            tc_i = sp_("tc_i", [P, NTL], i32)
            tc_f = sp_("tc_f", [P, NTL])
            te_f = sp_("te_f", [P, NTL])
            pos_f = sp_("pos_f", [EP, EC])
            pos_i = sp_("pos_i", [EP, EC], i32)
            lo_i = sp_("lo_i", [EP, EC], i32)
            hi_i = sp_("hi_i", [EP, EC], i32)
            addr["dst"] = sp_("addr_dst", [EP, EC], i32)
            recs["dst"] = sp_("recs_dst", [EP, EC, 4], i32)
            rec = sp_("rec", [P, TILES, 4], i32)
            gid_f = sp_("gid_f", [P, NB])
            fill = sp_("fill", [P, TILES, 4], i32)
            SB = 8
            st_idx = sp_("st_idx", [EP, 2, SB], i32)
            st_rec = sp_("st_rec", [EP, 2, SB, 4], i32)
            ps_before = part.enter_context(nc.psum_tensor("ps_before", [P, NTL], f32))
            ps_total = part.enter_context(nc.psum_tensor("ps_total", [P, NTL], f32))
            ps_key = [part.enter_context(nc.psum_tensor(f"ps_key{d}", [P, 512], f32)) for d in (0, 1)]
            ps_rec = [part.enter_context(nc.psum_tensor(f"ps_rec{d}", [P, 512], f32)) for d in (0, 1)]
            ps_next = ps_key
            T = {n: part.enter_context(nc.semaphore(f"t_{n}")) for n in
                 ("diag", "keys", "below", "rank", "apart", "order", "permuted", "sorted")}
            s_sort = part.enter_context(nc.semaphore("s_sort"))
            block = part.enter_context(nc.Block())

            def sorted_(n):
                return n + 5

            def batches(eng, body):
                with eng.Fori(0, NB // 2 - 1) as m:
                    for par in range(2):
                        body(m * 2 + (par + 2), par)

            def where_unordered(eng, body):
                eng.wait_ge(s_sort, 1)
                reg = eng.alloc_register("unordered")
                eng.load([reg], unordered[0:1, 0:1])
                with eng.If_ne(reg, 0):
                    body()
                eng.end_ifs()

            def slots(n):
                return bass.ds(n * BT, BT)

            col = {"dst": 0, "src": 1}

            @block.sync
            def _(sp):
                for n, name in enumerate(("dst", "src", "edge_type_474")):
                    sp.dma_start(keys[:, n, :], a[name].rearrange("(p c) -> p c", p=EP)).then_inc(s_load, 16)
                sp.wait_ge(s_const, 9)
                for k in ("dst", "src"):
                    sp.dma_start(rec_dram[k].rearrange("(p t) f -> p (t f)", p=P),
                                 fill[:].rearrange("p t f -> p (t f)")).then_inc(s_fill, 16)
                for h in range(2):
                    sp.wait_ge(s_scat[h], EC // 2 * 16)
                sp.dma_start(rec[:].rearrange("p t f -> p (t f)"),
                             rec_dram["dst"].rearrange("(p t) f -> p (t f)", p=P)).then_inc(s_rec, 16)

            @block.gpsimd
            def _(pool):
                nc.gpsimd.iota(iota_row[:], [[1, P]], base=0, channel_multiplier=0,
                               allow_small_or_imprecise_dtypes=True).then_inc(s_const, 1)
                nc.gpsimd.iota(iota_bin[:], [[1, NTL]], base=0, channel_multiplier=0,
                               allow_small_or_imprecise_dtypes=True).then_inc(s_const, 1)
                nc.gpsimd.iota(iota_batch[:], [[1, NB]], base=0, channel_multiplier=0,
                               allow_small_or_imprecise_dtypes=True).then_inc(s_const, 1)
                nc.gpsimd.memset(ones_row[:], 1.0).then_inc(s_const, 1)
                nc.gpsimd.memset(fill[:], 0).then_inc(s_const, 1)
                pool.wait_ge(s_const, 5)
                nc.gpsimd.iota(row[:], [[0, 1]], base=0, channel_multiplier=1,
                               allow_small_or_imprecise_dtypes=True).then_inc(s_const, 1)
                nc.gpsimd.memset(fill[:, :, 1:2], 2 * P).then_inc(s_const, 1)
                nc.gpsimd.affine_select(out=ident[:], in_=ones_row[:], compare_op=ALU.is_equal, fill=0.0, base=0,
                                        pattern=[[-1, P]], channel_multiplier=1).then_inc(s_const, 1)
                nc.gpsimd.affine_select(out=before[:], in_=ones_row[:], compare_op=ALU.is_gt, fill=0.0, base=0,
                                        pattern=[[1, P]], channel_multiplier=-1).then_inc(s_const, 1)
                nc.gpsimd.affine_select(out=shift[0][:], in_=ones_row[:], compare_op=ALU.is_equal, fill=0.0, base=-1,
                                        pattern=[[1, P]], channel_multiplier=-1).then_inc(s_const, 1)
                nc.gpsimd.affine_select(out=shift[1][:], in_=ones_row[:], compare_op=ALU.is_equal, fill=0.0, base=1,
                                        pattern=[[1, P]], channel_multiplier=-1).then_inc(s_const, 1)
                pool.wait_ge(s_fill, 32)
                pool.wait_ge(s_pos, 1)

                def scatter(m, h, reused):
                    if reused:
                        pool.wait_ge(s_scat[h], m * (SB * 16))
                    at_ = bass.ds(m * (2 * SB) + h * SB, SB)
                    nc.gpsimd.tensor_copy(st_idx[:, h, :], addr["dst"][:, at_]).then_inc(s_stage, 1)
                    nc.gpsimd.tensor_copy(st_rec[:, h, :, :], recs["dst"][:, at_, :]).then_inc(s_stage, 1)
                    pool.wait_ge(s_stage, m * 4 + 2 * h + 2)
                    pool.sem_inc(s_issue, 1)
                    for c in range(SB):
                        nc.gpsimd.indirect_dma_start(
                            out=rec_dram["dst"][:, :],
                            out_offset=bass.IndirectOffsetOnAxis(ap=st_idx[:, h, c:c + 1], axis=0),
                            in_=st_rec[:, h, c, :], in_offset=None).then_inc(s_scat[h], 16)

                for h in range(2):
                    scatter(0, h, False)
                with pool.Fori(1, EC // (2 * SB)) as m:
                    for h in range(2):
                        scatter(m, h, True)

                def node_diagonal(n, par):
                    pool.wait_ge(T["keys"], sorted_(n - 2))
                    nc.gpsimd.tensor_tensor(node_diag[:, par], ident[:].unsqueeze(1).broadcast_to([P, BT, P]),
                                            node128[:, slots(n)].unsqueeze(2).broadcast_to([P, BT, P]),
                                            ALU.mult).then_inc(T["diag"], 1)

                def diagonals():
                    node_diagonal(0, 0)
                    node_diagonal(1, 1)
                    batches(pool, node_diagonal)

                where_unordered(pool, diagonals)
                pool.wait_ge(s_sort, 2)

            @block.scalar
            def _(act):
                def distances(n, par):
                    act.wait_ge(T["rank"], sorted_(n))
                    act.wait_ge(T["order"], sorted_(n - 1))
                    for t in range(BT):
                        last = nc.scalar.activation(apart[:, t, :], iota_row[:], ACT.Abs, scale=-1.0,
                                                    bias=rank[:, par, t:t + 1])
                    last.then_inc(T["apart"], 1)

                def ranks_onehot(n, par):
                    act.wait_ge(T["apart"], sorted_(n))
                    act.wait_ge(T["permuted"], sorted_(n - 2))
                    nc.scalar.activation(order[:, par], apart[:], ACT.Relu, bias=1.0,
                                         scale=-1.0).then_inc(T["order"], 1)

                def records_kept(n, par):
                    act.wait_ge(T["permuted"], sorted_(n))
                    nc.scalar.activation(rec_f[:, slots(n), :].rearrange("p t f -> p (t f)"),
                                         ps_rec[par][:, 0:BT * 4], ACT.Copy).then_inc(T["sorted"], 1)

                def body(n, par):
                    distances(n, par)
                    records_kept(n - 2, par)
                    ranks_onehot(n, par)

                def onehots_and_records():
                    distances(0, 0)
                    ranks_onehot(0, 0)
                    distances(1, 1)
                    ranks_onehot(1, 1)
                    batches(act, body)
                    records_kept(NB - 2, 0)
                    records_kept(NB - 1, 1)

                where_unordered(act, onehots_and_records)

            @block.tensor
            def _(pe):
                for q in range(2):
                    pe.wait_ge(s_npb, q + 1)
                    nc.tensor.matmul(ps_before[0:EP, :], before[0:EP, 0:EP], n_bin[:], start=True, stop=True)
                    nc.tensor.matmul(ps_total[:], ones_row[0:EP, :], n_bin[:], start=True, stop=True).then_inc(s_cnt, 1)

                def other_keys(n, par):
                    pe.wait_ge(T["diag"], sorted_(n))
                    pe.wait_ge(T["below"], sorted_(n - 2))
                    nc.tensor.matmul(ps_key[par][:], ones_bf[:], row_diag[:].rearrange("p t e -> p (t e)"),
                                     start=True, stop=False)
                    nc.tensor.matmul(ps_key[par][:], ones_bf[:], node_diag[:, par].rearrange("p t e -> p (t e)"),
                                     start=False, stop=True).then_inc(T["keys"], 1)

                def permuted(n, par):
                    pe.wait_ge(T["order"], sorted_(n))
                    pe.wait_ge(T["sorted"], sorted_(n - 2))
                    for t in range(BT):
                        last = nc.tensor.matmul(ps_rec[par][:, t * 4:(t + 1) * 4], order[:, par, t, :],
                                                rec_f[:, bass.ds(n * BT + t, 1), :].rearrange("p a f -> p (a f)"),
                                                start=True, stop=True)
                    last.then_inc(T["permuted"], 1)

                def body(n, par):
                    other_keys(n, par)
                    permuted(n - 2, par)

                def keys_and_records():
                    other_keys(0, 0)
                    other_keys(1, 1)
                    batches(pe, body)
                    permuted(NB - 2, 0)
                    permuted(NB - 1, 1)

                pe.wait_ge(s_npb, 3)
                nc.tensor.matmul(ps_next[0][:, 0:TILES], shift[0][:], node1[:], start=True,
                                 stop=True).then_inc(s_cnt, 1)
                pe.wait_ge(s_npb, 4)
                nc.tensor.matmul(ps_total[:, 0:1], ones_row[:], any_falls[:], start=True,
                                 stop=True).then_inc(s_cnt, 1)
                where_unordered(pe, keys_and_records)
                pe.wait_ge(s_npb, 5)
                for d in (0, 1):
                    nc.tensor.matmul(ps_next[d][:, 0:TILES], shift[d][:], node1[:], start=True,
                                     stop=True).then_inc(s_cnt, 1)

            @block.vector
            def _(dve):
                count = [0]

                def link(ins):
                    count[0] += 1
                    ins.then_inc(s_chain, 1)
                    dve.wait_ge(s_chain, count[0])

                dve.wait_ge(s_const, 11)
                link(nc.vector.tensor_copy(ident_bf[:], ident[:]))
                link(nc.vector.memset(last[:, 0:1], 0.0))
                dve.wait_ge(s_load, 48)
                for q, k in enumerate(("dst", "src")):
                    key, other = keys[:, col[k], :], keys[:, 1 - col[k], :]
                    link(nc.vector.memset(recs[k][:, :, 3:4], 0))
                    link(nc.vector.tensor_copy(recs[k][:, :, 0], other))
                    link(nc.vector.tensor_scalar(recs[k][:, :, 1], key, P - 1, None, ALU.bitwise_and))
                    link(nc.vector.tensor_copy(recs[k][:, :, 2], keys[:, 2, :]))
                    link(nc.vector.tensor_scalar(bin_i[:], key, 7, None, ALU.logical_shift_right))
                    link(nc.vector.tensor_copy(bin_f[:], bin_i[:]))
                    link(nc.vector.tensor_tensor(
                        hot[:], bin_f[:].unsqueeze(1).broadcast_to([EP, NTL, EC]),
                        iota_bin[0:EP].unsqueeze(2).broadcast_to([EP, NTL, EC]), ALU.is_equal))
                    flat_hot = hot[:].rearrange("p b c -> p (b c)")
                    link(nc.vector.tensor_tensor_scan(cum[:].rearrange("p b c -> p (b c)"), flat_hot, flat_hot,
                                                      0.0, ALU.add, ALU.max))
                    link(nc.vector.tensor_copy(last[:, 1:NTL + 1], cum[:, :, EC - 1]))
                    nc.vector.tensor_tensor(n_bin[:], last[:, 1:NTL + 1], last[:, 0:NTL],
                                            ALU.subtract).then_inc(s_npb, 1)
                    dve.wait_ge(s_cnt, q + 1)
                    link(nc.vector.tensor_scalar(tc_f[:], ps_total[:], float(SLOTS - 1), None, ALU.add))
                    link(nc.vector.tensor_copy(tc_i[:], tc_f[:]))
                    link(nc.vector.tensor_scalar(tc_i[:], tc_i[:], SHIFT, None, ALU.logical_shift_right))
                    link(nc.vector.tensor_copy(tc_f[:], tc_i[:]))
                    link(nc.vector.tensor_tensor_scan(te_f[:], tc_f[:], tc_f[:], 0.0, ALU.add, ALU.max))
                    link(nc.vector.tensor_tensor(tc_f[:], te_f[:], tc_f[:], ALU.subtract))
                    link(nc.vector.scalar_tensor_tensor(offs[:], tc_f[0:EP], float(SLOTS), ps_before[0:EP, :],
                                                        ALU.mult, ALU.add))
                    link(nc.vector.tensor_tensor(offs[:], offs[:], last[:, 0:NTL], ALU.subtract))
                    link(nc.vector.tensor_scalar(offs[:], offs[:], -1.0, None, ALU.add))
                    link(nc.vector.tensor_tensor(cum[:], cum[:], offs[:].unsqueeze(2).broadcast_to([EP, NTL, EC]),
                                                 ALU.add))
                    link(nc.vector.tensor_tensor(cum[:], cum[:], hot[:], ALU.mult))
                    link(nc.vector.tensor_reduce(pos_f[:], cum[:].rearrange("p b c -> p c b"), X, ALU.add))
                    link(nc.vector.tensor_copy(pos_i[:], pos_f[:]))
                    link(nc.vector.tensor_scalar(lo_i[:], pos_i[:], P - 1, None, ALU.bitwise_and))
                    link(nc.vector.tensor_scalar(hi_i[:], pos_i[:], 7, None, ALU.logical_shift_right))
                    nc.vector.scalar_tensor_tensor(addr[k][:], lo_i[:], float(TILES), hi_i[:],
                                                   ALU.mult, ALU.add).then_inc(s_pos, 1)
                    link(nc.vector.tensor_tensor(
                        cmp[:], iota_batch[:].unsqueeze(2).broadcast_to([P, NB, NTL]),
                        te_f[:].unsqueeze(1).broadcast_to([P, NB, NTL]), ALU.is_ge))
                    link(nc.vector.tensor_reduce(gid_f[:], cmp[:], X, ALU.add))
                    link(nc.vector.tensor_scalar(gid_f[:], gid_f[:], float(NTL - 1), None, ALU.min))
                    link(nc.vector.tensor_copy(gid[k][:], gid_f[:]))
                for t in T.values():
                    dve.sem_inc(t, 4)
                link(nc.vector.memset(ones_bf[:], 1.0))
                link(nc.vector.tensor_tensor(row_diag[:], ident[:].unsqueeze(1).broadcast_to([P, BT, P]),
                                             iota_row[:].unsqueeze(1).broadcast_to([P, BT, P]), ALU.mult))
                dve.wait_ge(s_rec, 16)
                link(nc.vector.tensor_scalar(node128[:], rec[:, :, 1], float(P), None, ALU.mult))
                link(nc.vector.tensor_scalar(slot_key[:], node128[:], row[:, 0:1], None, ALU.add))
                link(nc.vector.tensor_copy(rec_f[:], rec[:]))
                nc.vector.tensor_scalar(node1[:], rec[:, :, 1], 1.0, None, ALU.add).then_inc(s_npb, 1)
                dve.wait_ge(s_cnt, 3)
                link(nc.vector.tensor_tensor(falls[:], node1[:], ps_next[0][:, 0:TILES], ALU.is_lt))
                nc.vector.tensor_reduce(any_falls[:], falls[:], X, ALU.add).then_inc(s_npb, 1)
                dve.wait_ge(s_cnt, 4)
                link(nc.vector.tensor_copy(unordered[:], ps_total[:, 0:1]))
                dve.sem_inc(s_sort, 1)

                def lower_keys(n, par):
                    dve.wait_ge(T["keys"], sorted_(n))
                    dve.wait_ge(T["rank"], sorted_(n - 2))
                    nc.vector.tensor_tensor(below[:, par], ps_key[par][:].rearrange("p (t e) -> p t e", t=BT),
                                            slot_key[:, slots(n)].unsqueeze(2).broadcast_to([P, BT, P]),
                                            ALU.is_lt).then_inc(T["below"], 1)

                def ranks(n, par):
                    dve.wait_ge(T["below"], sorted_(n))
                    dve.wait_ge(T["apart"], sorted_(n - 2))
                    nc.vector.tensor_reduce(rank[:, par], below[:, par], X, ALU.add).then_inc(T["rank"], 1)

                def body(n, par):
                    lower_keys(n, par)
                    ranks(n - 1, 1 - par)

                def all_ranks():
                    lower_keys(0, 0)
                    lower_keys(1, 1)
                    ranks(0, 0)
                    batches(dve, body)
                    ranks(NB - 1, 1)
                    dve.wait_ge(T["sorted"], sorted_(NB - 1))

                where_unordered(dve, all_ranks)
                link(nc.vector.tensor_copy(other_end["dst"][:], rec_f[:, :, 0]))
                link(nc.vector.tensor_copy(relation[:], rec_f[:, :, 2]))
                dve.sem_inc(s_sort, 1)
                link(nc.vector.tensor_scalar(neg_local["dst"][:], rec_f[:, :, 1], -1.0, None, ALU.mult))
                nc.vector.tensor_scalar(node1[:], rec_f[:, :, 1], 1.0, None, ALU.add).then_inc(s_npb, 1)
                dve.wait_ge(s_cnt, 6)
                link(nc.vector.tensor_tensor(is_last[:], node1[:], ps_next[1][:, 0:TILES], ALU.not_equal))
                link(nc.vector.tensor_tensor(node1[:], node1[:], ps_next[0][:, 0:TILES], ALU.not_equal))
                link(nc.vector.tensor_scalar(reset[:], node1[:], -BIG, None, ALU.mult))

        WMAX = 3 * (P + 1)
        XN = sb("XN", [P, NTL, D])
        HN = sb("HN", [P, NTL, D])
        QN = sb("QN", [P, NTL, D])
        SK = sb("SK", [P, NTL, D + 4])
        ARENA = sb("ARENA", [P, NTL * 136 + NTL * 256])
        MX = sb("MX", [P, NTL, 8])
        AD = sb("AD", [P, NTL, 1])
        NV = sb("NV", [P, NTL, 8])
        NW = sb("NW", [P, NTL, 8])
        W4 = [sb(f"W4_{n}", [D, 4 * D]) for n in range(2)]
        B4 = [sb(f"B4_{n}", [P, 4 * D]) for n in range(2)]
        WG = [sb(f"WG_{n}", [D, D]) for n in range(2)]
        VG = [sb(f"VG_{n}", [P, 3, D]) for n in range(2)]
        WQKV = sb("WQKV", [D, 3 * D])
        WOUT = sb("WOUT", [D, D])
        WKG = sb("WKG", [D, 3, D])
        HS = sb("HS", [P, 2, 3, P])
        HT = sb("HT", [P, 2, 3, P])
        idx = sb("idx", [P, UN, BT], i32)
        idx_rel = sb("idx_rel", [P, UN, BT], i32)
        gat_buf = sb("gat_buf", [P, UN, BT, 256])
        OH = sb("OH", [P, UN, BT, P])
        OB = sb("OB", [P, 2, BT, P], bf16)
        OD = sb("OD", [P, 2, BT, P])
        OHT = sb("OHT", [P, UN, BT, P])
        OTB = sb("OTB", [P, UN, BT, P], bf16)
        AD3 = sb("AD3", [P, NTL, 3], bf16)
        PR = sb("PR", [P, 2, BT, D])
        UR = sb("UR", [P, BT, D])
        SC = sb("SC", [P, 2, P])
        RS = sb("RS", [P, 2, P], bf16)
        ST = sb("ST", [P, 2, P], bf16)
        SM = sb("SM", [P, 2, P])
        MR = sb("MR", [P, 2, BT, 9])
        SPREAD = sb("SPREAD", [P, BT, 9])
        NO = sb("NO", [P, 2, BT])
        TM = sb("TM", [P, 2, BT, 8])
        MS = sb("MS", [P, 2, 8])
        MT = sb("MT", [P, 2, 8])
        CA = sb("CA", [P, 2, 8])
        CO = sb("CO", [P, 2, 8])
        SU = sb("SU", [P, 2, BT, 8])
        WV = sb("WV", [P, 2, BT * WMAX])

        psum = [ctx.enter_context(nc.psum_tensor(f"bank{n}", [P, 512], f32)) for n in range(8)]
        ps_qe = psum[0:2]
        ps_oht = psum[2]
        ps_awake = psum[3]
        ps_sct = psum[4]
        ps_sel = psum[5]
        ps_me = ps_sel[:, 128:160]
        ps_ct = psum[6:8]
        ps_ht = psum[0:2]
        ps_pj = psum[4:6]

        names = ("idx_ready rel_ready od_ready edge_ready gather_issued oh_ready ohtps_ready oht_ready qe_ready prod_ready pair_ready "
                 "s_ready rs_ready stps_ready st_ready sct_ready scan_ready back_ready ends_ready sel_ready no_ready tm_ready ms_ready mt_ready ca_ready "
                 "m_ready me_ready dif_ready sub_ready a_ready co_ready wv_ready ct_ready scaled acc_ready ur_ready").split()
        S = {n: sem(n) for n in names}
        s_stage2 = sem("s_stage2")
        s_scat2 = [sem(f"s_scat2{k}") for k in range(UN)]
        s_rec2 = sem("s_rec2")
        st2_idx = sb("st2_idx", [EP, UN, 1], i32)
        st2_rec = sb("st2_rec", [EP, UN, 1, 4], i32)
        gathered = [sem(f"gathered{k}") for k in range(UN)]
        s_w = sem("s_w")
        s_cst = sem("s_cst")
        s_node = sem("s_node")
        s_hn = sem("s_hn")
        s_var = sem("s_var")
        s_rt = sem("s_rt")
        s_hs = sem("s_hs")
        s_htps = sem("s_htps")
        s_ht = sem("s_ht")
        s_pj = sem("s_pj")
        s_pjr = sem("s_pjr")
        s_tw = sem("s_tw")
        s_td = sem("s_td")
        s_start = sem("s_start")
        s_end = sem("s_end")
        s_th = sem("s_th")
        s_out = sem("s_out")
        block = ctx.enter_context(nc.Block())

        def weights_of(l, par):
            h, c = LAYERS[l][1], LAYERS[l][2]
            return WV[:, par, 0:BT * h * (c + 1)].rearrange("p (t h c) -> p t h c", t=BT, h=h)

        def acc(l):
            h, c = LAYERS[l][1], LAYERS[l][2]
            return ARENA[:, 0:NTL * h * (c + 1)].rearrange("p (t h c) -> p t h c", t=NTL, h=h)

        KV = ARENA[:, NTL * 136:NTL * 136 + NTL * 256].rearrange("p (t c) -> p t c", t=NTL)

        REC2 = ARENA[:, NTL * 136:NTL * 136 + 4 * TILES].bitcast(i32)

        def ps_st(k):
            return ps_ct[(k + 1) % 2][:, 448:512].bitcast(bf16)

        def gb(l):
            return l * NB

        def mb(l):
            return sum(NB for x in LAYERS[:l] if x[4])

        def gathers(l):
            return 2 if LAYERS[l][0] == "kg" else 1

        SCATTERS = EC // (4 * UN)

        def arrived(l, q, k):
            before = sum(gathers(i) for i in range(l)) * len(range(k, NB, UN)) * BT * 16
            return before + (q + 1) * (gathers(l) * BT * 16)

        def following(n, q, k, by):
            return n + by, (q + (k + by) // UN if q is not None else None), (k + by) % UN

        def steps(eng, body):
            with eng.Fori(0, LOOPS) as m:
                for j in range(UN):
                    body(m * UN + (j + 1), m + (j + 1) // UN, (j + 1) % UN)
            for n in range(LOOPS * UN + 1, NB):
                body(n, n // UN, n % UN)

        def exists(n, by):
            return by <= NB - 1 - LOOPS * UN if not isinstance(n, int) else 0 <= n + by < NB

        def cols(n):
            return bass.ds(n * BT, BT)

        def held(eng, reg):
            return eng.snap(reg, min_val=0, max_val=NTL - 1)

        def groups(eng, regs, l, n):
            at_ = bass.ds(n, len(regs))
            eng.load(regs, gid[LAYERS[l][5]][0:1, at_])
            return [eng.snap(r, min_val=0, max_val=NTL - 1) for r in regs]

        @block.sync
        def _(sp):
            for l in range(2):
                sp.dma_start(W4[l][:], a[f"W4_{l}"]).then_inc(s_w, 16)
                sp.dma_start(B4[l][:], a[f"B4_{l}"].partition_broadcast(P)).then_inc(s_w, 16)
                sp.dma_start(WG[l][:], a[f"L1_gnn_W{l + 1}"]).then_inc(s_w, 16)
                for i, name in enumerate((f"att_src{l + 1}", f"att_dst{l + 1}", f"b{l + 1}")):
                    sp.dma_start(VG[l][:, i, :], a[f"L1_gnn_{name}"].partition_broadcast(P)).then_inc(s_w, 16)
            sp.dma_start(WQKV[:], a["WQKV"]).then_inc(s_w, 16)
            sp.dma_start(WOUT[:], a["WOUT"]).then_inc(s_w, 16)
            for i, name in enumerate(("w_edge", "w_node", "w_comp")):
                sp.dma_start(WKG[:, i, :], a[f"L3_gnn_{name}"]).then_inc(s_w, 16)
            sp.dma_start(XN[:, 0:NTL - 1, :],
                         a["x"][0:(NTL - 1) * P, :].rearrange("(t p) d -> p t d", p=P)).then_inc(s_w, 16)
            sp.wait_ge(s_cst, 1)
            sp.dma_start(XN[0:TAIL, NTL - 1, :], a["x"][(NTL - 1) * P:N, :]).then_inc(s_w, 16)
            for l, (kind, _, _, width, _, _) in enumerate(LAYERS):
                sp.wait_ge(s_tw, l + 1)
                src = {"conv": KV, "qkv": KV, "gat": SK[:], "kg": HN[:]}[kind]
                sp.dma_start(table[l].rearrange("(t p) c -> p t c", p=P), src).then_inc(s_td, 16)
                if l == 3:
                    sp.wait_ge(s_td, 64)
                    for k in range(UN):
                        sp.wait_ge(s_scat2[k], 4 * SCATTERS * 16)
                    sp.dma_start(REC2, rec_dram["src"].rearrange("(p t) f -> p (t f)", p=P)).then_inc(s_rec2, 16)
            sp.wait_ge(s_end, len(LAYERS) + 1)
            sp.dma_start(out[0:(NTL - 1) * P, :].rearrange("(t p) d -> p t d", p=P),
                         XN[:, 0:NTL - 1, :]).then_inc(s_out, 16)
            sp.dma_start(out[(NTL - 1) * P:N, :], XN[0:TAIL, NTL - 1, :]).then_inc(s_out, 16)
            sp.wait_ge(s_out, 32)

        N_W = 16 * (2 * 6 + 5 + 2)

        @block.gpsimd
        def _(pool):
            nc.gpsimd.memset(XN[:, NTL - 1, :], 0.0).then_inc(s_cst, 1)
            def stage(j, t, par, src, parts):
                pool.wait_ge(s_htps, j + 1)
                nc.gpsimd.tensor_copy(HS[:, par, 0:parts, :], src(t)).then_inc(s_hs, 1)

            def node_tiles(q, src, parts):
                pool.wait_ge(s_hn, q + 1)
                with pool.Fori(0, NTL // 2) as m:
                    for par in range(2):
                        stage(m * 2 + (q * NTL + par), m * 2 + par, par, src, parts)
                stage(q * NTL + NTL - 1, NTL - 1, 0, src, parts)

            def h_tile(t):
                return HN[:, bass.ds(t, 1), :]

            for l, (kind, _, _, width, _, key) in enumerate(LAYERS):
                node_tiles(l, h_tile, 1)
                pool.wait_ge(s_td, 16 * (l + 1))

                def scatter(n, k):
                    at_ = bass.ds(n + l * (EC // 4), 1)
                    nc.gpsimd.tensor_copy(st2_idx[:, k, :], addr["src"][:, at_]).then_inc(s_stage2, 1)
                    nc.gpsimd.tensor_copy(st2_rec[:, k, :, :], recs["src"][:, at_, :]).then_inc(s_stage2, 1)
                    pool.wait_ge(s_stage2, (n + l * (EC // 4)) * 2 + 2)
                    pool.sem_inc(S["gather_issued"], 1)
                    nc.gpsimd.indirect_dma_start(
                        out=rec_dram["src"][:, :],
                        out_offset=bass.IndirectOffsetOnAxis(ap=st2_idx[:, k, :], axis=0),
                        in_=st2_rec[:, k, 0, :], in_offset=None).then_inc(s_scat2[k], 16)

                def scattered(m, k):
                    pool.wait_ge(s_scat2[k], (m + 1 + l * SCATTERS) * 16)

                def gather(n, k):
                    pool.wait_ge(S["wv_ready"], done(gb(l) + n - UN))
                    nc.gpsimd.tensor_copy(idx[:, k, :], other_end[key][:, cols(n)]).then_inc(S["idx_ready"], 1)
                    if kind == "kg":
                        nc.gpsimd.tensor_copy(idx_rel[:, k, :], relation[:, cols(n)]).then_inc(S["rel_ready"], 1)
                        pool.wait_ge(S["rel_ready"], done(n))
                        pool.sem_inc(S["gather_issued"], 1)
                    pool.wait_ge(S["idx_ready"], done(gb(l) + n))
                    pool.sem_inc(S["gather_issued"], 1)
                    for t in range(BT):
                        nc.gpsimd.indirect_dma_start(
                            out=gat_buf[:, k, t, 0:width], out_offset=None, in_=table[l][:, :],
                            in_offset=bass.IndirectOffsetOnAxis(ap=idx[:, k, t:t + 1], axis=0),
                        ).then_inc(gathered[k], 16)
                        if kind == "kg":
                            nc.gpsimd.indirect_dma_start(
                                out=gat_buf[:, k, t, D:2 * D], out_offset=None, in_=a["L3_gnn_rel_emb"][:, :],
                                in_offset=bass.IndirectOffsetOnAxis(ap=idx_rel[:, k, t:t + 1], axis=0),
                            ).then_inc(gathered[k], 16)

                both = SCATTERS if l < 4 else 0
                if both:
                    with pool.Fori(0, both) as m:
                        for k in range(UN):
                            scatter(m * UN + k, k)
                            gather(m * UN + k, k)
                            scattered(m, k)
                with pool.Fori(both, NB // UN) as m:
                    for k in range(UN):
                        gather(m * UN + k, k)
                for n in range(NB // UN * UN, NB):
                    gather(n, n % UN)
            a5 = acc(5)
            node_tiles(6, lambda t: a5[:, bass.ds(t, 1), :, 0:D].rearrange("p a h d -> p (a h) d"), 3)

        @block.scalar
        def _(act):
            def node_sqrt(q):
                act.wait_ge(s_var, q + 1)
                nc.scalar.activation(NW[:, :, 0], NV[:, :, 0], ACT.Sqrt).then_inc(s_rt, 1)

            def evacuate_ht(j, par, parts=1):
                act.wait_ge(s_htps, j + 3)
                act.wait_ge(s_pj, j + 1)
                nc.scalar.activation(HT[:, par, 0:parts, :],
                                     ps_ht[par][:, 0:parts * P].rearrange("p (a b) -> p a b", a=parts),
                                     ACT.Copy).then_inc(s_ht, 1)

            def node_tiles(base, parts=1):
                with act.Fori(0, NTL // 2) as m:
                    for par in range(2):
                        evacuate_ht(m * 2 + (base + par), par, parts)
                evacuate_ht(base + NTL - 1, 0, parts)

            def softmax_layer(l):
                kind, h, c, width, has_max, key = LAYERS[l]

                def transposed_onehots(n, q, k):
                    act.wait_ge(S["ohtps_ready"], done(gb(l) + n))
                    if has_max:
                        act.wait_ge(S["me_ready"], done(mb(l) + n - UN))
                    act.wait_ge(S["qe_ready"], done(gb(l) + n - UN))
                    v = ps_oht[:].rearrange("p (t e) -> p t e", t=BT)
                    if kind == "gat":
                        nc.scalar.activation(OTB[:, k], v, ACT.Copy)
                    nc.scalar.activation(OHT[:, k], v, ACT.Copy).then_inc(S["oht_ready"], 1)

                def distances(n, q, k):
                    act.wait_ge(S["oh_ready"], done(gb(l) + n - 2))
                    for t in range(BT):
                        last = nc.scalar.activation(OD[:, k % 2, t, :], iota_row[:], ACT.Abs,
                                                    bias=neg_local[key][:, bass.ds(n * BT + t, 1)])
                    last.then_inc(S["od_ready"], 1)

                def onehots(n, q, k):
                    act.wait_ge(S["ct_ready"], done(gb(l) + n - UN))
                    act.wait_ge(S["od_ready"], done(gb(l) + n))
                    act.wait_ge(S["ohtps_ready"], done(gb(l) + n - 2))
                    nc.scalar.activation(OH[:, k], OD[:, k % 2], ACT.Relu, bias=1.0, scale=-1.0)
                    nc.scalar.activation(OB[:, k % 2], OD[:, k % 2], ACT.Relu, bias=1.0,
                                         scale=-1.0).then_inc(S["oh_ready"], 1)

                def run_starts(n, q, k):
                    act.wait_ge(S["stps_ready"], done(mb(l) + n - 2))
                    nc.scalar.activation(RS[:, k % 2, 0:BT * 8].rearrange("p (t h) -> p t h", t=BT),
                                         reset[:, cols(n)].unsqueeze(2).broadcast_to([P, BT, 8]),
                                         ACT.Copy).then_inc(S["rs_ready"], 1)

                def starts_evacuated(n, q, k):
                    act.wait_ge(S["stps_ready"], done(mb(l) + n))
                    act.wait_ge(S["scan_ready"], done(mb(l) + n - 2))
                    nc.scalar.activation(ST[:, k % 2, :], ps_st(k), ACT.Copy).then_inc(S["st_ready"], 1)

                def exponentials(n, q, k):
                    par = k % 2
                    act.wait_ge(S["ct_ready"], done(gb(l) + n - 2))
                    if has_max:
                        act.wait_ge(S["ca_ready"], done(mb(l) + n))
                        nc.scalar.activation(CO[:, par, 0:h], CA[:, par, 0:h], ACT.Exp).then_inc(S["co_ready"], 1)
                    act.wait_ge(S["sub_ready"], done(gb(l) + n))
                    nc.scalar.activation(weights_of(l, par)[:, :, :, c], SU[:, par, :, 0:h],
                                         ACT.Exp).then_inc(S["a_ready"], 1)

                def rows_weighted(n, k):
                    wv = weights_of(l, k % 2)
                    act.wait_ge(S["a_ready"], done(gb(l) + n))
                    for i, first in ((0, D), (1, 0)):
                        for t in range(BT):
                            last = nc.scalar.activation(wv[:, t, i, 0:c], gat_buf[:, k, t, first:first + D],
                                                        ACT.Copy, scale=wv[:, t, i, c:c + 1])
                    last.then_inc(S["edge_ready"], 1)

                def step(n, q, k):
                    if exists(n, 3):
                        onehots(*following(n, q, k, 3))
                    if has_max and exists(n, 1):
                        starts_evacuated(*following(n, q, k, 1))
                    exponentials(n, q, k)
                    if kind == "kg":
                        rows_weighted(n, k)
                    if has_max and exists(n, 2):
                        run_starts(*following(n, q, k, 2))
                    if exists(n, 4):
                        distances(*following(n, q, k, 4))
                    if exists(n, 3):
                        transposed_onehots(*following(n, q, k, 3))

                for n in range(3):
                    distances(n, 0, n)
                    onehots(n, 0, n)
                distances(3, 0, 3)
                for n in range(3):
                    transposed_onehots(n, 0, n)
                if has_max:
                    run_starts(0, 0, 0)
                    run_starts(1, 0, 1)
                    starts_evacuated(0, 0, 0)
                step(0, 0, 0)
                steps(act, step)

            node_sqrt(0)
            node_tiles(0)
            softmax_layer(0)
            node_tiles(NTL)
            softmax_layer(1)
            node_sqrt(1)
            node_tiles(2 * NTL)
            softmax_layer(2)
            node_tiles(3 * NTL)
            softmax_layer(3)
            node_sqrt(2)
            node_tiles(4 * NTL)
            softmax_layer(4)
            node_tiles(5 * NTL)
            node_sqrt(3)
            softmax_layer(5)
            with act.Fori(0, NTL // 2) as m:
                for par in range(2):
                    j = m * 2 + (6 * NTL + par)
                    evacuate_ht(j, par, 3)
                    act.wait_ge(s_pj, j + 3)
                    act.wait_ge(s_pjr, j + 1)
                    nc.scalar.activation(PR[:, par, 0:3, :], ps_pj[par][:, 0:3 * P].rearrange("p (a b) -> p a b", a=3),
                                         ACT.Tanh).then_inc(s_th, 1)
            evacuate_ht(7 * NTL - 1, 0, 3)
            act.wait_ge(s_pj, 7 * NTL - 1 + 3)
            act.wait_ge(s_pjr, 7 * NTL - 1 + 1)
            nc.scalar.activation(PR[:, 0, 0:3, :], ps_pj[0][:, 0:3 * P].rearrange("p (a b) -> p a b", a=3),
                                 ACT.Tanh).then_inc(s_th, 1)

        @block.tensor
        def _(pe):
            regs = [pe.alloc_register("pe_group")]

            def node_tile(j, par, w, parts, width):
                pe.wait_ge(s_hs, j + 1)
                pe.wait_ge(s_ht, j + 1)
                for i in range(parts):
                    last = nc.tensor.transpose(ps_ht[par][:, i * P:(i + 1) * P], HS[:, par, i, :], ident[:])
                last.then_inc(s_htps, 1)
                pe.wait_ge(s_ht, j + 3)
                pe.wait_ge(s_pjr, j + 1)
                for i in range(parts):
                    last = nc.tensor.matmul(ps_pj[par][:, i * P:i * P + width], HT[:, par, i, :], w(i),
                                            start=True, stop=True)
                last.then_inc(s_pj, 1)

            def node_tiles(base, w, parts, width):
                with pe.Fori(0, NTL // 2) as m:
                    for par in range(2):
                        node_tile(m * 2 + (base + par), par, w, parts, width)
                node_tile(base + NTL - 1, 0, w, parts, width)

            def softmax_layer(l):
                kind, h, c, width, has_max, key = LAYERS[l]
                w = h * (c + 1)
                expand = {"conv": QN, "qkv": QN, "gat": AD3, "kg": HN}[kind]
                ew = 3 if kind == "gat" else D

                def onehots_transposed(n, q, k):
                    pe.wait_ge(S["oh_ready"], done(gb(l) + n))
                    pe.wait_ge(S["oht_ready"], done(gb(l) + n - 1))
                    for t in range(BT):
                        last = nc.tensor.matmul(ps_oht[:, t * P:(t + 1) * P], OB[:, k % 2, t, :], ident_bf[:],
                                                start=True, stop=True)
                    last.then_inc(S["ohtps_ready"], 1)

                def expansion(n, q, k):
                    par = k % 2
                    g, = groups(pe, regs, l, n)
                    pe.wait_ge(S["oht_ready"], done(gb(l) + n))
                    pe.wait_ge(S["prod_ready"], done(gb(l) + n - 2))
                    for t in range(BT):
                        last = nc.tensor.matmul(ps_qe[par][:, t * P:t * P + ew],
                                                OTB[:, k, t, :] if kind == "gat" else OHT[:, k, t, :],
                                                expand[:, bass.ds(g, 1), :].rearrange("p a d -> p (a d)"),
                                                start=True, stop=True)
                    last.then_inc(S["qe_ready"], 1)

                def starts_transposed(n, q, k):
                    pe.wait_ge(S["rs_ready"], done(mb(l) + n))
                    pe.wait_ge(S["acc_ready"], done(gb(l) + n - 3))
                    nc.tensor.transpose(ps_st(k), RS[:, k % 2, :], ident_bf[:]).then_inc(S["stps_ready"], 1)

                def scores_transposed(n, q, k):
                    par = k % 2
                    pe.wait_ge(S["s_ready"], done(gb(l) + n))
                    pe.wait_ge(S["scan_ready"], done(mb(l) + n - 1))
                    nc.tensor.matmul(ps_sct[:, 0:P], SC[:, par, :], ident[:], start=True,
                                     stop=True).then_inc(S["sct_ready"], 1)

                def maxima_back(n, q, k):
                    pe.wait_ge(S["scan_ready"], done(mb(l) + n))
                    nc.tensor.matmul(ps_sel[:, 0:BT * 9], SM[:, k % 2, :], SPREAD[:].rearrange("p t h -> p (t h)"),
                                     start=True, stop=True).then_inc(S["back_ready"], 1)

                def maxima_by_node(n, q, k):
                    pe.wait_ge(S["ends_ready"], done(mb(l) + n))
                    for t in range(BT):
                        last = nc.tensor.matmul(ps_sel[:, 64 + t * 9:64 + (t + 1) * 9], OH[:, k, t, :],
                                                MR[:, k % 2, t, :], start=True, stop=True)
                    last.then_inc(S["sel_ready"], 1)

                def maxima_expanded(n, q, k):
                    par = k % 2
                    pe.wait_ge(S["mt_ready"], done(mb(l) + n))
                    for t in range(BT):
                        last = nc.tensor.matmul(ps_me[:, t * 8:t * 8 + h], OHT[:, k, t, :], MT[:, par, 0:h],
                                                start=True, stop=True)
                    last.then_inc(S["me_ready"], 1)

                def sums(n, k):
                    par = k % 2
                    pe.wait_ge(S["wv_ready"], done(gb(l) + n))
                    pe.wait_ge(S["acc_ready"], done(gb(l) + n - 2))
                    for t in range(BT):
                        last = nc.tensor.matmul(ps_ct[par][:, 0:w], OH[:, k, t, :], WV[:, par, t * w:(t + 1) * w],
                                                start=(t == 0), stop=(t == BT - 1))
                    last.then_inc(S["ct_ready"], 1)

                def stay_awake(count):
                    for _ in range(count):
                        nc.tensor.matmul(ps_awake[:], ident_bf[:],
                                         ident_bf[:].unsqueeze(1).broadcast_to([P, BT, P]), start=True, stop=True)

                awake = AWAKE[h]

                def step(n, q, k):
                    if has_max:
                        stay_awake(awake[0])
                        maxima_expanded(n, q, k)
                    if exists(n, 2):
                        expansion(*following(n, q, k, 2))
                    if has_max and exists(n, 1):
                        starts_transposed(*following(n, q, k, 1))
                        stay_awake(awake[1])
                        scores_transposed(*following(n, q, k, 1))
                        stay_awake(awake[2])
                        maxima_back(*following(n, q, k, 1))
                        stay_awake(awake[3])
                        maxima_by_node(*following(n, q, k, 1))
                    if has_max:
                        stay_awake(awake[4])
                    sums(n, k)
                    if exists(n, 3):
                        onehots_transposed(*following(n, q, k, 3))

                for n in range(3):
                    onehots_transposed(n, 0, n)
                pe.wait_ge(s_start, l + 1)
                expansion(0, 0, 0)
                expansion(1, 0, 1)
                if has_max:
                    stay_awake(24)
                    starts_transposed(0, 0, 0)
                    scores_transposed(0, 0, 0)
                    maxima_back(0, 0, 0)
                    maxima_by_node(0, 0, 0)
                step(0, 0, 0)
                steps(pe, step)

            pe.wait_ge(s_w, N_W)
            for q, (w, width) in enumerate(((W4[0], 512), (W4[1], 512), (WG[0], 128), (WG[1], 128), (WQKV, 384))):
                node_tiles(q * NTL, lambda i, w=w, width=width: w[:, 0:width], 1, width)
                softmax_layer(q)
            node_tiles(5 * NTL, lambda i: WOUT[:], 1, D)
            softmax_layer(5)
            node_tiles(6 * NTL, lambda i: WKG[:, i, :], 3, P)

        @block.vector
        def _(dve):
            regs = [dve.alloc_register(f"dve_group{t}") for t in range(2)]
            count = [0]

            def link(ins):
                count[0] += 1
                ins.then_inc(s_node, 1)
                dve.wait_ge(s_node, count[0])

            def over(v, n=D):
                return v.unsqueeze(2).broadcast_to([P, NTL, n])

            def along(v):
                return v.unsqueeze(1).broadcast_to([P, NTL, D])

            def layer_norm_relu(q):
                link(nc.vector.tensor_reduce(NV[:, :, 1], XN[:], X, ALU.add))
                link(nc.vector.tensor_scalar(NV[:, :, 1], NV[:, :, 1], 1.0 / D, None, ALU.mult))
                link(nc.vector.tensor_tensor(HN[:], XN[:], over(NV[:, :, 1]), ALU.subtract))
                link(nc.vector.tensor_tensor(QN[:], HN[:], HN[:], ALU.mult))
                link(nc.vector.tensor_reduce(NV[:, :, 2], QN[:], X, ALU.add))
                nc.vector.tensor_scalar(NV[:, :, 0], NV[:, :, 2], 1.0 / D, 1e-5, ALU.mult, ALU.add).then_inc(s_var, 1)
                dve.wait_ge(s_rt, q + 1)
                link(nc.vector.reciprocal(NW[:, :, 1], NW[:, :, 0]))
                link(nc.vector.tensor_tensor(HN[:], HN[:], over(NW[:, :, 1]), ALU.mult))
                link(nc.vector.tensor_scalar(HN[:], HN[:], 0.0, None, ALU.max))

            def products(base, body):
                with dve.Fori(0, NTL // 2) as m:
                    for par in range(2):
                        dve.wait_ge(s_pj, m * 2 + (base + par + 3))
                        body(m * 2 + par, par).then_inc(s_pjr, 1)
                dve.wait_ge(s_pj, base + NTL - 1 + 3)
                body(NTL - 1, 0).then_inc(s_pjr, 1)

            def at(v, t):
                return v[:, bass.ds(t, 1), :].rearrange("p a d -> p (a d)")

            def settle(base):
                dve.wait_ge(s_pjr, base + NTL + 2)

            def normalised_heads(l, guard_add):
                h, c = LAYERS[l][1], LAYERS[l][2]
                s = acc(l)
                w = NV[:, :, 0:h]
                if guard_add:
                    link(nc.vector.tensor_scalar(w, s[:, :, :, c], guard_add, None, ALU.add))
                else:
                    link(nc.vector.tensor_scalar(w, s[:, :, :, c], TINY, None, ALU.max))
                link(nc.vector.reciprocal(NW[:, :, 0:h], w))
                if h == 8:
                    hn = HN[:].rearrange("p t (h c) -> p (t h) c", h=h)
                    link(nc.vector.tensor_tensor(
                        hn, s.rearrange("p t h c -> p (t h) c")[:, :, 0:c],
                        NW[:].rearrange("p t h -> p (t h)").unsqueeze(2).broadcast_to([P, NTL * h, c]), ALU.mult))
                elif h == 1:
                    link(nc.vector.tensor_tensor(HN[:], s[:, :, 0, 0:c], over(NW[:, :, 0]), ALU.mult))
                else:
                    for i in range(h):
                        link(nc.vector.tensor_tensor(s[:, :, i, 0:c], s[:, :, i, 0:c], over(NW[:, :, i]), ALU.mult))

            def softmax_layer(l):
                kind, h, c, width, has_max, key = LAYERS[l]
                w = h * (c + 1)
                sums = acc(l)

                def scores_of(par):
                    return SC[:, par, 0:BT * 8].rearrange("p (t h) -> p t h", t=BT)[:, :, 0:h]

                def score_products(n, q, k):
                    par = k % 2
                    dve.wait_ge(S["qe_ready"], done(gb(l) + n))
                    dve.wait_ge(gathered[k], arrived(l, q, k))
                    qe = ps_qe[par][:].rearrange("p (t d) -> p t d", t=BT)
                    g = gat_buf[:, k]
                    if kind in ("conv", "qkv"):
                        nc.vector.tensor_tensor(PR[:, 0], qe, g[:, :, 0:D], ALU.mult).then_inc(S["prod_ready"], 1)
                    elif kind == "gat":
                        nc.vector.tensor_reduce(PR[:, 0, :, 1], qe[:, :, 0:3], X,
                                                ALU.add).then_inc(S["prod_ready"], 1)
                    else:
                        nc.vector.tensor_tensor(PR[:, 0], qe, g[:, :, D:2 * D], ALU.mult)
                        nc.vector.tensor_tensor(PR[:, 1], qe, g[:, :, 0:D], ALU.mult).then_inc(S["prod_ready"], 1)

                def scores(n, q, k):
                    par = k % 2
                    s = scores_of(par)
                    dve.wait_ge(S["prod_ready"], done(gb(l) + n))
                    if kind == "gat":
                        nc.vector.tensor_tensor(PR[:, 0, :, 0:1], PR[:, 0, :, 1:2], gat_buf[:, k, :, D:D + 1],
                                                ALU.add).then_inc(S["pair_ready"], 1)
                        dve.wait_ge(S["pair_ready"], done((l - 2) * NB + n))
                    if kind in ("conv", "qkv"):
                        nc.vector.tensor_reduce(SC[:, par, 0:BT * 8],
                                                PR[:, 0].rearrange("p t (h c) -> p (t h) c", h=h),
                                                X, ALU.add).then_inc(S["s_ready"], 1)
                    elif kind == "gat":
                        nc.vector.scalar_tensor_tensor(s, PR[:, 0, :, 0:1], 0.2, PR[:, 0, :, 0:1],
                                                       ALU.mult, ALU.max).then_inc(S["s_ready"], 1)
                    else:
                        nc.vector.tensor_reduce(s[:, :, 0], PR[:, 0], X, ALU.add)
                        nc.vector.tensor_reduce(s[:, :, 1], PR[:, 1], X, ALU.add).then_inc(S["pair_ready"], 1)
                        dve.wait_ge(S["pair_ready"], done(2 * NB + n))
                        nc.vector.tensor_tensor(s[:, :, 2], s[:, :, 0], s[:, :, 1],
                                                ALU.add).then_inc(S["s_ready"], 1)

                def clipped(n, q, k):
                    dve.wait_ge(S["s_ready"], done(gb(l) + n))
                    nc.vector.tensor_scalar(SU[:, k % 2, :, 0:h], scores_of(k % 2), -10.0, 10.0, ALU.max,
                                            ALU.min).then_inc(S["sub_ready"], 1)

                def run_maxima(n, q, k):
                    dve.wait_ge(S["sct_ready"], done(mb(l) + n))
                    dve.wait_ge(S["st_ready"], done(mb(l) + n))
                    dve.wait_ge(S["back_ready"], done(mb(l) + n - 2))
                    nc.vector.tensor_tensor_scan(SM[:, k % 2, :], ST[:, k % 2, :], ps_sct[:, 0:P], -BIG,
                                                 ALU.add, ALU.max).then_inc(S["scan_ready"], 1)

                def run_ends(n, q, k):
                    dve.wait_ge(S["back_ready"], done(mb(l) + n))
                    nc.vector.tensor_tensor(MR[:, k % 2], ps_sel[:, 0:BT * 9].rearrange("p (t h) -> p t h", t=BT),
                                            is_last[:, cols(n)].unsqueeze(2).broadcast_to([P, BT, 9]),
                                            ALU.mult).then_inc(S["ends_ready"], 1)

                def by_node():
                    return ps_sel[:, 64:64 + BT * 9].rearrange("p (t h) -> p t h", t=BT)

                def absent(n, q, k):
                    dve.wait_ge(S["sel_ready"], done(mb(l) + n))
                    nc.vector.tensor_scalar(NO[:, k % 2], by_node()[:, :, 8], -1.0, BIG, ALU.add,
                                            ALU.mult).then_inc(S["no_ready"], 1)

                def tile_maxima(n, q, k):
                    dve.wait_ge(S["no_ready"], done(mb(l) + n))
                    nc.vector.tensor_tensor(TM[:, k % 2], by_node()[:, :, 0:8],
                                            NO[:, k % 2].unsqueeze(2).broadcast_to([P, BT, 8]),
                                            ALU.add).then_inc(S["tm_ready"], 1)

                def batch_maxima(n, q, k):
                    dve.wait_ge(S["tm_ready"], done(mb(l) + n))
                    nc.vector.tensor_reduce(MS[:, k % 2, :], TM[:, k % 2].rearrange("p t h -> p h t"), X,
                                            ALU.max).then_inc(S["ms_ready"], 1)

                def new_maxima(n, k, group):
                    par = k % 2
                    m_old = MX[:, bass.ds(group, 1), 0:h].rearrange("p a h -> p (a h)")
                    dve.wait_ge(S["ms_ready"], done(mb(l) + n))
                    dve.wait_ge(S["m_ready"], done(mb(l) + n - 1))
                    nc.vector.tensor_tensor(MT[:, par, 0:h], m_old, MS[:, par, 0:h], ALU.max).then_inc(S["mt_ready"], 1)

                def change(n, k, group):
                    par = k % 2
                    m_old = MX[:, bass.ds(group, 1), 0:h].rearrange("p a h -> p (a h)")
                    dve.wait_ge(S["mt_ready"], done(mb(l) + n))
                    nc.vector.tensor_tensor(CA[:, par, 0:h], m_old, MT[:, par, 0:h],
                                            ALU.subtract).then_inc(S["ca_ready"], 1)

                def keep_maxima(n, k, group):
                    par = k % 2
                    m_old = MX[:, bass.ds(group, 1), 0:h].rearrange("p a h -> p (a h)")
                    dve.wait_ge(S["ca_ready"], done(mb(l) + n))
                    nc.vector.tensor_tensor(m_old, MT[:, par, 0:h], MS[:, par, 0:h], ALU.max).then_inc(S["m_ready"], 1)

                def below_maximum(n, k, meanwhile):
                    par = k % 2
                    su = SU[:, par, :, 0:h]
                    me = ps_me.rearrange("p (t h) -> p t h", t=BT)[:, :, 0:h]
                    dve.wait_ge(S["me_ready"], done(mb(l) + n))
                    nc.vector.tensor_tensor(su, scores_of(par), me, ALU.subtract).then_inc(S["dif_ready"], 1)
                    meanwhile()
                    dve.wait_ge(S["dif_ready"], done(mb(l) + n))
                    nc.vector.tensor_scalar(su, su, 0.0, None, ALU.min).then_inc(S["sub_ready"], 1)

                def rows_added(n, k):
                    g = gat_buf[:, k]
                    nc.vector.tensor_tensor(UR[:], g[:, :, 0:D], g[:, :, D:2 * D],
                                            ALU.add).then_inc(S["ur_ready"], 1)

                def weighted(n, k):
                    par = k % 2
                    dve.wait_ge(S["a_ready"], done(gb(l) + n))
                    g = gat_buf[:, k]
                    wv = weights_of(l, par)
                    if h == 8:
                        last = nc.vector.tensor_tensor(
                            wv[:, :, :, 0:c], g[:, :, D:2 * D].rearrange("p t (h c) -> p t h c", h=h),
                            wv[:, :, :, c:c + 1].broadcast_to([P, BT, h, c]), ALU.mult)
                    elif h == 1:
                        last = nc.vector.tensor_tensor(wv[:, :, 0, 0:c], g[:, :, 0:D],
                                                       wv[:, :, 0, c:c + 1].broadcast_to([P, BT, c]), ALU.mult)
                    else:
                        dve.wait_ge(S["ur_ready"], done(n))
                        dve.wait_ge(S["edge_ready"], done(n))
                        last = nc.vector.tensor_tensor(wv[:, :, 2, 0:c], UR[:],
                                                       wv[:, :, 2, c:c + 1].broadcast_to([P, BT, c]), ALU.mult)
                    last.then_inc(S["wv_ready"], 1)

                def rescale(n, k, group):
                    if has_max and h == 8:
                        total = sums[:, bass.ds(group, 1)].rearrange("p a h c -> p (a h) c")
                        dve.wait_ge(S["acc_ready"], done(gb(l) + n - 1))
                        dve.wait_ge(S["co_ready"], done(mb(l) + n))
                        nc.vector.tensor_tensor(total, total,
                                                CO[:, k % 2, :].unsqueeze(2).broadcast_to([P, h, c + 1]),
                                                ALU.mult).then_inc(S["scaled"], 1)

                def add_up(n, k, group):
                    par = k % 2
                    total = sums[:, bass.ds(group, 1)].rearrange("p a h c -> p (a h) c")
                    ct = ps_ct[par][:, 0:w].rearrange("p (h c) -> p h c", h=h)
                    dve.wait_ge(S["acc_ready"], done(gb(l) + n - 1))
                    dve.wait_ge(S["ct_ready"], done(gb(l) + n))
                    if h == 8:
                        if has_max:
                            dve.wait_ge(S["scaled"], done(gb(l) + n))
                        last = nc.vector.tensor_tensor(total, total, ct, ALU.add)
                    else:
                        dve.wait_ge(S["co_ready"], done(mb(l) + n))
                        for i in range(h):
                            last = nc.vector.scalar_tensor_tensor(total[:, i, :], total[:, i, :],
                                                                  CO[:, par, i:i + 1], ct[:, i, :],
                                                                  ALU.mult, ALU.add)
                    last.then_inc(S["acc_ready"], 1)

                def step(n, q, k):
                    before = now = held(dve, regs[0])
                    if exists(n, -1):
                        now = held(dve, regs[1])
                    ahead = following(n, q, k, 1) if exists(n, 1) else None
                    if has_max:
                        new_maxima(n, k, now)
                    if ahead:
                        score_products(*ahead)
                    if has_max:
                        change(n, k, now)
                    if exists(n, -1):
                        rescale(n - 1, (k - 1) % UN, before)
                    if not has_max:
                        weighted(n, k)
                        if ahead:
                            dve.load(regs, gid[key][0:1, bass.ds(n, 2)])
                    if ahead:
                        scores(*ahead)
                    if has_max:
                        keep_maxima(n, k, now)
                        below_maximum(n, k, lambda: add_up(n - 1, (k - 1) % UN, before) if exists(n, -1) else None)
                        if ahead:
                            run_maxima(*ahead)
                        if kind == "kg":
                            rows_added(n, k)
                        else:
                            weighted(n, k)
                        if ahead:
                            dve.load(regs, gid[key][0:1, bass.ds(n, 2)])
                            run_ends(*ahead)
                            absent(*ahead)
                            tile_maxima(*ahead)
                            batch_maxima(*ahead)
                        if kind == "kg":
                            weighted(n, k)
                    else:
                        if exists(n, -1):
                            add_up(n - 1, (k - 1) % UN, before)
                        if ahead:
                            clipped(*ahead)

                first = 0, 0, 0
                dve.load(regs, gid[key][0:1, 0:2])
                score_products(*first)
                scores(*first)
                if has_max:
                    run_maxima(*first)
                    run_ends(*first)
                    absent(*first)
                    tile_maxima(*first)
                    batch_maxima(*first)
                else:
                    clipped(*first)
                step(*first)
                steps(dve, step)
                k = (NB - 1) % UN
                _, g = groups(dve, regs, l, NB - 2)
                rescale(NB - 1, k, g)
                add_up(NB - 1, k, g)
                dve.wait_ge(S["acc_ready"], done(gb(l + 1) - 1))
                dve.sem_inc(s_end, 1)

            def clear(l):
                link(nc.vector.memset(acc(l), 0.0))
                link(nc.vector.memset(MX[:], -BIG))

            for s in S.values():
                dve.sem_inc(s, CR)
            dve.sem_inc(s_ht, 2)
            dve.sem_inc(s_htps, 2)
            dve.sem_inc(s_pj, 2)
            dve.sem_inc(s_pjr, 2)
            dve.wait_ge(s_cst, 1)
            link(nc.vector.memset(SC[:], 0.0))
            link(nc.vector.memset(SC[:, :, BT * 8:BT * 8 + 1], 1.0))
            link(nc.vector.memset(RS[:], 0.0))
            link(nc.vector.tensor_copy(SPREAD[:, :, 0:8], ident[:, 0:BT * 8].rearrange("p (t h) -> p t h", t=BT)))
            link(nc.vector.tensor_copy(SPREAD[:, :, 8:9],
                                       ident[:, BT * 8:BT * 8 + 1].unsqueeze(1).broadcast_to([P, BT, 1])))
            dve.wait_ge(s_w, N_W)
            for l in range(2):
                link(nc.vector.tensor_scalar(B4[l][:, 0:D], B4[l][:, 0:D], 0.25, None, ALU.mult))

            layer_norm_relu(0)
            for l in range(2):
                dve.sem_inc(s_hn, 1)

                def conv_products(t, par, l=l):
                    ps = ps_pj[par]
                    nc.vector.scalar_tensor_tensor(at(QN, t), ps[:, 0:D], 0.25, B4[l][:, 0:D], ALU.mult, ALU.add)
                    nc.vector.tensor_tensor(at(KV, t), ps[:, D:3 * D], B4[l][:, D:3 * D], ALU.add)
                    return nc.vector.tensor_tensor(at(SK[:, :, 0:D], t), ps[:, 3 * D:4 * D], B4[l][:, 3 * D:4 * D],
                                                   ALU.add)

                products(l * NTL, conv_products)
                settle(l * NTL)
                dve.sem_inc(s_tw, 1)
                clear(l)
                dve.sem_inc(s_start, 1)
                softmax_layer(l)
                normalised_heads(l, None)
                link(nc.vector.tensor_tensor(HN[:], HN[:], SK[:, :, 0:D], ALU.add))
                if l == 0:
                    link(nc.vector.tensor_scalar(HN[:], HN[:], 0.0, None, ALU.max))
            link(nc.vector.tensor_tensor(XN[:], XN[:], HN[:], ALU.add))

            layer_norm_relu(1)
            for g in range(2):
                l = 2 + g
                dve.sem_inc(s_hn, 1)
                products(l * NTL, lambda t, par: nc.vector.tensor_copy(at(SK[:, :, 0:D], t), ps_pj[par][:, 0:D]))
                settle(l * NTL)
                link(nc.vector.tensor_tensor(QN[:], SK[:, :, 0:D], along(VG[g][:, 0, :]), ALU.mult))
                link(nc.vector.tensor_reduce(SK[:, :, D], QN[:], X, ALU.add))
                link(nc.vector.memset(SK[:, :, D + 1:D + 4], 0.0))
                dve.sem_inc(s_tw, 1)
                link(nc.vector.tensor_tensor(QN[:], SK[:, :, 0:D], along(VG[g][:, 1, :]), ALU.mult))
                link(nc.vector.tensor_reduce(AD[:, :, 0], QN[:], X, ALU.add))
                link(nc.vector.tensor_copy(AD3[:, :, 0:1], AD[:]))
                link(nc.vector.tensor_tensor(NV[:, :, 0:1], AD[:], AD3[:, :, 0:1], ALU.subtract))
                link(nc.vector.tensor_copy(AD3[:, :, 1:2], NV[:, :, 0:1]))
                link(nc.vector.tensor_tensor(AD3[:, :, 2:3], NV[:, :, 0:1], AD3[:, :, 1:2], ALU.subtract))
                link(nc.vector.tensor_tensor(NV[:, :, 0], SK[:, :, D], AD[:, :, 0], ALU.add))
                link(nc.vector.scalar_tensor_tensor(MX[:, :, 0], NV[:, :, 0], 0.2, NV[:, :, 0], ALU.mult, ALU.max))
                link(nc.vector.tensor_copy(acc(l)[:, :, 0, 0:D], SK[:, :, 0:D]))
                link(nc.vector.memset(acc(l)[:, :, 0, D:D + 1], 1.0))
                dve.sem_inc(s_start, 1)
                softmax_layer(l)
                normalised_heads(l, 1e-16)
                link(nc.vector.tensor_tensor(HN[:], HN[:], along(VG[g][:, 2, :]), ALU.add))
                link(nc.vector.tensor_scalar(HN[:], HN[:], 0.0, None, ALU.max))
            link(nc.vector.tensor_tensor(XN[:], XN[:], HN[:], ALU.add))

            dve.wait_ge(s_rec2, 16)
            rec2 = REC2.rearrange("p (t f) -> p t f", f=4)
            link(nc.vector.tensor_copy(other_end["src"][:], rec2[:, :, 0]))
            link(nc.vector.tensor_scalar(neg_local["src"][:], rec2[:, :, 1], -1.0, None, ALU.mult))
            layer_norm_relu(2)
            dve.sem_inc(s_hn, 1)

            def qkv_products(t, par):
                ps = ps_pj[par]
                nc.vector.tensor_scalar(at(QN, t), ps[:, 0:D], 0.25, None, ALU.mult)
                return nc.vector.tensor_copy(at(KV, t), ps[:, D:3 * D])

            products(4 * NTL, qkv_products)
            settle(4 * NTL)
            dve.sem_inc(s_tw, 1)
            clear(4)
            dve.sem_inc(s_start, 1)
            softmax_layer(4)
            normalised_heads(4, 1e-8)
            dve.sem_inc(s_hn, 1)
            products(5 * NTL, lambda t, par: nc.vector.tensor_tensor(at(XN, t), at(XN, t), ps_pj[par][:, 0:D], ALU.add))
            settle(5 * NTL)

            layer_norm_relu(3)
            dve.sem_inc(s_tw, 1)
            clear(5)
            dve.sem_inc(s_start, 1)
            softmax_layer(5)
            normalised_heads(5, None)
            link(nc.vector.tensor_tensor(XN[:], XN[:], HN[:], ALU.add))
            dve.sem_inc(s_hn, 1)

            def add_tanh(t, par, q):
                dve.wait_ge(s_pjr, q + 6 * NTL + 1)
                dve.wait_ge(s_th, q + 1)
                nc.vector.tensor_reduce(UR[:, par, :], PR[:, par, 0:3, :].rearrange("p a d -> p d a"), X,
                                        ALU.add).then_inc(S["ur_ready"], 1)
                dve.wait_ge(S["ur_ready"], done(NB + q))
                nc.vector.tensor_tensor(at(XN, t), at(XN, t), UR[:, par, :], ALU.add).then_inc(s_pjr, 1)

            with dve.Fori(0, NTL // 2) as m:
                for par in range(2):
                    add_tanh(m * 2 + par, par, m * 2 + par)
            add_tanh(NTL - 1, 0, NTL - 1)
            settle(6 * NTL)
            dve.sem_inc(s_end, 1)


def kernel(**inputs):
    import numpy as np
    import concourse.bacc as bacc
    from concourse.bass_utils import run_bass_kernel_spmd

    x = {k: np.asarray(v) for k, v in inputs.items()}
    arrays = {k: x[k] for k in ("x", "src", "dst", "edge_type_474", "L1_gnn_W1", "L1_gnn_W2", "L3_gnn_rel_emb",
                                "L3_gnn_w_edge", "L3_gnn_w_node", "L3_gnn_w_comp")}
    for l in range(2):
        for kind in ("W4", "B4"):
            part = "w" if kind == "W4" else "b"
            arrays[f"{kind}_{l}"] = np.concatenate([x[f"L0_gnn_{n}_{part}{l}"] for n in "qkvs"], axis=-1)
        for n in (f"att_src{l + 1}", f"att_dst{l + 1}", f"b{l + 1}"):
            arrays[f"L1_gnn_{n}"] = x[f"L1_gnn_{n}"].reshape(D)
    arrays["WQKV"] = np.ascontiguousarray(x["L2_gnn_W_qkv"].T)
    arrays["WOUT"] = np.ascontiguousarray(x["L2_gnn_W_out"].T)

    nc = bacc.Bacc("TRN2", target_bir_lowering=False, num_devices=1)
    feed, aps = {}, {}
    for name, v in arrays.items():
        feed[f"in_{name}"] = np.ascontiguousarray(v)
        aps[name] = nc.dram_tensor(f"in_{name}", v.shape, mybir.dt.from_np(v.dtype), kind="ExternalInput").ap()
    out = nc.dram_tensor("out", (N, D), mybir.dt.float32, kind="ExternalOutput").ap()
    build(nc, aps, out)
    r = run_bass_kernel_spmd(nc, [feed], core_ids=[0])
    return r.results[0]["out"]
```
